# Optimizing a Trainium2 kernel written in Bass

```python
import numpy as np
import jax
import jax.numpy as jnp

def _softmax(x, axis=-1):
    return jax.nn.softmax(x, axis=axis)

def _gelu(x):
    return jax.nn.gelu(x, approximate=True)

def _silu(x):
    return jax.nn.silu(x)

def _sigmoid(x):
    return jax.nn.sigmoid(x)

def _layernorm(x, axis=-1, eps=1e-05):
    m = jnp.mean(x, axis=axis, keepdims=True)
    v = jnp.var(x, axis=axis, keepdims=True)
    return (x - m) / jnp.sqrt(v + eps)

def _scatter_add(tgt, idx, src, axis=0):
    return tgt.at[idx].add(src)

def _segment_sum(src, seg, n):
    return jax.ops.segment_sum(src, seg, n)
kernel_name = 'mk_decoder_postln_d2_seqx_r8_7f4757'

def setup_inputs(seed: int=0):
    np.random.seed(seed)
    _w = jnp.asarray

    def _rec_inputs():
        import jax
        import jax.numpy as jnp
        _rk = jax.random.key(seed)
        x = 7.22e-05 + 1 * jax.random.normal(jax.random.fold_in(_rk, 1), (8, 128, 256), jnp.float32)
        _lenS = 128 - jax.random.randint(jax.random.fold_in(_rk, 7), (8,), 0, max(1, 128 // 4) + 1, jnp.int32)
        _lenS2 = 128 - jax.random.randint(jax.random.fold_in(_rk, 8), (8,), 0, max(1, 128 // 4) + 1, jnp.int32)
        _ctx_2048P = jax.random.normal(jax.random.fold_in(_rk, 11), (8, 16, 256), jnp.float32)
        _ctx_2048c = jax.random.dirichlet(jax.random.fold_in(_rk, 511), 0.3 * jnp.ones((16,), jnp.float32), (8, 128))
        _ctx_2048t = jnp.einsum('bsk,bkd->bsd', _ctx_2048c, _ctx_2048P)
        _ctx_2048t = _ctx_2048t * jax.lax.rsqrt(jnp.mean(jnp.square(_ctx_2048t)) + 1e-12) * 0.953939
        ctx_2048 = 4.13588e-05 + 0.999923 * (_ctx_2048t + 0.3 * jax.random.normal(jax.random.fold_in(_rk, 611), (8, 128, 256), jnp.float32))
        return (x, ctx_2048)
    x, ctx_2048 = _rec_inputs()

    def _L0_attn_setup():
        import jax, jax.numpy as jnp
        import numpy as np
        B, S, D_IN = (1, 128, 256)
        H_QK, H_V, DK, DV = (8, 16, 128, 128)
        KCONV = 4
        D_OUT = H_QK * DK
        D_OUT_VG = H_V * DV
        FUSED = 2 * D_OUT + D_OUT_VG
        EPS = 1e-06

        def l2_norm(t):
            return t / jnp.sqrt(jnp.sum(t * t, axis=-1, keepdims=True) + EPS)

        def rms_norm(t, w):
            var = jnp.mean(t * t, axis=-1, keepdims=True)
            return t * jax.lax.rsqrt(var + EPS) * w

        def gated_delta_rule(q, k, v, beta, alpha):
            q = q * q.shape[-1] ** (-0.5)
            S0 = jnp.zeros(q.shape[:2] + (q.shape[-1], v.shape[-1]), q.dtype)

            def step(Sm, inp):
                q_t, k_t, v_t, b_t, a_t = inp
                Sm = Sm * a_t[..., None, None]
                kv = jnp.einsum('bhk,bhkv->bhv', k_t, Sm)
                u = (v_t - kv) * b_t[..., None]
                Sm = Sm + k_t[..., None] * u[:, :, None, :]
                o = jnp.einsum('bhk,bhkv->bhv', q_t, Sm)
                return (Sm, o)
            xs = (jnp.moveaxis(q, 2, 0), jnp.moveaxis(k, 2, 0), jnp.moveaxis(v, 2, 0), jnp.moveaxis(beta, 2, 0), jnp.moveaxis(alpha, 2, 0))
            Sf, outs = jax.lax.scan(step, S0, xs)
            return (jnp.moveaxis(outs, 0, 2), Sf)
        key = jax.random.key(seed)
        ks = jax.random.split(key, 8)
        return {'x': jax.random.normal(ks[0], (B, S, D_IN), jnp.float32), 'w_qkv': jax.random.normal(ks[1], (FUSED, D_IN), jnp.float32) * 0.02, 'w_gate': jax.random.normal(ks[2], (D_OUT_VG, D_IN), jnp.float32) * 0.02, 'w_beta': jax.random.normal(ks[3], (H_V, D_IN), jnp.float32) * 0.02, 'w_alpha': jax.random.normal(ks[4], (H_V, D_IN), jnp.float32) * 0.02, 'log_A': jnp.log(jax.random.uniform(ks[5], (H_V,), jnp.float32, 0.001, 16.0)), 'dt_bias': jnp.ones((H_V,), jnp.float32), 'conv_w': jax.random.normal(ks[6], (FUSED, 1, KCONV), jnp.float32) * 0.1, 'rms_w': jnp.ones((DV,), jnp.float32), 'w_out': jax.random.normal(ks[7], (D_IN, D_OUT_VG), jnp.float32) * 0.02}
    _L0_attn_all = _L0_attn_setup()
    _L0_attn_in = {k: v for k, v in _L0_attn_all.items() if k in ('w_qkv', 'w_gate', 'w_beta', 'w_alpha', 'log_A', 'dt_bias', 'conv_w', 'rms_w', 'w_out')}
    del _L0_attn_all

    def _L0_xattn_setup():
        import jax, jax.numpy as jnp
        import numpy as np
        B, D, N, H = (4, 128, 256, 16)
        HD = D // H

        def rotate_half(x):
            x1 = x[..., 0::2]
            x2 = x[..., 1::2]
            return jnp.stack((-x2, x1), axis=-1).reshape(x.shape)

        def apply_cached_rotary_emb(freqs, t):
            return t * freqs[0] + rotate_half(t) * freqs[1]
        key = jax.random.key(seed)
        ks = jax.random.split(key, 13)
        s = 1.0 / np.sqrt(D)
        inp = {'query': jax.random.normal(ks[0], (B, D, N), jnp.float32), 'key': jax.random.normal(ks[1], (B, D, N), jnp.float32), 'value': jax.random.normal(ks[2], (B, D, N), jnp.float32), 'encoding': jax.random.normal(ks[3], (2, 1, 1, N, HD), jnp.float32), 'Wq': jax.random.normal(ks[4], (D, D), jnp.float32) * s, 'bq': jax.random.normal(ks[5], (D,), jnp.float32) * s, 'Wk': jax.random.normal(ks[6], (D, D), jnp.float32) * s, 'bk': jax.random.normal(ks[7], (D,), jnp.float32) * s, 'Wv': jax.random.normal(ks[8], (D, D), jnp.float32) * s, 'bv': jax.random.normal(ks[9], (D,), jnp.float32) * s, 'Wm': jax.random.normal(ks[10], (D, D), jnp.float32) * s, 'bm': jax.random.normal(ks[11], (D,), jnp.float32) * s}
        return inp
    _L0_xattn_all = _L0_xattn_setup()
    _L0_xattn_in = {k: v for k, v in _L0_xattn_all.items() if k in ('encoding', 'Wq', 'bq', 'Wk', 'bk', 'Wv', 'bv', 'Wm', 'bm')}
    del _L0_xattn_all

    def _L0_ffn_setup():
        import jax, jax.numpy as jnp
        import numpy as np
        MIN_EXPERTS = 2
        NEG_INF = -1000000000.0

        def _l2norm(x, axis):
            return x / jnp.maximum(jnp.linalg.norm(x, axis=axis, keepdims=True), 1e-12)

        def _ste(x):
            return x + jax.lax.stop_gradient((x > 0).astype(x.dtype) - x)

        def _forward(hidden_states, sim_matrix, gates, q_proj, k_proj, v_proj, o_proj):
            B, T, C = hidden_states.shape
            E = gates.shape[0]
            H = q_proj.shape[-1]
            x = hidden_states.reshape(B * T, C)
            logits = _l2norm(x, -1) @ _l2norm(sim_matrix, 0) - jax.nn.sigmoid(gates)
            gated = jax.nn.relu(logits)
            mask = _ste(gated)
            inactive = jnp.sum(mask, axis=1) == 0
            fb_idx = jax.lax.top_k(logits, MIN_EXPERTS)[1]
            fb_mask = jnp.max(jax.nn.one_hot(fb_idx, E, dtype=mask.dtype), axis=1)
            mask = jnp.where(inactive[:, None] & (fb_mask > 0), jnp.ones_like(mask), mask)
            masked_logits = jnp.where(mask > 0, gated, jnp.full_like(gated, NEG_INF))
            probs = jax.nn.softmax(masked_logits, axis=-1)
            w = probs * (mask > 0)

            def mix(proj):
                pe = jnp.einsum('nc,ech->neh', x, proj)
                return jnp.einsum('ne,neh->nh', w, pe).reshape(B, T, H)
            q, k, v = (mix(q_proj), mix(k_proj), mix(v_proj))
            scale = 1.0 / jnp.sqrt(jnp.asarray(H, dtype=q.dtype))
            scores = jnp.einsum('bqh,bkh->bqk', q, k) * scale
            causal = jnp.tril(jnp.ones((T, T), dtype=bool))
            scores = jnp.where(causal[None], scores, jnp.full_like(scores, NEG_INF))
            attn = jax.nn.softmax(scores, axis=-1)
            ao = jnp.einsum('bqk,bkh->bqh', attn, v).reshape(B * T, H)
            wa = jnp.einsum('ne,nh->enh', w, ao)
            out = jnp.einsum('enh,ehc->nc', wa, o_proj)
            return out.reshape(B, T, C)
        key = jax.random.key(seed)
        ks = jax.random.split(key, 6)
        B, T, C, H, E = (4, 256, 256, 128, 16)
        xavier_qkv = float(np.sqrt(2.0 / (C + H)))
        return {'hidden_states': jax.random.normal(ks[0], (B, T, C), dtype=jnp.float32), 'sim_matrix': jax.random.normal(ks[1], (C, E), dtype=jnp.float32), 'gates': jnp.full((E,), -6.0, dtype=jnp.float32), 'q_proj': jax.random.normal(ks[2], (E, C, H), dtype=jnp.float32) * xavier_qkv, 'k_proj': jax.random.normal(ks[3], (E, C, H), dtype=jnp.float32) * xavier_qkv, 'v_proj': jax.random.normal(ks[4], (E, C, H), dtype=jnp.float32) * xavier_qkv, 'o_proj': jax.random.normal(ks[5], (E, H, C), dtype=jnp.float32) * xavier_qkv}
    _L0_ffn_all = _L0_ffn_setup()
    _L0_ffn_in = {k: v for k, v in _L0_ffn_all.items() if k in ('sim_matrix', 'gates', 'q_proj', 'k_proj', 'v_proj', 'o_proj')}
    del _L0_ffn_all

    def _L1_attn_setup():
        import jax, jax.numpy as jnp
        import numpy as np
        import math
        D_MODEL = 256
        N_HEADS = 16
        D_HEAD = 128
        BATCH = 2
        SEQ = 256
        key = jax.random.key(seed)
        ks = jax.random.split(key, 5)
        std = 0.02
        x = jax.random.normal(ks[0], (BATCH, SEQ, D_MODEL), dtype=jnp.float32)
        W_Q = std * jax.random.normal(ks[1], (N_HEADS, D_HEAD, D_MODEL), dtype=jnp.float32)
        W_K = std * jax.random.normal(ks[2], (N_HEADS, D_HEAD, D_MODEL), dtype=jnp.float32)
        W_V = std * jax.random.normal(ks[3], (N_HEADS, D_HEAD, D_MODEL), dtype=jnp.float32)
        W_O = std * jax.random.normal(ks[4], (N_HEADS, D_MODEL, D_HEAD), dtype=jnp.float32)
        return {'x': x, 'W_Q': W_Q, 'W_K': W_K, 'W_V': W_V, 'W_O': W_O}
    _L1_attn_all = _L1_attn_setup()
    _L1_attn_in = {k: v for k, v in _L1_attn_all.items() if k in ('W_Q', 'W_K', 'W_V', 'W_O')}
    del _L1_attn_all

    def _L1_xattn_setup():
        import jax, jax.numpy as jnp
        import numpy as np
        D_MODEL = 256
        NUM_HEADS = 16
        HEAD_DIM = D_MODEL // NUM_HEADS

        def _fq_sym(x, axis):
            s = jnp.max(jnp.abs(x), axis=axis, keepdims=True) / 127.0
            s = jnp.maximum(s, 1e-08)
            q = jnp.clip(jnp.round(x / s), -127.0, 127.0) * s
            return x + jax.lax.stop_gradient(q - x)

        def _fq_unsigned(x, axis):
            s = jnp.max(x, axis=axis, keepdims=True) / 255.0
            s = jnp.maximum(s, 1e-08)
            q = jnp.clip(jnp.round(x / s), 0.0, 255.0) * s
            return x + jax.lax.stop_gradient(q - x)
        key = jax.random.key(seed)
        ks = jax.random.split(key, 8)
        B, N, M, C = (2, 256, 64, D_MODEL)
        return {'x': jax.random.normal(ks[0], (B, N, C), jnp.float32), 'cond': jax.random.normal(ks[1], (B, M, C), jnp.float32), 'Wq': jax.random.normal(ks[2], (C, C), jnp.float32) * 0.02, 'bq': jnp.zeros((C,), jnp.float32), 'Wkv': jax.random.normal(ks[3], (C, 2 * C), jnp.float32) * 0.02, 'bkv': jnp.zeros((2 * C,), jnp.float32), 'Wp': jax.random.normal(ks[4], (C, C), jnp.float32) * 0.02, 'bp': jnp.zeros((C,), jnp.float32)}
    _L1_xattn_all = _L1_xattn_setup()
    _L1_xattn_in = {k: v for k, v in _L1_xattn_all.items() if k in ('Wq', 'bq', 'Wkv', 'bkv', 'Wp', 'bp')}
    del _L1_xattn_all

    def _L1_ffn_setup():
        import jax, jax.numpy as jnp
        import numpy as np
        EPS = 1e-05

        def rmsnorm(x, weight, eps=EPS):
            var = jnp.mean(x * x, axis=-1, keepdims=True)
            return x * jax.lax.rsqrt(var + eps) * weight

        def activation_quant(x):
            scale = 127.0 / jnp.clip(jnp.max(jnp.abs(x), axis=-1, keepdims=True), 1e-05, None)
            return jnp.clip(jnp.round(x * scale), -128, 127) / scale

        def weight_quant(w):
            scale = 1.0 / jnp.clip(jnp.mean(jnp.abs(w)), 1e-05, None)
            return jnp.clip(jnp.round(w * scale), -1, 1) / scale

        def bitlinear(x, w):
            xq = activation_quant(x)
            wq = weight_quant(w)
            return jnp.einsum('bsh,oh->bso', xq, wq)
        key = jax.random.key(seed)
        k1, k2, k3 = jax.random.split(key, 3)
        B, S, H, F = (4, 256, 256, 704)
        x = jax.random.normal(k1, (B, S, H), dtype=jnp.float32)
        w_gate_up = jax.random.normal(k2, (2 * F, H), dtype=jnp.float32) * 0.02
        w_down = jax.random.normal(k3, (H, F), dtype=jnp.float32) * 0.02
        norm_weight = jnp.ones((H,), dtype=jnp.float32)
        return {'x': x, 'w_gate_up': w_gate_up, 'w_down': w_down, 'norm_weight': norm_weight}
    _L1_ffn_all = _L1_ffn_setup()
    _L1_ffn_in = {k: v for k, v in _L1_ffn_all.items() if k in ('w_gate_up', 'w_down', 'norm_weight')}
    del _L1_ffn_all
    return {'x': x, 'ctx_2048': ctx_2048, 'L0_attn_w_qkv': _L0_attn_in['w_qkv'], 'L0_attn_w_gate': _L0_attn_in['w_gate'], 'L0_attn_w_beta': _L0_attn_in['w_beta'], 'L0_attn_w_alpha': _L0_attn_in['w_alpha'], 'L0_attn_log_A': _L0_attn_in['log_A'], 'L0_attn_dt_bias': _L0_attn_in['dt_bias'], 'L0_attn_conv_w': _L0_attn_in['conv_w'], 'L0_attn_rms_w': _L0_attn_in['rms_w'], 'L0_attn_w_out': _L0_attn_in['w_out'], 'L0_xattn_encoding': _L0_xattn_in['encoding'], 'L0_xattn_Wq': _L0_xattn_in['Wq'], 'L0_xattn_bq': _L0_xattn_in['bq'], 'L0_xattn_Wk': _L0_xattn_in['Wk'], 'L0_xattn_bk': _L0_xattn_in['bk'], 'L0_xattn_Wv': _L0_xattn_in['Wv'], 'L0_xattn_bv': _L0_xattn_in['bv'], 'L0_xattn_Wm': _L0_xattn_in['Wm'], 'L0_xattn_bm': _L0_xattn_in['bm'], 'L0_ffn_sim_matrix': _L0_ffn_in['sim_matrix'], 'L0_ffn_gates': _L0_ffn_in['gates'], 'L0_ffn_q_proj': _L0_ffn_in['q_proj'], 'L0_ffn_k_proj': _L0_ffn_in['k_proj'], 'L0_ffn_v_proj': _L0_ffn_in['v_proj'], 'L0_ffn_o_proj': _L0_ffn_in['o_proj'], 'L1_attn_W_Q': _L1_attn_in['W_Q'], 'L1_attn_W_K': _L1_attn_in['W_K'], 'L1_attn_W_V': _L1_attn_in['W_V'], 'L1_attn_W_O': _L1_attn_in['W_O'], 'L1_xattn_Wq': _L1_xattn_in['Wq'], 'L1_xattn_bq': _L1_xattn_in['bq'], 'L1_xattn_Wkv': _L1_xattn_in['Wkv'], 'L1_xattn_bkv': _L1_xattn_in['bkv'], 'L1_xattn_Wp': _L1_xattn_in['Wp'], 'L1_xattn_bp': _L1_xattn_in['bp'], 'L1_ffn_w_gate_up': _L1_ffn_in['w_gate_up'], 'L1_ffn_w_down': _L1_ffn_in['w_down'], 'L1_ffn_norm_weight': _L1_ffn_in['norm_weight']}

def reference(x, ctx_2048, L0_attn_w_qkv, L0_attn_w_gate, L0_attn_w_beta, L0_attn_w_alpha, L0_attn_log_A, L0_attn_dt_bias, L0_attn_conv_w, L0_attn_rms_w, L0_attn_w_out, L0_xattn_encoding, L0_xattn_Wq, L0_xattn_bq, L0_xattn_Wk, L0_xattn_bk, L0_xattn_Wv, L0_xattn_bv, L0_xattn_Wm, L0_xattn_bm, L0_ffn_sim_matrix, L0_ffn_gates, L0_ffn_q_proj, L0_ffn_k_proj, L0_ffn_v_proj, L0_ffn_o_proj, L1_attn_W_Q, L1_attn_W_K, L1_attn_W_V, L1_attn_W_O, L1_xattn_Wq, L1_xattn_bq, L1_xattn_Wkv, L1_xattn_bkv, L1_xattn_Wp, L1_xattn_bp, L1_ffn_w_gate_up, L1_ffn_w_down, L1_ffn_norm_weight):
    import jax
    import jax.numpy as jnp

    def _L0_attn_ref(x, w_qkv, w_gate, w_beta, w_alpha, log_A, dt_bias, conv_w, rms_w, w_out):
        import jax, jax.numpy as jnp
        import numpy as np
        B, S, D_IN = (1, 128, 256)
        H_QK, H_V, DK, DV = (8, 16, 128, 128)
        KCONV = 4
        D_OUT = H_QK * DK
        D_OUT_VG = H_V * DV
        FUSED = 2 * D_OUT + D_OUT_VG
        EPS = 1e-06

        def l2_norm(t):
            return t / jnp.sqrt(jnp.sum(t * t, axis=-1, keepdims=True) + EPS)

        def rms_norm(t, w):
            var = jnp.mean(t * t, axis=-1, keepdims=True)
            return t * jax.lax.rsqrt(var + EPS) * w

        def gated_delta_rule(q, k, v, beta, alpha):
            q = q * q.shape[-1] ** (-0.5)
            S0 = jnp.zeros(q.shape[:2] + (q.shape[-1], v.shape[-1]), q.dtype)

            def step(Sm, inp):
                q_t, k_t, v_t, b_t, a_t = inp
                Sm = Sm * a_t[..., None, None]
                kv = jnp.einsum('bhk,bhkv->bhv', k_t, Sm)
                u = (v_t - kv) * b_t[..., None]
                Sm = Sm + k_t[..., None] * u[:, :, None, :]
                o = jnp.einsum('bhk,bhkv->bhv', q_t, Sm)
                return (Sm, o)
            xs = (jnp.moveaxis(q, 2, 0), jnp.moveaxis(k, 2, 0), jnp.moveaxis(v, 2, 0), jnp.moveaxis(beta, 2, 0), jnp.moveaxis(alpha, 2, 0))
            Sf, outs = jax.lax.scan(step, S0, xs)
            return (jnp.moveaxis(outs, 0, 2), Sf)
        b, seq_len, _ = x.shape
        fused_qkv = x @ w_qkv.T
        beta = jax.nn.sigmoid(x @ w_beta.T).transpose(0, 2, 1)
        token_projs = x @ w_alpha.T
        alpha = jnp.exp(-jnp.exp(log_A) * jax.nn.softplus(token_projs + dt_bias))
        alpha = alpha.transpose(0, 2, 1)
        conv_in = fused_qkv.transpose(0, 2, 1)
        conv_out = jax.lax.conv_general_dilated(conv_in, conv_w, window_strides=(1,), padding=[(KCONV - 1, 0)], dimension_numbers=('NCH', 'OIH', 'NCH'), feature_group_count=FUSED)
        fused_qkv = jax.nn.silu(conv_out).transpose(0, 2, 1)
        query = fused_qkv[..., :D_OUT].reshape(b, seq_len, H_QK, DK).transpose(0, 2, 1, 3)
        key = fused_qkv[..., D_OUT:2 * D_OUT].reshape(b, seq_len, H_QK, DK).transpose(0, 2, 1, 3)
        value = fused_qkv[..., 2 * D_OUT:].reshape(b, seq_len, H_V, DV).transpose(0, 2, 1, 3)
        query, key = (l2_norm(query), l2_norm(key))
        rep = H_V // H_QK
        if rep > 1:
            query = jnp.repeat(query, rep, axis=1)
            key = jnp.repeat(key, rep, axis=1)
        ctx, _ = gated_delta_rule(query, key, value, beta, alpha)
        ctx = rms_norm(ctx.astype(jnp.float32), rms_w)
        ctx = ctx.transpose(0, 2, 1, 3).reshape(b, seq_len, D_OUT_VG)
        gate = jax.nn.silu(x @ w_gate.T)
        return gate * ctx @ w_out.T

    def _L0_xattn_ref(query, key, value, encoding, Wq, bq, Wk, bk, Wv, bv, Wm, bm):
        import jax, jax.numpy as jnp
        import numpy as np
        B, D, N, H = (4, 128, 256, 16)
        HD = D // H

        def rotate_half(x):
            x1 = x[..., 0::2]
            x2 = x[..., 1::2]
            return jnp.stack((-x2, x1), axis=-1).reshape(x.shape)

        def apply_cached_rotary_emb(freqs, t):
            return t * freqs[0] + rotate_half(t) * freqs[1]
        b, d_model, n = query.shape

        def proj(W, bias, x):
            return jnp.einsum('oi,bin->bon', W, x) + bias[None, :, None]
        q = proj(Wq, bq, query).reshape(b, HD, H, n)
        k = proj(Wk, bk, key).reshape(b, HD, H, n)
        v = proj(Wv, bv, value).reshape(b, HD, H, n)
        q = jnp.transpose(apply_cached_rotary_emb(encoding, jnp.transpose(q, (0, 2, 3, 1))), (0, 3, 1, 2))
        k = jnp.transpose(apply_cached_rotary_emb(encoding, jnp.transpose(k, (0, 2, 3, 1))), (0, 3, 1, 2))
        scores = jnp.einsum('bdhn,bdhm->bhnm', q, k) / np.float32(np.sqrt(HD))
        prob = jax.nn.softmax(scores, axis=-1)
        x = jnp.einsum('bhnm,bdhm->bdhn', prob, v)
        out = jnp.einsum('oi,bin->bon', Wm, x.reshape(b, d_model, n)) + bm[None, :, None]
        return out

    def _L0_ffn_ref(hidden_states, sim_matrix, gates, q_proj, k_proj, v_proj, o_proj):
        import jax, jax.numpy as jnp
        import numpy as np
        MIN_EXPERTS = 2
        NEG_INF = -1000000000.0

        def _l2norm(x, axis):
            return x / jnp.maximum(jnp.linalg.norm(x, axis=axis, keepdims=True), 1e-12)

        def _ste(x):
            return x + jax.lax.stop_gradient((x > 0).astype(x.dtype) - x)

        def _forward(hidden_states, sim_matrix, gates, q_proj, k_proj, v_proj, o_proj):
            B, T, C = hidden_states.shape
            E = gates.shape[0]
            H = q_proj.shape[-1]
            x = hidden_states.reshape(B * T, C)
            logits = _l2norm(x, -1) @ _l2norm(sim_matrix, 0) - jax.nn.sigmoid(gates)
            gated = jax.nn.relu(logits)
            mask = _ste(gated)
            inactive = jnp.sum(mask, axis=1) == 0
            fb_idx = jax.lax.top_k(logits, MIN_EXPERTS)[1]
            fb_mask = jnp.max(jax.nn.one_hot(fb_idx, E, dtype=mask.dtype), axis=1)
            mask = jnp.where(inactive[:, None] & (fb_mask > 0), jnp.ones_like(mask), mask)
            masked_logits = jnp.where(mask > 0, gated, jnp.full_like(gated, NEG_INF))
            probs = jax.nn.softmax(masked_logits, axis=-1)
            w = probs * (mask > 0)

            def mix(proj):
                pe = jnp.einsum('nc,ech->neh', x, proj)
                return jnp.einsum('ne,neh->nh', w, pe).reshape(B, T, H)
            q, k, v = (mix(q_proj), mix(k_proj), mix(v_proj))
            scale = 1.0 / jnp.sqrt(jnp.asarray(H, dtype=q.dtype))
            scores = jnp.einsum('bqh,bkh->bqk', q, k) * scale
            causal = jnp.tril(jnp.ones((T, T), dtype=bool))
            scores = jnp.where(causal[None], scores, jnp.full_like(scores, NEG_INF))
            attn = jax.nn.softmax(scores, axis=-1)
            ao = jnp.einsum('bqk,bkh->bqh', attn, v).reshape(B * T, H)
            wa = jnp.einsum('ne,nh->enh', w, ao)
            out = jnp.einsum('enh,ehc->nc', wa, o_proj)
            return out.reshape(B, T, C)
        return _forward(hidden_states, sim_matrix, gates, q_proj, k_proj, v_proj, o_proj)

    def _L1_attn_ref(x, W_Q, W_K, W_V, W_O):
        import jax, jax.numpy as jnp
        import numpy as np
        import math
        D_MODEL = 256
        N_HEADS = 16
        D_HEAD = 128
        BATCH = 2
        SEQ = 256
        d_head = W_Q.shape[1]
        seq_len = x.shape[1]
        scale = 1.0 / math.sqrt(d_head)
        q = jnp.einsum('bsd,hed->bhse', x, W_Q)
        k = jnp.einsum('bsd,hed->bhse', x, W_K)
        v = jnp.einsum('bsd,hed->bhse', x, W_V)
        scores = jnp.einsum('bhse,bhme->bhsm', q, k) * scale
        causal = jnp.triu(jnp.ones((seq_len, seq_len), dtype=bool), k=1)
        scores = jnp.where(causal, jnp.float32(-1000000000.0), scores)
        pattern = jax.nn.softmax(scores, axis=-1)
        z = jnp.einsum('bhsm,bhme->bhse', pattern, v)
        out = jnp.einsum('bhse,hde->bsd', z, W_O)
        return out

    def _L1_xattn_ref(x, cond, Wq, bq, Wkv, bkv, Wp, bp):
        import jax, jax.numpy as jnp
        import numpy as np
        D_MODEL = 256
        NUM_HEADS = 16
        HEAD_DIM = D_MODEL // NUM_HEADS

        def _fq_sym(x, axis):
            s = jnp.max(jnp.abs(x), axis=axis, keepdims=True) / 127.0
            s = jnp.maximum(s, 1e-08)
            q = jnp.clip(jnp.round(x / s), -127.0, 127.0) * s
            return x + jax.lax.stop_gradient(q - x)

        def _fq_unsigned(x, axis):
            s = jnp.max(x, axis=axis, keepdims=True) / 255.0
            s = jnp.maximum(s, 1e-08)
            q = jnp.clip(jnp.round(x / s), 0.0, 255.0) * s
            return x + jax.lax.stop_gradient(q - x)
        B, N, C = x.shape
        H, hd = (NUM_HEADS, HEAD_DIM)
        q = (x @ Wq + bq).reshape(1, B * N, H, hd)
        kv = (cond @ Wkv + bkv).reshape(1, -1, 2, H, hd)
        k, v = (kv[:, :, 0], kv[:, :, 1])
        scale = 1.0 / np.sqrt(hd).astype(np.float32)
        q = jnp.transpose(q * scale, (0, 2, 1, 3))
        k = jnp.transpose(k, (0, 2, 1, 3))
        v = jnp.transpose(v, (0, 2, 1, 3))
        q = _fq_sym(q, axis=-1)
        k = _fq_sym(k, axis=-1)
        v = _fq_sym(v, axis=2)
        attn = jnp.einsum('bhqd,bhkd->bhqk', q, k)
        attn = jax.nn.softmax(attn.astype(jnp.float32), axis=-1)
        attn = _fq_unsigned(attn, axis=-1)
        out = jnp.einsum('bhqk,bhkd->bhqd', attn, v)
        out = jnp.transpose(out, (0, 2, 1, 3)).reshape(B, N, C)
        return out @ Wp + bp

    def _L1_ffn_ref(x, w_gate_up, w_down, norm_weight):
        import jax, jax.numpy as jnp
        import numpy as np
        EPS = 1e-05

        def rmsnorm(x, weight, eps=EPS):
            var = jnp.mean(x * x, axis=-1, keepdims=True)
            return x * jax.lax.rsqrt(var + eps) * weight

        def activation_quant(x):
            scale = 127.0 / jnp.clip(jnp.max(jnp.abs(x), axis=-1, keepdims=True), 1e-05, None)
            return jnp.clip(jnp.round(x * scale), -128, 127) / scale

        def weight_quant(w):
            scale = 1.0 / jnp.clip(jnp.mean(jnp.abs(w)), 1e-05, None)
            return jnp.clip(jnp.round(w * scale), -1, 1) / scale

        def bitlinear(x, w):
            xq = activation_quant(x)
            wq = weight_quant(w)
            return jnp.einsum('bsh,oh->bso', xq, wq)
        x_norm = rmsnorm(x, norm_weight)
        gate_up = bitlinear(x_norm, w_gate_up)
        gate, up = jnp.split(gate_up, 2, axis=-1)
        hidden = jnp.square(jax.nn.relu(gate)) * up
        return bitlinear(hidden, w_down)
    x = _layernorm(x + _L0_attn_ref(x, L0_attn_w_qkv, L0_attn_w_gate, L0_attn_w_beta, L0_attn_w_alpha, L0_attn_log_A, L0_attn_dt_bias, L0_attn_conv_w, L0_attn_rms_w, L0_attn_w_out), axis=-1)
    x = _layernorm(x + _L0_xattn_ref(x, ctx_2048, ctx_2048, L0_xattn_encoding, L0_xattn_Wq, L0_xattn_bq, L0_xattn_Wk, L0_xattn_bk, L0_xattn_Wv, L0_xattn_bv, L0_xattn_Wm, L0_xattn_bm), axis=-1)
    x = _layernorm(x + _L0_ffn_ref(x, L0_ffn_sim_matrix, L0_ffn_gates, L0_ffn_q_proj, L0_ffn_k_proj, L0_ffn_v_proj, L0_ffn_o_proj), axis=-1)
    x = _layernorm(x + _L1_attn_ref(x, L1_attn_W_Q, L1_attn_W_K, L1_attn_W_V, L1_attn_W_O), axis=-1)
    x = _layernorm(x + _L1_xattn_ref(x, ctx_2048, L1_xattn_Wq, L1_xattn_bq, L1_xattn_Wkv, L1_xattn_bkv, L1_xattn_Wp, L1_xattn_bp), axis=-1)
    x = _layernorm(x + _L1_ffn_ref(x, L1_ffn_w_gate_up, L1_ffn_w_down, L1_ffn_norm_weight), axis=-1)
    return x

_drawn_inputs = setup_inputs


def setup_inputs(seed=0):
    import zlib

    import numpy as np

    out = dict(_drawn_inputs(seed))
    spreads = {'L0_attn_dt_bias': (1.0, 0.6),
     'L0_attn_rms_w': (1.0, 0.6),
     'L0_ffn_gates': (-6.0, 0.6),
     'L1_xattn_bq': (0.0, 0.8),
     'L1_xattn_bkv': (0.0, 0.275),
     'L1_xattn_bp': (0.0, 0.1),
     'L1_ffn_norm_weight': (1.0, 0.6)}
    factors = {'L0_attn_w_beta': 8.0,
     'L0_attn_w_alpha': 8.0,
     'L0_attn_log_A': 5.993,
     'L0_xattn_bv': 8.0,
     'L0_xattn_bm': 8.0,
     'L0_ffn_q_proj': 8.0,
     'L0_ffn_k_proj': 8.0,
     'L1_attn_W_Q': 8.0,
     'L1_attn_W_K': 8.0,
     'L1_xattn_Wq': 8.0,
     'L1_xattn_Wkv': 3.584,
     'L1_ffn_w_gate_up': 4.144,
     'L1_ffn_w_down': 3.041}
    for name, (base, spread) in spreads.items():
        noise = np.random.default_rng([zlib.crc32(name.encode()), seed]).standard_normal(out[name].shape)
        drawn = base * np.exp(spread * noise) if base else spread * noise
        out[name] = jnp.asarray(drawn.astype(out[name].dtype))
    for name, factor in factors.items():
        out[name] = (out[name] * factor).astype(out[name].dtype)
    return out
```

```python
import numpy as np
from contextlib import ExitStack

import concourse.bass as bass
from concourse import mybir

F32 = mybir.dt.float32
BF16 = mybir.dt.bfloat16
ALU = mybir.AluOpType
ACT = mybir.ActivationFunctionType
AX = mybir.AxisListType

B, S, C = 8, 128, 256
N = B * S
CT = C // 128
BANK = 512
PER_BANK = BANK // 128
HALVES = N // BANK
LN_EPS = 1e-5
ROUND = 12582912.0
MASKED = -1e9
ALLOWED = 3e38


class Core:

    def __init__(self, nc, ctx):
        self.nc, self.ctx = nc, ctx
        self.stage_sems = []
        self.x = self.sb(ctx, "x_tok", [128, B, C])
        self.y = self.sb(ctx, "y_tok", [128, B, C])
        self.xt = self.sb(ctx, "x_chan", [128, CT, N])
        self.ident = self.sb(ctx, "ident", [128, 128])
        self.ident_bf = self.sb(ctx, "ident_bf", [128, 128], BF16)
        self.zero_bf = self.sb(ctx, "zero_bf", [128, BANK], BF16)
        self.ones = self.sb(ctx, "ones", [128, 128])
        self.causal = self.sb(ctx, "causal", [128, 128])
        self.psum = ctx.enter_context(nc.psum_tensor("psum", [128, 8 * BANK], F32))
        self.bank = [self.psum[:, i * BANK:(i + 1) * BANK] for i in range(8)]

    def sb(self, ctx, name, shape, dt=F32):
        return ctx.enter_context(self.nc.sbuf_tensor(name, shape, dt))

    def bank_bf(self, i):
        return self.bank[i].bitcast(BF16)

    def sem(self, ctx, name):
        handle = self.nc.alloc_semaphore(name)
        self.stage_sems.append(handle)
        return handle

    def end_stage(self):
        self.nc.clear_and_free_semaphores(self.stage_sems)
        self.nc.all_engine_barrier()
        self.stage_sems = []


def make_constants(core, x_dram):
    nc = core.nc
    with ExitStack() as ctx:
        filled, shaped, x_in = (core.sem(ctx, n) for n in ("const_filled", "const_shaped", "x_in"))
        with nc.Block() as block:

            @block.sync
            def _(sp):
                sp.dma_start(core.x[:], x_dram.rearrange("b s c -> s b c")).then_inc(x_in, 16)
                sp.wait_ge(x_in, 16)

            @block.gpsimd
            def _(pool):
                nc.gpsimd.memset(core.ident[:], 0.0)
                nc.gpsimd.memset(core.ones[:], 1.0)
                nc.gpsimd.memset(core.zero_bf[:], 0.0)
                nc.gpsimd.memset(core.causal[:], ALLOWED).then_inc(filled, 1)
                pool.wait_ge(filled, 1)
                nc.gpsimd.affine_select(out=core.ident[:], in_=core.ident[:], compare_op=ALU.not_equal, fill=1.0,
                                        base=0, pattern=[[-1, 128]], channel_multiplier=1).then_inc(shaped, 1)
                nc.gpsimd.affine_select(out=core.causal[:], in_=core.causal[:], compare_op=ALU.is_ge, fill=MASKED,
                                        base=0, pattern=[[-1, 128]], channel_multiplier=1).then_inc(shaped, 1)
                pool.wait_ge(shaped, 1)
                nc.gpsimd.tensor_copy(core.ident_bf[:], core.ident[:]).then_inc(shaped, 1)


def norm_and_turn(core, tag, normalize=True, turn=True, out_dram=None):
    nc = core.nc
    with ExitStack() as ctx:
        stats = core.sb(ctx, f"{tag}_stats", [128, B, 6])
        mv = core.sb(ctx, f"{tag}_mv", [128, B, 2])
        var = core.sb(ctx, f"{tag}_var", [128, B])
        sd = core.sb(ctx, f"{tag}_sd", [128, B])
        rstd = core.sb(ctx, f"{tag}_rstd", [128, B])
        t0 = core.sb(ctx, f"{tag}_t0", [128, B])
        stats_ready, mv_ready, var_ready, sd_ready, rstd_steps, x_ready, turned, stored = (
            core.sem(ctx, f"{tag}_{n}") for n in
            ("stats_ready", "mv_ready", "var_ready", "sd_ready", "rstd_steps", "x_ready", "turned", "stored"))
        with nc.Block() as block:

            @block.vector
            def _(dve):
                if normalize:
                    for b in range(B):
                        nc.vector.bn_stats(stats[:, b, :], core.y[:, b, :]).then_inc(stats_ready, 1)
                    for b in range(B):
                        dve.wait_ge(stats_ready, b + 1)
                        nc.vector.bn_aggr(mv[:, b, :], stats[:, b, :]).then_inc(mv_ready, 1)
                    dve.wait_ge(mv_ready, B)
                    nc.vector.tensor_scalar(var[:], mv[:, :, 1], LN_EPS, None, ALU.add).then_inc(var_ready, 1)
                    dve.wait_ge(sd_ready, 1)
                    nc.vector.reciprocal(rstd[:], sd[:]).then_inc(rstd_steps, 1)
                    dve.wait_ge(rstd_steps, 1)
                    nc.vector.tensor_tensor(t0[:], rstd[:], rstd[:], ALU.mult).then_inc(rstd_steps, 1)
                    dve.wait_ge(rstd_steps, 2)
                    nc.vector.tensor_tensor(t0[:], t0[:], var[:], ALU.mult).then_inc(rstd_steps, 1)
                    dve.wait_ge(rstd_steps, 3)
                    nc.vector.tensor_scalar(t0[:], t0[:], -0.5, 1.5, ALU.mult, ALU.add).then_inc(rstd_steps, 1)
                    dve.wait_ge(rstd_steps, 4)
                    nc.vector.tensor_tensor(rstd[:], rstd[:], t0[:], ALU.mult).then_inc(rstd_steps, 1)
                    dve.wait_ge(rstd_steps, 5)
                    for b in range(B):
                        nc.vector.tensor_scalar(core.x[:, b, :], core.y[:, b, :], mv[:, b, 0:1], rstd[:, b:b + 1],
                                                ALU.subtract, ALU.mult).then_inc(x_ready, 1)
                if turn:
                    for half in range(HALVES):
                        dve.wait_ge(turned, half + 1)
                        nc.vector.tensor_copy(core.xt[:, 1, half * BANK:(half + 1) * BANK], core.bank[half * CT + 1][:])

            @block.scalar
            def _(act):
                if normalize:
                    act.wait_ge(var_ready, 1)
                    nc.scalar.activation(sd[:], var[:], ACT.Sqrt).then_inc(sd_ready, 1)
                if turn:
                    for half in range(HALVES):
                        act.wait_ge(turned, half + 1)
                        nc.scalar.copy(core.xt[:, 0, half * BANK:(half + 1) * BANK], core.bank[half * CT][:])

            if turn:
                @block.tensor
                def _(pe):
                    for half in range(HALVES):
                        for k in range(PER_BANK):
                            b = half * PER_BANK + k
                            if normalize:
                                pe.wait_ge(x_ready, b + 1)
                            for ct in range(CT):
                                mm = nc.tensor.transpose(core.bank[half * CT + ct][:, k * 128:(k + 1) * 128],
                                                         core.x[:, b, ct * 128:(ct + 1) * 128], core.ident[:])
                        mm.then_inc(turned, 1)

            if out_dram is not None:
                @block.sync
                def _(sp):
                    sp.wait_ge(x_ready, B)
                    sp.dma_start(out_dram.rearrange("b s c -> s b c"), core.x[:]).then_inc(stored, 16)
                    sp.wait_ge(stored, 16)


GRAM_HEADS = 8
DELTA_LEVELS = 6


def delta_masks():
    i = np.arange(128)
    up_to = (i[:, None] <= i[None, :])
    after = (i[:, None] > i[None, :])
    future = np.where(i[None, :] < i[:, None], -30000.0, 0.0)
    first = -((i[None, :] == i[:, None] + 1) & (i[:, None] % 2 == 0)).astype(np.float32)
    parts = [up_to, after, future, first]
    for level in range(DELTA_LEVELS):
        m = 2 << level
        parts.append(i[:, None] // m == 2 * np.arange(64 // m)[None, :] + 1)
    for level in range(DELTA_LEVELS):
        m = 2 << level
        parts.append(-(i[:, None] // m % 2 == 0).astype(np.float32))
    return np.concatenate([p.astype(np.float32) for p in parts], axis=1)


def gated_delta(core, w_dram, w_small_dram, bias_dram, rms_dram, masks_dram):
    nc = core.nc
    G, V, K, TAPS = GRAM_HEADS, 2, 4, 4
    EPS = 1e-6
    LV = DELTA_LEVELS
    PAD = TAPS - 1
    WQKV, WTAP, WGATE, WOUT = K * CT * 128, K * TAPS, CT * V * 128, V * C
    xt, ident, bank, psum = core.xt, core.ident, core.bank, core.psum
    LOG_TERMS = (1 / 15, 1 / 13, 1 / 11, 1 / 9, 1 / 7, 1 / 5, 1 / 3)
    with ExitStack() as ctx:
        def sb(name, shape, dt=F32):
            return core.sb(ctx, "a_" + name, shape, dt)

        def sem(name):
            return core.sem(ctx, "a_" + name)

        masks = sb("masks", [128, masks_dram.shape[1]])
        up_to, after, future, first_pairs = (masks[:, i * 128:(i + 1) * 128] for i in range(4))
        future_bf = sb("future_bf", [128, PER_BANK, 128], BF16)
        odd_rows, even_rows, at_col = [], [], 4 * 128
        for level in range(LV):
            odd_rows.append(masks[:, at_col:at_col + (32 >> level)])
            at_col += 32 >> level
        for level in range(LV):
            even_rows.append(masks[:, at_col + level:at_col + level + 1])

        w_qkv, taps = sb("w_qkv", [128, K, CT, 128]), sb("taps", [128, K, TAPS])
        w_gate, w_out = sb("w_gate", [128, CT, V * 128]), sb("w_out", [128, V, C])
        w_small, bias, rms_col = sb("w_small", [128, CT, 32]), sb("bias", [128, 2, 16]), sb("rms_col", [128, 1])
        beta, la = sb("beta", [128, V * G, B]), sb("log_alpha", [128, V * G, B])
        s0, s1, s2, s3 = (sb(f"small{i}", [128, V * G, B]) for i in range(4))
        pads = [sb(f"pad{k}", [128, B, PAD + S]) for k in range(K)]
        act_t = [sb(f"act_t{k}", [128, B, S]) for k in range(K)]
        squares = sb("squares", [128, 2, B, S])
        ss, norm, rr, r0, nt = (sb(n, [128, 2, B]) for n in ("ss", "norm", "rr", "r0", "nt"))
        length = sb("length", [128, B])
        cs = sb("cs", [128, V, B])
        steps = [sb(f"steps{v}", [128, B, S]) for v in range(V)]
        decay = [sb(f"decay{v}", [128, B, S]) for v in range(V)]
        lt = [sb(f"lt{v}", [128, B, S]) for v in range(V)]
        x_inv = [sb(f"x_inv{v}", [128, B, S]) for v in range(V)]
        xt_inv = [sb(f"xt_inv{v}", [128, B, S]) for v in range(V)]
        y_buf = [sb(f"y_buf{v}", [128, B, S]) for v in range(V)]
        rhs = [sb(f"rhs{v}", [128, B, S]) for v in range(V)]
        gate = sb("gate", [128, B, V, 128])
        sol = [sb(f"sol{v}", [128, B, 128]) for v in range(V)]
        out_ss, m2, n2, q2, t2 = (sb(n, [128, V, B]) for n in ("out_ss", "m2", "n2", "q2", "t2"))

        small_in, masks_in, wq_in, wg_in, wo_in = (sem(n) for n in ("small_in", "masks_in", "wq_in", "wg_in", "wo_in"))
        cleared, future_done, small_made, pre_a, pre_d = (
            sem(n) for n in ("cleared", "future_done", "small_made", "pre_a", "pre_d"))
        p_made, p_kept, tapped, silued = (sem(n) for n in ("p_made", "p_kept", "tapped", "silued"))
        sq_ready, ss_made, ss_ready, norm_ready, g_made, q_made, ss_out, out_norm, y_added = (
            sem(n) for n in ("sq_ready", "ss_made", "ss_ready", "norm_ready", "g_made", "q_made", "ss_out",
                             "out_norm", "y_added"))
        chain, gate_made, gate_kept, out_made, scratch, scratch_d, horner = (
            sem(n) for n in ("chain", "gate_made", "gate_kept", "out_made", "scratch", "scratch_d", "horner"))
        steps_ready, d_made, decay_ready, l_ready, a_ready, vt_made, rhs_ready, xt_first, xi_made, x_first = (
            [sem(f"{n}{v}") for v in range(V)] for n in
            ("steps_ready", "d_made", "decay_ready", "l_ready", "a_ready", "vt_made", "rhs_ready", "xt_first",
             "xi_made", "x_first"))
        w_made, w_kept, o_made, o_kept, ct_made, ct_kept = (
            [sem(f"{n}{v}") for v in range(V)] for n in ("w_made", "w_kept", "o_made", "o_kept", "ct_made", "ct_kept"))
        y_made, y_kept, u_made, x_kept, ut_made, xt_kept = (
            [sem(f"{n}{v}") for v in range(V)] for n in ("y_made", "y_kept", "u_made", "x_kept", "ut_made", "xt_kept"))

        CHAIN, POINTS = 15, 2 * LV

        def pair(v):
            return psum[:, (4 + 2 * v) * BANK:(6 + 2 * v) * BANK].rearrange("p (b t) -> p b t", b=B)

        def flat(t):
            return t[:].rearrange("p b t -> p (b t)")

        def even(t3, m):
            return t3.rearrange("p b (j two m) -> p b j two m", two=2, m=m)[:, :, :, 0, :]

        def odd(t3, m):
            return t3.rearrange("p b (j two m) -> p b j two m", two=2, m=m)[:, :, :, 1, :]

        def split(bank_ap, m):
            return bank_ap.rearrange("p (b j m) -> p b j m", b=B, m=m)

        def heads_of(eng, step):
            step(0, True, True)
            with eng.Fori(1, G - 1) as g:
                step(g, False, True)
            step(G - 1, False, False)

        with nc.Block() as block:

            @block.sync
            def _(sp):
                def row(g):
                    return w_dram[bass.ds(g, 1)].rearrange("o p c -> (o p) c")

                def load_qkv(g):
                    sp.dma_start(w_qkv[:].rearrange("p k t e -> p (k t e)"), row(g)[:, 0:WQKV]).then_inc(wq_in, 16)
                    sp.dma_start(taps[:].rearrange("p k j -> p (k j)"), row(g)[:, WQKV:WQKV + WTAP]).then_inc(wq_in, 16)

                def load_gate(g):
                    sp.dma_start(w_gate[:].rearrange("p t e -> p (t e)"),
                                 row(g)[:, WQKV + WTAP:WQKV + WTAP + WGATE]).then_inc(wg_in, 16)

                def load_out(g):
                    sp.dma_start(w_out[:].rearrange("p v c -> p (v c)"),
                                 row(g)[:, WQKV + WTAP + WGATE:]).then_inc(wo_in, 16)

                load_qkv(0)
                sp.dma_start(w_small[:].rearrange("p t e -> p (t e)"), w_small_dram).then_inc(small_in, 16)
                sp.dma_start(bias[:], bias_dram.unsqueeze(0).broadcast_to([128, 2, 16])).then_inc(small_in, 16)
                sp.dma_start(rms_col[:], rms_dram).then_inc(small_in, 16)
                sp.dma_start(masks[:], masks_dram).then_inc(masks_in, 16)
                load_gate(0)
                load_out(0)
                sp.wait_ge(tapped, K * TAPS)
                load_qkv(1)

                def reload(g, more):
                    sp.wait_ge(gate_made, 4 * g + 4)
                    load_gate(g + 1)
                    if more:
                        sp.wait_ge(tapped, K * TAPS * (g + 2))
                        load_qkv(g + 2)
                    sp.wait_ge(out_made, 4 * g + 4)
                    load_out(g + 1)

                with sp.Fori(0, G - 2) as g:
                    reload(g, True)
                reload(G - 2, False)

            @block.gpsimd
            def _(pool):
                for v in range(V):
                    nc.gpsimd.memset(y_buf[v][:], 0.0).then_inc(cleared, 1)
                for k in range(K):
                    nc.gpsimd.memset(pads[k][:], 0.0).then_inc(cleared, 1)
                pool.wait_ge(masks_in, 16)
                nc.gpsimd.tensor_copy(future_bf[:], future.unsqueeze(1).broadcast_to([128, PER_BANK, 128])).then_inc(future_done, 1)

                def square(g, kind):
                    pool.wait_ge(silued, K * g + kind + 1)
                    nc.gpsimd.tensor_tensor(squares[:, kind], act_t[kind][:], act_t[kind][:], ALU.mult).then_inc(sq_ready, 1)

                def make_steps(g, v):
                    nc.gpsimd.tensor_tensor(steps[v][:],
                                            la[:, bass.ds(V * g + v, 1), :].rearrange("p o b -> p (o b)").unsqueeze(2).broadcast_to([128, B, S]),
                                            up_to.unsqueeze(1).broadcast_to([128, B, S]), ALU.mult).then_inc(steps_ready[v], 1)

                def step(g, first, more):
                    for v in range(V):
                        pool.wait_ge(l_ready[v], g + 1)
                        if not first:
                            pool.wait_ge(w_made[v], g)
                        nc.gpsimd.tensor_tensor(xt_inv[v][:], lt[v][:], first_pairs.unsqueeze(1).broadcast_to([128, B, S]),
                                                ALU.mult).then_inc(scratch, 1)
                        pool.wait_ge(scratch, 2 * g + v + 1)
                        nc.gpsimd.tensor_tensor(xt_inv[v][:], xt_inv[v][:], ident[:].unsqueeze(1).broadcast_to([128, B, S]),
                                                ALU.add).then_inc(xt_first[v], 1)
                    if more:
                        for v in range(V):
                            pool.wait_ge(d_made[v], g + 1)
                            make_steps(g + 1, v)
                        pool.wait_ge(ss_made, g + 1)
                        for kind in range(2):
                            square(g + 1, kind)

                pool.wait_ge(pre_d, 17)
                for v in range(V):
                    make_steps(0, v)
                for kind in range(2):
                    square(0, kind)
                heads_of(pool, step)

            @block.tensor
            def _(pe):
                def project(g, n):
                    kind, half = n // 2, n % 2
                    for ct in range(CT):
                        mm = nc.tensor.matmul(bank[n % 4], w_qkv[:, kind, ct, :], xt[:, ct, half * BANK:(half + 1) * BANK],
                                              start=(ct == 0), stop=(ct == CT - 1))
                    mm.then_inc(p_made, 1)

                def project_gate(j):
                    for k in range(2):
                        b = 2 * j + k
                        for ct in range(CT):
                            mm = nc.tensor.matmul(bank[j][:, k * V * 128:(k + 1) * V * 128], xt[:, ct, b * S:(b + 1) * S],
                                                  w_gate[:, ct, :], start=(ct == 0), stop=(ct == CT - 1))
                    mm.then_inc(gate_made, 1)

                def point(g, i, more):
                    if i < 8 and more:
                        if i == 0:
                            pe.wait_ge(wq_in, 32 * (g + 2))
                        if i < 4:
                            for v in range(V):
                                pe.wait_ge(a_ready[v], g + 1)
                        else:
                            pe.wait_ge(p_kept, 8 * (g + 1) + i - 3)
                        project(g + 1, i)
                    if i >= 8:
                        if i == 8:
                            pe.wait_ge(wg_in, 16 * (g + 1))
                        if more:
                            pe.wait_ge(p_kept, 8 * (g + 1) + i - 3)
                        elif i == 8:
                            for v in range(V):
                                pe.wait_ge(a_ready[v], g + 1)
                        project_gate(i - 8)

                def step(g, first, more):
                    pe.wait_ge(sq_ready, 2 * g + 2)
                    if not first:
                        pe.wait_ge(ct_kept[0], g)
                    for kind in range(2):
                        for b in range(B):
                            mm = nc.tensor.matmul(bank[4][:, kind * B + b:kind * B + b + 1], squares[:, kind, b, :],
                                                  core.ones[:, 0:1], start=True, stop=True)
                    mm.then_inc(ss_made, 1)
                    pe.wait_ge(silued, K * g + 2)
                    if first:
                        pe.wait_ge(p_kept, 8)
                    else:
                        pe.wait_ge(y_added, 4 * g)
                    for kind, made in ((1, g_made), (0, q_made)):
                        for b in range(B):
                            o = (0 if kind == 1 else 2) * BANK + b * S
                            mm = nc.tensor.matmul(psum[:, o:o + S], act_t[1][:, b, :], act_t[kind][:, b, :],
                                                  start=True, stop=True)
                        mm.then_inc(made, 1)
                    for v in range(V):
                        pe.wait_ge(steps_ready[v], g + 1)
                        if v == 0:
                            pe.wait_ge(ss_ready, g + 1)
                        if not first:
                            pe.wait_ge(ct_kept[v], g)
                        for half in range(HALVES):
                            dst = bank[4 + 2 * v + half]
                            nc.tensor.matmul(dst, after, steps[v][:, half * PER_BANK:(half + 1) * PER_BANK, :].rearrange("p b t -> p (b t)"),
                                             start=True, stop=False)
                            mm = nc.tensor.matmul(dst, core.ident_bf[:], future_bf[:].rearrange("p b t -> p (b t)"), start=False, stop=True)
                        mm.then_inc(d_made[v], 1)
                    pe.wait_ge(silued, K * g + 4)
                    for v in range(V):
                        pe.wait_ge(decay_ready[v], g + 1)
                        for b in range(B):
                            mm = nc.tensor.transpose(pair(v)[:, b, :], act_t[2 + v][:, b, :], ident[:])
                        mm.then_inc(vt_made[v], 1)
                    for v in range(V):
                        pe.wait_ge(xt_first[v], g + 1)
                        pe.wait_ge(rhs_ready[v], g + 1)
                        for b in range(B):
                            mm = nc.tensor.transpose(pair(v)[:, b, :], xt_inv[v][:, b, :], ident[:])
                        mm.then_inc(xi_made[v], 1)
                    for level in range(LV):
                        m = 2 << level
                        for v in range(V):
                            if level == 0:
                                pe.wait_ge(x_first[v], g + 1)
                            else:
                                pe.wait_ge(x_kept[v], (LV - 1) * g + level)
                                pe.wait_ge(xt_kept[v], LV * g + level)
                            for b in range(B):
                                mm = nc.tensor.matmul(split(bank[4 + 2 * v], m)[:, b], lt[v][:, b, :],
                                                      even(x_inv[v][:], m)[:, b], start=True, stop=True)
                            mm.then_inc(y_made[v], 1)
                        point(g, 2 * level, more)
                        for v in range(V):
                            pe.wait_ge(y_kept[v], LV * g + level + 1)
                            if level < LV - 1:
                                for b in range(B):
                                    mm = nc.tensor.matmul(split(bank[5 + 2 * v], m)[:, b], xt_inv[v][:, b, :],
                                                          even(y_buf[v][:], m)[:, b], start=True, stop=True)
                                mm.then_inc(u_made[v], 1)
                            for b in range(B):
                                mm = nc.tensor.matmul(split(bank[4 + 2 * v], m)[:, b], y_buf[v][:, b, :],
                                                      odd(xt_inv[v][:], m)[:, b], start=True, stop=True)
                            mm.then_inc(ut_made[v], 1)
                        point(g, 2 * level + 1, more)
                    for v in range(V):
                        pe.wait_ge(xt_kept[v], LV * g + LV)
                        for b in range(B):
                            mm = nc.tensor.matmul(pair(v)[:, b, :], xt_inv[v][:, b, :], rhs[v][:, b, :], start=True, stop=True)
                        mm.then_inc(w_made[v], 1)
                    for v in range(V):
                        pe.wait_ge(w_kept[v], g + 1)
                        for b in range(B):
                            mm = nc.tensor.matmul(pair(v)[:, b, :], decay[v][:, b, :], sol[v][:, b, :], start=True, stop=True)
                        mm.then_inc(o_made[v], 1)
                    for v in range(V):
                        pe.wait_ge(o_kept[v], g + 1)
                        for b in range(B):
                            mm = nc.tensor.transpose(pair(v)[:, b, :], sol[v][:, b, :], ident[:])
                        mm.then_inc(ct_made[v], 1)
                    pe.wait_ge(wo_in, 16 * (g + 1))
                    for v in range(V):
                        pe.wait_ge(ct_kept[v], g + 1)
                    pe.wait_ge(gate_kept, 4 * g + 4)
                    for j in range(4):
                        for k in range(2):
                            b = 2 * j + k
                            for v in range(V):
                                mm = nc.tensor.matmul(bank[j][:, k * C:(k + 1) * C], rhs[v][:, b, :], w_out[:, v, :],
                                                      start=(v == 0), stop=(v == V - 1))
                        mm.then_inc(out_made, 1)

                pe.wait_ge(small_in, 48)
                for b in range(B):
                    for ct in range(CT):
                        mm = nc.tensor.matmul(bank[4][:, b * 32:(b + 1) * 32], xt[:, ct, b * S:(b + 1) * S], w_small[:, ct, :],
                                              start=(ct == 0), stop=(ct == CT - 1))
                mm.then_inc(small_made, 1)
                pe.wait_ge(wq_in, 32)
                for n in range(8):
                    if n >= 4:
                        pe.wait_ge(p_kept, n - 3)
                    project(0, n)
                pe.wait_ge(masks_in, 16)
                pe.wait_ge(future_done, 1)
                heads_of(pe, step)

            @block.scalar
            def _(act):
                def keep_projection(g, n):
                    kind, half = n // 2, n % 2
                    act.wait_ge(p_made, 8 * g + n + 1)
                    nc.scalar.copy(pads[kind][:, half * PER_BANK:(half + 1) * PER_BANK, PAD:],
                                   bank[n % 4].rearrange("p (b t) -> p b t", b=PER_BANK)).then_inc(p_kept, 1)

                def silu(g, kind):
                    act.wait_ge(tapped, K * TAPS * g + TAPS * (kind + 1))
                    nc.scalar.activation(flat(act_t[kind]), flat(act_t[kind]), ACT.Silu).then_inc(silued, 1)

                def keep_gate(g, j):
                    act.wait_ge(gate_made, 4 * g + j + 1)
                    nc.scalar.activation(gate[:, 2 * j:2 * j + 2].rearrange("p b v e -> p (b v e)"), bank[j], ACT.Silu).then_inc(gate_kept, 1)

                def point(g, i, more):
                    if more and i < 8:
                        keep_projection(g + 1, i)
                    if more and i >= 4 and i % 2 == 0:
                        silu(g + 1, (i - 4) // 2)
                    if i >= 8:
                        keep_gate(g, i - 8)

                def step(g, first, more):
                    act.wait_ge(ss_ready, g + 1)
                    nc.scalar.activation(norm[:], ss[:], ACT.Sqrt).then_inc(norm_ready, 1)
                    for v in range(V):
                        act.wait_ge(d_made[v], g + 1)
                        if not first:
                            act.wait_ge(o_made[v], g)
                        nc.scalar.activation(flat(decay[v]), pair(v).rearrange("p b t -> p (b t)"), ACT.Exp).then_inc(decay_ready[v], 1)
                    act.wait_ge(chain, CHAIN * g + 8)
                    for v in range(V):
                        act.wait_ge(vt_made[v], g + 1)
                        if not first:
                            act.wait_ge(out_made, 4 * g)
                        for b in range(B):
                            mm = nc.scalar.activation(rhs[v][:, b, :], pair(v)[:, b, :], ACT.Copy, scale=length[:, b:b + 1])
                        mm.then_inc(rhs_ready[v], 1)
                    for v in range(V):
                        act.wait_ge(xi_made[v], g + 1)
                        nc.scalar.copy(flat(x_inv[v]), pair(v).rearrange("p b t -> p (b t)")).then_inc(x_first[v], 1)
                    for i in range(POINTS):
                        point(g, i, more)
                    for v in range(V):
                        act.wait_ge(w_made[v], g + 1)
                        if not first:
                            act.wait_ge(ct_made[v], g)
                        nc.scalar.copy(flat(sol[v]), pair(v).rearrange("p b t -> p (b t)")).then_inc(w_kept[v], 1)
                    for v in range(V):
                        act.wait_ge(o_made[v], g + 1)
                        for b in range(B):
                            mm = nc.scalar.activation(x_inv[v][:, b, :], pair(v)[:, b, :], ACT.Square, accum_out=out_ss[:, v, b:b + 1])
                    mm.then_inc(ss_out, 1)
                    act.wait_ge(chain, CHAIN * g + 10)
                    nc.scalar.activation(n2[:], m2[:], ACT.Sqrt).then_inc(out_norm, 1)
                    for v in range(V):
                        act.wait_ge(ct_made[v], g + 1)
                        nc.scalar.activation(flat(rhs[v]), pair(v).rearrange("p b t -> p (b t)"), ACT.Copy, scale=rms_col[:]).then_inc(ct_kept[v], 1)

                act.wait_ge(pre_d, 2)
                nc.scalar.activation(s0[:], s0[:], ACT.Exp, scale=-1.0).then_inc(pre_a, 1)
                act.wait_ge(pre_d, 3)
                nc.scalar.activation(s2[:], s2[:], ACT.Exp).then_inc(pre_a, 1)
                nc.scalar.activation(bias[:, 1], bias[:, 1], ACT.Exp).then_inc(pre_a, 1)
                act.wait_ge(cleared, V + K)
                for n in range(8):
                    keep_projection(0, n)
                for kind in range(K):
                    silu(0, kind)
                heads_of(act, step)

            @block.vector
            def _(dve):
                vec = nc.vector

                def tap(g, kind, j):
                    n = K * TAPS * g + TAPS * kind + j
                    src = pads[kind][:, :, j:j + S]
                    if j == 0:
                        dve.wait_ge(wq_in, 32 * (g + 1))
                        dve.wait_ge(p_kept, 8 * g + 2 * kind + 2)
                        vec.tensor_scalar(act_t[kind][:], src, taps[:, kind, 0:1], None, ALU.mult).then_inc(tapped, 1)
                    else:
                        dve.wait_ge(tapped, n)
                        vec.scalar_tensor_tensor(out=act_t[kind][:], in0=src, scalar=taps[:, kind, j:j + 1], in1=act_t[kind][:],
                                                 op0=ALU.mult, op1=ALU.add).then_inc(tapped, 1)

                def point(g, i, more):
                    if more and 2 <= i < 10:
                        n = 2 * (i - 2)
                        if i == 2:
                            dve.wait_ge(q_made, g + 1)
                        if i == 6:
                            for v in range(V):
                                dve.wait_ge(vt_made[v], g + 1)
                        for t in (n, n + 1):
                            tap(g + 1, t // TAPS, t % TAPS)

                def step(g, first, more):
                    def link(i):
                        dve.wait_ge(chain, CHAIN * g + i)

                    dve.wait_ge(ss_made, g + 1)
                    vec.tensor_scalar(ss[:].rearrange("p k b -> p (k b)"), bank[4][:, 0:2 * B], EPS, None, ALU.add).then_inc(ss_ready, 1)
                    dve.wait_ge(ss_ready, g + 1)
                    vec.reciprocal(rr[:], ss[:]).then_inc(chain, 1)
                    link(1)
                    vec.tensor_tensor(cs[:], beta[:, bass.ds(V * g, V), :], rr[:, 1:2].broadcast_to([128, V, B]), ALU.mult).then_inc(chain, 1)
                    dve.wait_ge(norm_ready, g + 1)
                    vec.reciprocal(r0[:], norm[:]).then_inc(chain, 1)
                    link(3)
                    vec.tensor_tensor(nt[:], r0[:], r0[:], ALU.mult).then_inc(chain, 1)
                    link(4)
                    vec.tensor_tensor(nt[:], nt[:], ss[:], ALU.mult).then_inc(chain, 1)
                    link(5)
                    vec.tensor_scalar(nt[:], nt[:], -0.5, 1.5, ALU.mult, ALU.add).then_inc(chain, 1)
                    link(6)
                    vec.tensor_tensor(r0[:], r0[:], nt[:], ALU.mult).then_inc(chain, 1)
                    link(7)
                    vec.tensor_tensor(length[:], r0[:, 1], ss[:, 1], ALU.mult).then_inc(chain, 1)
                    for v in range(V):
                        dve.wait_ge(decay_ready[v], g + 1)
                        dve.wait_ge(g_made, g + 1)
                        for b in range(B):
                            mm = vec.scalar_tensor_tensor(out=lt[v][:, b, :], in0=decay[v][:, b, :], scalar=cs[:, v, b:b + 1],
                                                          in1=psum[:, b * S:(b + 1) * S], op0=ALU.mult, op1=ALU.mult)
                        mm.then_inc(l_ready[v], 1)
                    for v in range(V):
                        dve.wait_ge(q_made, g + 1)
                        dve.wait_ge(l_ready[v], g + 1)
                        for b in range(B):
                            o = 2 * BANK + b * S
                            mm = vec.scalar_tensor_tensor(out=decay[v][:, b, :], in0=decay[v][:, b, :], scalar=cs[:, v, b:b + 1],
                                                          in1=psum[:, o:o + S], op0=ALU.mult, op1=ALU.mult)
                        mm.then_inc(a_ready[v], 1)
                    for level in range(LV):
                        m = 2 << level
                        for v in range(V):
                            dve.wait_ge(y_made[v], LV * g + level + 1)
                            vec.tensor_tensor(even(y_buf[v][:], m), split(bank[4 + 2 * v], m),
                                              odd_rows[level].unsqueeze(1).unsqueeze(3).broadcast_to([128, B, 64 // m, m]),
                                              ALU.mult).then_inc(y_kept[v], 1)
                        point(g, 2 * level, more)
                        for v in range(V):
                            if level < LV - 1:
                                dve.wait_ge(u_made[v], (LV - 1) * g + level + 1)
                                vec.tensor_tensor(even(x_inv[v][:], m), even(x_inv[v][:], m), split(bank[5 + 2 * v], m),
                                                  ALU.subtract).then_inc(x_kept[v], 1)
                            dve.wait_ge(ut_made[v], LV * g + level + 1)
                            vec.scalar_tensor_tensor(out=odd(xt_inv[v][:], m), in0=split(bank[4 + 2 * v], m),
                                                     scalar=even_rows[level], in1=odd(xt_inv[v][:], m),
                                                     op0=ALU.mult, op1=ALU.add).then_inc(xt_kept[v], 1)
                        point(g, 2 * level + 1, more)
                    dve.wait_ge(ss_out, g + 1)
                    vec.tensor_tensor(m2[:], out_ss[:], rr[:, 0:1].broadcast_to([128, V, B]), ALU.mult).then_inc(chain, 1)
                    link(9)
                    vec.tensor_scalar(m2[:], m2[:], 1.0 / (128 * 128), EPS, ALU.mult, ALU.add).then_inc(chain, 1)
                    dve.wait_ge(out_norm, g + 1)
                    vec.reciprocal(q2[:], n2[:]).then_inc(chain, 1)
                    link(11)
                    vec.tensor_tensor(t2[:], q2[:], q2[:], ALU.mult).then_inc(chain, 1)
                    link(12)
                    vec.tensor_tensor(t2[:], t2[:], m2[:], ALU.mult).then_inc(chain, 1)
                    link(13)
                    vec.tensor_scalar(t2[:], t2[:], -0.5 * 128 ** -0.5, 1.5 * 128 ** -0.5, ALU.mult, ALU.add).then_inc(chain, 1)
                    link(14)
                    vec.tensor_tensor(q2[:], q2[:], t2[:], ALU.mult).then_inc(scratch_d, 1)
                    dve.wait_ge(scratch_d, g + 1)
                    vec.tensor_tensor(q2[:], q2[:], r0[:, 0:1].broadcast_to([128, V, B]), ALU.mult).then_inc(chain, 1)
                    link(15)
                    dve.wait_ge(gate_kept, 4 * g + 4)
                    for v in range(V):
                        dve.wait_ge(o_made[v], g + 1)
                        for b in range(B):
                            mm = vec.scalar_tensor_tensor(out=sol[v][:, b, :], in0=pair(v)[:, b, :], scalar=q2[:, v, b:b + 1],
                                                          in1=gate[:, b, v, :], op0=ALU.mult, op1=ALU.mult)
                        mm.then_inc(o_kept[v], 1)
                    for j in range(4):
                        dve.wait_ge(out_made, 4 * g + j + 1)
                        if not first:
                            dve.wait_ge(y_added, 4 * (g - 1) + j + 1)
                        res = core.x if first else core.y
                        vec.tensor_tensor(core.y[:, 2 * j:2 * j + 2, :], res[:, 2 * j:2 * j + 2, :],
                                          bank[j].rearrange("p (b c) -> p b c", b=2), ALU.add).then_inc(y_added, 1)

                dve.wait_ge(small_made, 1)
                dve.wait_ge(small_in, 48)

                def pre(i):
                    dve.wait_ge(pre_d, i)

                proj = bank[4][:, 0:B * 32].rearrange("p (b h) -> p h b", b=B)
                vec.tensor_tensor(s1[:], proj[:, 16:32, :], bias[:, 0, :].unsqueeze(2).broadcast_to([128, 16, B]), ALU.add).then_inc(pre_d, 1)
                vec.tensor_copy(s0[:], proj[:, 0:16, :]).then_inc(pre_d, 1)
                pre(1)
                vec.scalar_tensor_tensor(out=s2[:], in0=s1[:], scalar=-1.0, in1=s1[:], op0=ALU.mult, op1=ALU.min).then_inc(pre_d, 1)
                dve.wait_ge(pre_a, 1)
                vec.tensor_scalar(s0[:], s0[:], 1.0, None, ALU.add).then_inc(pre_d, 1)
                pre(4)
                vec.reciprocal(beta[:], s0[:]).then_inc(pre_d, 1)
                dve.wait_ge(pre_a, 2)
                pre(5)
                vec.tensor_scalar(s0[:], s2[:], 2.0, None, ALU.add).then_inc(pre_d, 1)
                pre(6)
                vec.reciprocal(s0[:], s0[:]).then_inc(pre_d, 1)
                pre(7)
                vec.tensor_tensor(s2[:], s2[:], s0[:], ALU.mult).then_inc(pre_d, 1)
                pre(8)
                vec.tensor_tensor(s3[:], s2[:], s2[:], ALU.mult).then_inc(pre_d, 1)
                pre(9)
                vec.tensor_scalar(s0[:], s3[:], LOG_TERMS[0], LOG_TERMS[1], ALU.mult, ALU.add).then_inc(pre_d, 1)
                pre(10)
                for i, c in enumerate(LOG_TERMS[2:] + (1.0,)):
                    vec.tensor_tensor(s0[:], s0[:], s3[:], ALU.mult).then_inc(horner, 1)
                    dve.wait_ge(horner, 2 * i + 1)
                    vec.tensor_scalar(s0[:], s0[:], c, None, ALU.add).then_inc(horner, 1)
                    dve.wait_ge(horner, 2 * i + 2)
                vec.tensor_tensor(s0[:], s0[:], s2[:], ALU.mult).then_inc(pre_d, 1)
                vec.tensor_scalar(s1[:], s1[:], 0.0, None, ALU.max).then_inc(pre_d, 1)
                pre(12)
                vec.tensor_scalar(s0[:], s0[:], 2.0, None, ALU.mult).then_inc(pre_d, 1)
                pre(13)
                vec.tensor_tensor(s1[:], s0[:], s1[:], ALU.add).then_inc(pre_d, 1)
                dve.wait_ge(pre_a, 3)
                pre(14)
                vec.tensor_tensor(s1[:], s1[:], bias[:, 1, :].unsqueeze(2).broadcast_to([128, 16, B]), ALU.mult).then_inc(pre_d, 1)
                pre(15)
                vec.tensor_scalar(la[:], s1[:], -1.0, None, ALU.mult).then_inc(pre_d, 2)
                pre(17)
                dve.wait_ge(cleared, V + K)
                dve.wait_ge(masks_in, 16)
                for kind in range(K):
                    for j in range(TAPS):
                        tap(0, kind, j)
                heads_of(dve, step)


def rotary_cross_attention(core, ctx_dram, w_dram, cols_dram, bv_dram, enc_dram, sign_dram):
    nc = core.nc
    HEADS, D, P = 16, 8, C
    SCALE = float(D) ** -0.5
    G = 4
    PT = P // 128
    UNITS = 2 * (HEADS // G) * PT
    HALF_UNITS = UNITS // 2
    psum, bank, ident = core.psum, core.bank, core.ident
    with ExitStack() as ctx:
        def sb(name, shape, dt=F32):
            return core.sb(ctx, "b_" + name, shape, dt)

        def sem(name):
            return core.sem(ctx, "b_" + name)

        w = sb("w", [128, 6, 128])
        cols, bv, sign = sb("cols", [128, 5]), sb("bv", [128, 128]), sb("sign", [128, 1])
        enc = sb("enc", [128, 2, P])
        src = [sb(f"src{s}", [128, P]) for s in range(2)]
        t1, t2 = sb("t1", [128, P]), sb("t2", [128, P])
        qr, kr = sb("qr", [128, P]), sb("kr", [128, P])
        q = [sb(f"q{s}", [D, HEADS, P]) for s in range(2)]
        k = [sb(f"k{s}", [D, HEADS, P]) for s in range(2)]
        v = [sb(f"v{s}", [128, PT, HEADS * D]) for s in range(2)]
        probs = [sb(f"probs{i}", [128, G, P]) for i in range(2)]
        probs_t = [sb(f"probs_t{i}", [128, G * PT, 128]) for i in range(2)]
        top, neg_top, total, inv = ([sb(f"{n}{i}", [128, G]) for i in range(2)] for n in ("top", "neg_top", "total", "inv"))
        att = [sb(f"att{s}", [128, PT, HEADS * D]) for s in range(2)]
        att_t = sb("att_t", [128, P])

        w_in, sign_done, t1_done, t2_done = sem("w_in"), sem("sign_done"), sem("t1_done"), sem("t2_done")
        src_in = [sem(f"src_in{s}") for s in range(2)]
        heads_in = [sem(f"heads_in{s}") for s in range(2)]
        q_made, k_made, v_made, q_read, k_read, q_rot, k_rot, v_kept, att_turned, att_kept, out_made, y_done = (
            sem(n) for n in ("q_made", "k_made", "v_made", "q_read", "k_read", "q_rot", "k_rot", "v_kept",
                             "att_turned", "att_kept", "out_made", "y_done"))
        s_made, top_ready, neg_ready, exp_done, t_made, kept_a, kept_d, pv_made, inv_ready, pv_kept = (
            sem(n) for n in ("s_made", "top_ready", "neg_ready", "exp_done", "t_made", "kept_a", "kept_d",
                             "pv_made", "inv_ready", "pv_kept"))

        def place(u):
            return u // HALF_UNITS, (u % HALF_UNITS) // PT, u % PT

        def at(i, u):
            return UNITS * i + (u + 1)

        with nc.Block() as block:

            @block.sync
            def _(sp):
                sp.dma_start(w[:].rearrange("p k o -> p (k o)"), w_dram).then_inc(w_in, 16)
                sp.dma_start(cols[:], cols_dram).then_inc(w_in, 16)
                sp.dma_start(sign[:], sign_dram).then_inc(w_in, 16)
                sp.dma_start(bv[:], bv_dram.unsqueeze(0).broadcast_to([128, 128])).then_inc(w_in, 16)
                for d in range(D):
                    sp.dma_start(enc[d * HEADS:(d + 1) * HEADS, :, :],
                                 enc_dram[:, d, :].unsqueeze(0).broadcast_to([HEADS, 2, P])).then_inc(w_in, 16)

                def load(b, s):
                    sp.dma_start(src[s][:], ctx_dram[bass.ds(b, 1)].rearrange("o s p -> (o s) p")).then_inc(src_in[s], 16)

                def spread(b, s):
                    sp.wait_ge(q_rot, b + 1)
                    sp.dma_start(q[s][:], qr[:]).then_inc(heads_in[s], 16)
                    sp.wait_ge(k_rot, b + 1)
                    sp.dma_start(k[s][:], kr[:]).then_inc(heads_in[s], 16)

                load(0, 0)
                load(1, 1)
                spread(0, 0)
                spread(1, 1)
                with sp.Fori(0, B // 2 - 1) as i:
                    for s in range(2):
                        b = 2 * i + 2 + s
                        sp.wait_ge(v_made, b - 1)
                        load(b, s)
                        spread(b, s)

            @block.tensor
            def _(pe):
                def project(kind, s, rhs, made):
                    for j in range(2):
                        mm = nc.tensor.matmul(bank[7][:, j * P:(j + 1) * P], w[:, kind + j, :], rhs, start=True, stop=True)
                    mm.then_inc(made, 1)

                def prepare_q(b, s, first=False):
                    if not first:
                        pe.wait_ge(v_kept, b)
                    project(0, s, core.x[:, bass.ds(b, 1), :].rearrange("p o c -> p (o c)"), q_made)

                def prepare_k(b, s):
                    pe.wait_ge(src_in[s], 8 * (b - s) + 16)
                    pe.wait_ge(q_read, b + 1)
                    project(2, s, src[s][:], k_made)

                def prepare_v(b, s):
                    pe.wait_ge(k_read, b + 1)
                    for t in range(PT):
                        mm = nc.tensor.matmul(bank[7][:, t * 128:(t + 1) * 128], src[s][:, t * 128:(t + 1) * 128],
                                              w[:, 4, :], start=True, stop=True)
                    mm.then_inc(v_made, 1)

                def turn_att(b, s):
                    pe.wait_ge(pv_kept, HALF_UNITS * (b + 1))
                    for t in range(PT):
                        mm = nc.tensor.transpose(bank[7][:, t * 128:(t + 1) * 128], att[s][:, t, :], ident[:])
                    mm.then_inc(att_turned, 1)

                def output(b):
                    pe.wait_ge(att_kept, b + 1)
                    nc.tensor.matmul(bank[7][:, 0:P], w[:, 5, :], att_t[:], start=True, stop=True).then_inc(out_made, 1)

                def scores(i, u, first=False):
                    s, g, t = place(u)
                    if u % HALF_UNITS == 0:
                        pe.wait_ge(heads_in[s], 32 * i + 32)
                    if not first:
                        pe.wait_ge(exp_done, at(i, u - 2))
                    for j in range(G):
                        o = (2 * (u % 2)) * BANK + j * P
                        mm = nc.tensor.matmul(psum[:, o:o + P], q[s][:, g * G + j, t * 128:(t + 1) * 128],
                                              k[s][:, g * G + j, :], start=True, stop=True)
                    mm.then_inc(s_made, 1)

                def turn_probs(i, u, first=False):
                    pe.wait_ge(exp_done, at(i, u))
                    if not first:
                        pe.wait_ge(kept_a, at(i, u - 1))
                        pe.wait_ge(kept_d, at(i, u - 1))
                    for j in range(G):
                        for m in range(PT):
                            o = 4 * BANK + (j * PT + m) * 128
                            mm = nc.tensor.transpose(psum[:, o:o + 128], probs[u % 2][:, j, m * 128:(m + 1) * 128], ident[:])
                    mm.then_inc(t_made, 1)

                def mix(i, u, first=False):
                    s, g, t = place(u)
                    pe.wait_ge(kept_a, at(i, u))
                    pe.wait_ge(kept_d, at(i, u))
                    if not first:
                        pe.wait_ge(pv_kept, at(i, u - 1))
                    for j in range(G):
                        for m in range(PT):
                            h = g * G + j
                            mm = nc.tensor.matmul(bank[6][:, j * D:(j + 1) * D], probs_t[u % 2][:, j * PT + m, :],
                                                  v[s][:, m, h * D:(h + 1) * D], start=(m == 0), stop=(m == PT - 1))
                    mm.then_inc(pv_made, 1)

                def pair(i, first, more):
                    for u in range(UNITS):
                        s, step = u // HALF_UNITS, u % HALF_UNITS
                        b = 2 * i + s
                        if u + 2 < UNITS:
                            scores(i, u + 2)
                        elif more:
                            scores(i + 1, u + 2 - UNITS)
                        turn_probs(i, u, first and u == 0)
                        if u > 0:
                            mix(i, u - 1, first and u == 1)
                        elif not first:
                            mix(i - 1, UNITS - 1)
                        if more or s == 0:
                            if step == 0:
                                if not (first and s == 0):
                                    if first and s == 1:
                                        pe.wait_ge(v_kept, 2)
                                    else:
                                        pe.wait_ge(y_done, b - 1)
                                prepare_q(b + 1, 1 - s)
                            elif step == 1:
                                prepare_k(b + 1, 1 - s)
                            elif step == 2:
                                prepare_v(b + 1, 1 - s)
                        if not (first and s == 0):
                            if step == 3:
                                pe.wait_ge(v_kept, (b + 2) if (more or s == 0) else B)
                                if not (first and s == 1):
                                    pe.wait_ge(y_done, b - 1)
                                turn_att(b - 1, 1 - s)
                            elif step == 4:
                                output(b - 1)

                pe.wait_ge(w_in, 16 * (4 + D))
                prepare_q(0, 0, True)
                prepare_k(0, 0)
                prepare_v(0, 0)
                scores(0, 0, True)
                scores(0, 1, True)
                pair(0, True, True)
                with pe.Fori(1, B // 2 - 1) as i:
                    pair(i, False, True)
                pair(B // 2 - 1, False, False)
                mix(B // 2 - 1, UNITS - 1)
                pe.wait_ge(y_done, B - 1)
                turn_att(B - 1, 1)
                output(B - 1)

            @block.scalar
            def _(act):
                def exps(i, u):
                    act.wait_ge(neg_ready, at(i, u))
                    for j in range(G):
                        o = (2 * (u % 2)) * BANK + j * P
                        ex = nc.scalar.activation(probs[u % 2][:, j, :], psum[:, o:o + P], ACT.Exp,
                                                  bias=neg_top[u % 2][:, j:j + 1], scale=SCALE,
                                                  accum_out=total[u % 2][:, j:j + 1])
                    ex.then_inc(exp_done, 1)

                def keep_probs(i, u):
                    act.wait_ge(t_made, at(i, u))
                    nc.scalar.copy(probs_t[u % 2][:, 0:G * PT // 2, :].rearrange("p m n -> p (m n)"),
                                   bank[4]).then_inc(kept_a, 1)

                def keep_att(b):
                    act.wait_ge(att_turned, b + 1)
                    nc.scalar.copy(att_t[:], bank[7][:, 0:P]).then_inc(att_kept, 1)

                def pair(i, first, more):
                    for u in range(UNITS):
                        s, step = u // HALF_UNITS, u % HALF_UNITS
                        if u + 1 < UNITS:
                            exps(i, u + 1)
                        elif more:
                            exps(i + 1, 0)
                        keep_probs(i, u)
                        if step == 3 and not (first and s == 0):
                            keep_att(2 * i + s - 1)

                exps(0, 0)
                pair(0, True, True)
                with act.Fori(1, B // 2 - 1) as i:
                    pair(i, False, True)
                pair(B // 2 - 1, False, False)
                keep_att(B - 1)

            @block.vector
            def _(dve):
                vec = nc.vector

                def rotate(b, col, made, read, rot, out, first_of_kind):
                    dve.wait_ge(made, b + 1)
                    if first_of_kind is not None:
                        dve.wait_ge(first_of_kind[0], first_of_kind[1])
                    vec.scalar_tensor_tensor(out=t1[:], in0=bank[7][:, 0:P], scalar=cols[:, col:col + 1],
                                             in1=enc[:, 0, :], op0=ALU.add, op1=ALU.mult)
                    vec.scalar_tensor_tensor(out=t2[:], in0=bank[7][:, P:2 * P], scalar=cols[:, col + 1:col + 2],
                                             in1=enc[:, 1, :], op0=ALU.add, op1=ALU.mult).then_inc(read, 1)
                    dve.wait_ge(read, b + 1)
                    vec.tensor_tensor(out[:], t1[:], t2[:], ALU.add).then_inc(rot, 1)

                def rotate_q(b, s, again=True):
                    rotate(b, 0, q_made, q_read, q_rot, qr, sent(b, s) if again else None)

                def rotate_k(b, s, again=True):
                    dve.wait_ge(q_rot, b + 1)
                    rotate(b, 2, k_made, k_read, k_rot, kr, sent(b, s) if again else None)

                def sent(b, s):
                    return heads_in[1 - s], 16 * (b + s)

                def keep_v(b, s):
                    dve.wait_ge(v_made, b + 1)
                    vec.tensor_tensor(v[s][:], bank[7][:, 0:P].rearrange("p (t o) -> p t o", t=PT),
                                      bv[:].unsqueeze(1).broadcast_to([128, PT, 128]), ALU.add).then_inc(v_kept, 1)

                def finish(b):
                    dve.wait_ge(out_made, b + 1)
                    vec.scalar_tensor_tensor(out=core.y[:, bass.ds(b, 1), :].rearrange("p o c -> p (o c)"),
                                             in0=bank[7][:, 0:P], scalar=cols[:, 4:5],
                                             in1=core.x[:, bass.ds(b, 1), :].rearrange("p o c -> p (o c)"),
                                             op0=ALU.add, op1=ALU.add).then_inc(y_done, 1)

                def maxima(i, u):
                    dve.wait_ge(s_made, at(i, u))
                    o = (2 * (u % 2)) * BANK
                    vec.tensor_reduce(top[u % 2][:], psum[:, o:o + G * P].rearrange("p (j m) -> p j m", j=G), AX.X,
                                      ALU.max).then_inc(top_ready, 1)
                    dve.wait_ge(top_ready, at(i, u))
                    vec.tensor_scalar(neg_top[u % 2][:], top[u % 2][:], -SCALE, None, ALU.mult).then_inc(neg_ready, 1)

                def keep_probs(i, u, first=False):
                    dve.wait_ge(t_made, at(i, u))
                    if u >= 2 or not first:
                        dve.wait_ge(pv_kept, at(i, u - 2))
                    vec.tensor_copy(probs_t[u % 2][:, G * PT // 2:, :].rearrange("p m n -> p (m n)"),
                                    bank[5]).then_inc(kept_d, 1)
                    vec.reciprocal(inv[u % 2][:], total[u % 2][:]).then_inc(inv_ready, 1)

                def keep_mix(i, u):
                    s, g, t = place(u)
                    dve.wait_ge(inv_ready, at(i, u))
                    dve.wait_ge(pv_made, at(i, u))
                    vec.tensor_tensor(att[s][:, t, g * G * D:(g + 1) * G * D].rearrange("p (j d) -> p j d", j=G),
                                      bank[6][:, 0:G * D].rearrange("p (j d) -> p j d", j=G),
                                      inv[u % 2][:].unsqueeze(2).broadcast_to([128, G, D]), ALU.mult).then_inc(pv_kept, 1)

                def pair(i, first, more):
                    for u in range(UNITS):
                        s, step = u // HALF_UNITS, u % HALF_UNITS
                        b = 2 * i + s
                        keep_probs(i, u, first)
                        if u + 2 < UNITS:
                            maxima(i, u + 2)
                        elif more:
                            maxima(i + 1, u + 2 - UNITS)
                        if u > 0:
                            keep_mix(i, u - 1)
                        elif not first:
                            keep_mix(i - 1, UNITS - 1)
                        if more or s == 0:
                            if step == 0:
                                rotate_q(b + 1, 1 - s)
                            elif step == 1:
                                rotate_k(b + 1, 1 - s)
                            elif step == 2:
                                keep_v(b + 1, 1 - s)
                        if not (first and s == 0) and step == 4:
                            finish(b - 1)

                dve.wait_ge(w_in, 16 * (4 + D))
                vec.tensor_scalar(enc[:, 1, :], enc[:, 1, :], sign[:], None, ALU.mult).then_inc(sign_done, 1)
                dve.wait_ge(sign_done, 1)
                rotate_q(0, 0, False)
                rotate_k(0, 0, False)
                keep_v(0, 0)
                maxima(0, 0)
                maxima(0, 1)
                pair(0, True, True)
                with dve.Fori(1, B // 2 - 1) as i:
                    pair(i, False, True)
                pair(B // 2 - 1, False, False)
                keep_mix(B // 2 - 1, UNITS - 1)
                finish(B - 1)


def route_tokens(core, sim_dram, gates_dram, weights_dram):
    nc = core.nc
    EX = 16
    FIRST = 64.0
    with ExitStack() as ctx:
        def sb(name, shape, dt=F32):
            return core.sb(ctx, "r_" + name, shape, dt)

        def sem(name):
            return core.sem(ctx, "r_" + name)

        sim, sim_sq = sb("sim", [128, CT, EX]), sb("sim_sq", [128, CT, EX])
        gates, number = sb("gates", [128, EX]), sb("number", [128, EX])
        sim_len, x_len = sb("sim_len", [128, EX]), sb("x_len", [128, B])
        x_sq = sb("x_sq", [128, B])
        logits, e_all, is_on, key, pick1, pick2, low = (
            sb(n, [128, B, EX]) for n in ("logits", "e_all", "is_on", "key", "pick1", "pick2", "low"))
        top, top2, first, idle, total = (sb(n, [128, B]) for n in ("top", "top2", "first", "idle", "total"))
        w_t = sb("w_t", [EX, N])
        inputs_in, number_ready, sim_sq_ready, sim_sums, logits_made, w_turned = (
            sem(n) for n in ("inputs_in", "number_ready", "sim_sq_ready", "sim_sums", "logits_made", "w_turned"))
        act_step, step, w_kept, stored = (sem(n) for n in ("act_step", "step", "w_kept", "stored"))
        sums, raw = core.bank[7][:, 0:EX], core.bank[6][:, 0:B * EX].rearrange("p (b e) -> p b e", b=B)

        def over_e(t):
            return t[:].unsqueeze(2).broadcast_to([128, B, EX])

        def over_b(t):
            return t[:].unsqueeze(1).broadcast_to([128, B, EX])

        with nc.Block() as block:

            @block.sync
            def _(sp):
                sp.dma_start(sim[:], sim_dram.rearrange("(t p) e -> p t e", p=128)).then_inc(inputs_in, 16)
                sp.dma_start(gates[:], gates_dram.unsqueeze(0).broadcast_to([128, EX])).then_inc(inputs_in, 16)
                sp.wait_ge(w_kept, 2)
                sp.dma_start(weights_dram, w_t[:]).then_inc(stored, 16)
                sp.wait_ge(stored, 16)

            @block.gpsimd
            def _(pool):
                nc.gpsimd.iota(number[:], [[1, EX]], base=0, channel_multiplier=0,
                               allow_small_or_imprecise_dtypes=True).then_inc(number_ready, 1)

            @block.tensor
            def _(pe):
                pe.wait_ge(sim_sq_ready, 1)
                for ct in range(CT):
                    mm = nc.tensor.matmul(sums, core.ones[:], sim_sq[:, ct, :], start=(ct == 0), stop=(ct == CT - 1))
                mm.then_inc(sim_sums, 1)
                pe.wait_ge(step, 3)
                for b in range(B):
                    for ct in range(CT):
                        mm = nc.tensor.matmul(raw[:, b, :], core.xt[:, ct, b * S:(b + 1) * S], sim[:, ct, :],
                                              start=(ct == 0), stop=(ct == CT - 1))
                mm.then_inc(logits_made, 1)
                pe.wait_ge(step, LAST)
                for b in range(B):
                    mm = nc.tensor.transpose(core.bank[4 + b // PER_BANK][0:EX, (b % PER_BANK) * S:(b % PER_BANK + 1) * S],
                                             e_all[:, b, :], core.ident[:])
                mm.then_inc(w_turned, 1)

            @block.scalar
            def _(act):
                for b in range(B):
                    sq = nc.scalar.activation(core.y[:, b, :], core.x[:, b, :], ACT.Square, accum_out=x_sq[:, b:b + 1])
                sq.then_inc(act_step, 1)
                act.wait_ge(act_step, 1)
                nc.scalar.activation(x_len[:], x_sq[:], ACT.Sqrt).then_inc(act_step, 1)
                act.wait_ge(sim_sums, 1)
                nc.scalar.activation(sim_len[:], sums, ACT.Sqrt).then_inc(act_step, 1)
                act.wait_ge(inputs_in, 32)
                nc.scalar.activation(gates[:], gates[:], ACT.Exp, scale=-1.0).then_inc(act_step, 1)
                act.wait_ge(step, SHIFTED)
                nc.scalar.activation(e_all[:], e_all[:], ACT.Exp).then_inc(act_step, 1)
                act.wait_ge(w_turned, 1)
                for half in range(HALVES):
                    nc.scalar.copy(w_t[:, half * BANK:(half + 1) * BANK],
                                   core.bank[4 + half][0:EX, :]).then_inc(w_kept, 1)

            @block.vector
            def _(dve):
                v = nc.vector
                dve.wait_ge(inputs_in, 32)
                v.tensor_tensor(sim_sq[:], sim[:], sim[:], ALU.mult).then_inc(sim_sq_ready, 1)
                dve.wait_ge(act_step, 3)
                v.tensor_scalar(sim_len[:], sim_len[:], 1e-12, None, ALU.max).then_inc(step, 1)
                dve.wait_ge(step, 1)
                v.reciprocal(sim_len[:], sim_len[:]).then_inc(step, 1)
                dve.wait_ge(step, 2)
                v.tensor_tensor(sim[:], sim[:], sim_len[:].unsqueeze(1).broadcast_to([128, CT, EX]),
                                ALU.mult).then_inc(step, 1)
                v.tensor_scalar(x_len[:], x_len[:], 1e-12, None, ALU.max).then_inc(step, 1)
                dve.wait_ge(step, 4)
                v.reciprocal(x_len[:], x_len[:]).then_inc(step, 1)
                dve.wait_ge(act_step, 4)
                v.tensor_scalar(gates[:], gates[:], 1.0, None, ALU.add).then_inc(step, 1)
                dve.wait_ge(step, 6)
                v.reciprocal(gates[:], gates[:]).then_inc(step, 1)
                dve.wait_ge(logits_made, 1)
                dve.wait_ge(step, 7)
                v.tensor_tensor(logits[:], raw, over_e(x_len), ALU.mult).then_inc(step, 1)
                dve.wait_ge(step, 8)
                v.tensor_tensor(logits[:], logits[:], over_b(gates), ALU.subtract).then_inc(step, 1)
                dve.wait_ge(step, 9)
                v.tensor_reduce(top[:], logits[:], AX.X, ALU.max).then_inc(step, 1)
                dve.wait_ge(step, 10)
                v.tensor_tensor(e_all[:], logits[:], over_e(top), ALU.subtract).then_inc(step, 1)
                v.tensor_scalar(is_on[:], logits[:], 0.0, None, ALU.is_gt).then_inc(step, 1)
                v.tensor_scalar(idle[:], top[:], 0.0, None, ALU.is_le).then_inc(step, 1)
                dve.wait_ge(number_ready, 1)
                v.tensor_tensor(pick1[:], logits[:], over_e(top), ALU.is_equal).then_inc(step, 1)
                dve.wait_ge(step, 14)
                v.scalar_tensor_tensor(out=key[:], in0=pick1[:], scalar=-FIRST, in1=over_b(number),
                                       op0=ALU.mult, op1=ALU.add).then_inc(step, 1)
                dve.wait_ge(step, 15)
                v.tensor_reduce(first[:], key[:], AX.X, ALU.min).then_inc(step, 1)
                dve.wait_ge(step, 16)
                v.tensor_tensor(pick1[:], key[:], over_e(first), ALU.is_equal).then_inc(step, 1)
                dve.wait_ge(step, 17)
                v.scalar_tensor_tensor(out=low[:], in0=pick1[:], scalar=-1e30, in1=logits[:],
                                       op0=ALU.mult, op1=ALU.add).then_inc(step, 1)
                dve.wait_ge(step, 18)
                v.tensor_reduce(top2[:], low[:], AX.X, ALU.max).then_inc(step, 1)
                dve.wait_ge(step, 19)
                v.tensor_tensor(pick2[:], low[:], over_e(top2), ALU.is_equal).then_inc(step, 1)
                dve.wait_ge(step, 20)
                v.scalar_tensor_tensor(out=key[:], in0=pick2[:], scalar=-FIRST, in1=over_b(number),
                                       op0=ALU.mult, op1=ALU.add).then_inc(step, 1)
                dve.wait_ge(step, 21)
                v.tensor_reduce(first[:], key[:], AX.X, ALU.min).then_inc(step, 1)
                dve.wait_ge(step, 22)
                v.tensor_tensor(pick2[:], key[:], over_e(first), ALU.is_equal).then_inc(step, 1)
                dve.wait_ge(step, 23)
                v.tensor_tensor(pick1[:], pick1[:], pick2[:], ALU.add).then_inc(step, 1)
                dve.wait_ge(step, 24)
                v.tensor_tensor(pick1[:], pick1[:], over_e(idle), ALU.mult).then_inc(step, 1)
                dve.wait_ge(act_step, 5)
                v.tensor_tensor(e_all[:], e_all[:], is_on[:], ALU.mult).then_inc(step, 1)
                dve.wait_ge(step, 26)
                v.tensor_tensor(e_all[:], e_all[:], pick1[:], ALU.add).then_inc(step, 1)
                dve.wait_ge(step, 27)
                v.tensor_reduce(total[:], e_all[:], AX.X, ALU.add).then_inc(step, 1)
                dve.wait_ge(step, 28)
                v.reciprocal(total[:], total[:]).then_inc(step, 1)
                dve.wait_ge(step, 29)
                v.tensor_tensor(e_all[:], e_all[:], over_e(total), ALU.mult).then_inc(step, 1)


SHIFTED, LAST = 11, 30


def expert_attention(core, w_qkv, w_o, weights_dram):
    nc = core.nc
    EX, H = 16, 128
    SCALE = float(H) ** -0.5
    xt, ident, bank = core.xt, core.ident, core.bank
    acc = bank[0:4]
    with ExitStack() as ctx:
        def sb(name, shape, dt=F32):
            return core.sb(ctx, "c_" + name, shape, dt)

        def sem(name):
            return core.sem(ctx, "c_" + name)

        w_slot = [sb(f"w_qkv{p}", [128, 3, CT, H]) for p in range(2)]
        wo_slot = [sb(f"w_o{p}", [128, C]) for p in range(2)]
        mix = [sb(f"mix{p}", [128, N]) for p in range(2)]
        xw = [sb(f"xw{p}", [128, CT, N]) for p in range(2)]
        aw = [sb(f"aw{p}", [128, N]) for p in range(2)]
        qkv_t = sb("qkv_t", [128, 3, N])
        v = sb("v", [128, B, H])
        masked, probs, probs_t = (sb(n, [128, B, S]) for n in ("masked", "probs", "probs_t"))
        ao_t = sb("ao_t", [128, N])
        top, neg_top, total, inv = (sb(n, [128, B]) for n in ("top", "neg_top", "total", "inv"))
        w_in, mix_in, wo_in, mix2_in = ([sem(f"{n}{p}") for p in range(2)] for n in ("w_in", "mix_in", "wo_in", "mix2_in"))
        xw_ready, mixed, aw_ready, added, closed = (sem(n) for n in ("xw_ready", "mixed", "aw_ready", "added", "closed"))
        kept_act, kept_dve, v_turned, v_kept, s_made, t_made, z_made = (
            sem(n) for n in ("kept_act", "kept_dve", "v_turned", "v_kept", "s_made", "t_made", "z_made"))
        mask_done, top_ready, neg_ready, exp_done, inv_ready, p_ready, z_kept = (
            sem(n) for n in ("mask_done", "top_ready", "neg_ready", "exp_done", "inv_ready", "p_ready", "z_kept"))
        t_kept = sem("t_kept")

        def loads(e, p):
            return 8 * (e - p) + 16

        def cols(half):
            return slice(half * BANK, (half + 1) * BANK)

        def rows(t, half):
            return t[:, half * PER_BANK:(half + 1) * PER_BANK]

        def flat(t, half):
            return rows(t, half).rearrange("p b e -> p (b e)")

        with nc.Block() as block:

            @block.sync
            def _(sp):
                def row(e):
                    return weights_dram[bass.ds(e, 1), :].broadcast_to([128, N])

                def load(e, p):
                    sp.dma_start(mix[p][:], row(e)).then_inc(mix_in[p], 16)
                    sp.dma_start(w_slot[p][:], w_qkv[bass.ds(e, 1)].rearrange("o p (k t e) -> (o p) k t e", k=3, t=CT)
                                 ).then_inc(w_in[p], 16)

                def load_out(e, p):
                    sp.dma_start(aw[p][:], row(e)).then_inc(mix2_in[p], 16)
                    sp.dma_start(wo_slot[p][:], w_o[bass.ds(e, 1)].rearrange("o p c -> (o p) c")).then_inc(wo_in[p], 16)

                for e in range(2):
                    load(e, e)
                with sp.Fori(0, EX // 2 - 1) as i:
                    for p in range(2):
                        sp.wait_ge(mixed, 2 * i + p + 1)
                        load(2 * i + p + 2, p)
                for e in range(2):
                    load_out(e, e)
                with sp.Fori(0, EX // 2 - 1) as i:
                    for p in range(2):
                        sp.wait_ge(added, 2 * i + p + 1)
                        load_out(2 * i + p + 2, p)

            @block.tensor
            def _(pe):
                def clear(banks):
                    for a in banks:
                        nc.tensor.matmul(a[:], core.zero_bf[:, 0:128], core.zero_bf[:], start=True, stop=True,
                                         skip_group_check=True)

                clear(bank[0:6])
                with pe.Fori(0, EX // 2) as i:
                    for p in range(2):
                        e = 2 * i + p
                        pe.wait_ge(w_in[p], loads(e, p))
                        for ct in range(CT):
                            pe.wait_ge(xw_ready, 2 * e + (ct + 1))
                            for kind in range(3):
                                for half in range(HALVES):
                                    mm = nc.tensor.matmul(bank[2 * kind + half][:], w_slot[p][:, kind, ct, :],
                                                          xw[p][:, ct, cols(half)], start=False, stop=True,
                                                          skip_group_check=True)
                        mm.then_inc(mixed, 1)
                pe.wait_ge(kept_act, 3)
                pe.wait_ge(kept_dve, 3)
                for half in range(HALVES):
                    for k in range(PER_BANK):
                        b = half * PER_BANK + k
                        mm = nc.tensor.matmul(bank[half][:, k * S:(k + 1) * S], qkv_t[:, 0, b * S:(b + 1) * S],
                                              qkv_t[:, 1, b * S:(b + 1) * S], start=True, stop=True)
                    mm.then_inc(s_made, 1)
                for half in range(HALVES):
                    for k in range(PER_BANK):
                        b = half * PER_BANK + k
                        mm = nc.tensor.transpose(bank[2 + half][:, k * S:(k + 1) * S], qkv_t[:, 2, b * S:(b + 1) * S],
                                                 ident[:])
                    mm.then_inc(v_turned, 1)
                for half in range(HALVES):
                    pe.wait_ge(p_ready, half + 1)
                    for k in range(PER_BANK):
                        mm = nc.tensor.transpose(bank[4 + half][:, k * S:(k + 1) * S], probs[:, half * PER_BANK + k, :],
                                                 ident[:])
                    mm.then_inc(t_made, 1)
                pe.wait_ge(v_kept, 2)
                for half in range(HALVES):
                    pe.wait_ge(t_kept, half + 1)
                    for k in range(PER_BANK):
                        b = half * PER_BANK + k
                        mm = nc.tensor.matmul(bank[6 + half][:, k * S:(k + 1) * S], v[:, b, :], probs_t[:, b, :],
                                              start=True, stop=True)
                    mm.then_inc(z_made, 1)
                pe.wait_ge(mask_done, 2)
                clear(acc)
                with pe.Fori(0, EX // 2) as i:
                    for p in range(2):
                        e = 2 * i + p
                        pe.wait_ge(wo_in[p], loads(e, p))
                        pe.wait_ge(aw_ready, e + 1)
                        for b in range(B):
                            mm = nc.tensor.matmul(acc[b // 2][:, (b % 2) * C:(b % 2 + 1) * C],
                                                  aw[p][:, b * S:(b + 1) * S], wo_slot[p][:],
                                                  start=False, stop=True, skip_group_check=True)
                        mm.then_inc(added, 1)

            @block.scalar
            def _(act):
                act.wait_ge(mixed, EX)
                for kind in range(3):
                    nc.scalar.copy(qkv_t[:, kind, cols(0)], bank[2 * kind][:]).then_inc(kept_act, 1)
                for half in range(HALVES):
                    act.wait_ge(v_turned, half + 1)
                    nc.scalar.copy(flat(v, half), bank[2 + half][:]).then_inc(v_kept, 1)
                for half in range(HALVES):
                    act.wait_ge(neg_ready, half + 1)
                    for b in range(half * PER_BANK, (half + 1) * PER_BANK):
                        ex = nc.scalar.activation(probs[:, b, :], masked[:, b, :], ACT.Exp, bias=neg_top[:, b:b + 1],
                                                  scale=SCALE, accum_out=total[:, b:b + 1])
                    ex.then_inc(exp_done, 1)
                for half in range(HALVES):
                    act.wait_ge(t_made, half + 1)
                    nc.scalar.copy(flat(probs_t, half), bank[4 + half][:]).then_inc(t_kept, 1)

            @block.vector
            def _(dve):
                with dve.Fori(0, EX // 2) as i:
                    for p in range(2):
                        e = 2 * i + p
                        dve.wait_ge(mix_in[p], loads(e, p))
                        for ct in range(CT):
                            nc.vector.tensor_tensor(xw[p][:, ct, :], xt[:, ct, :], mix[p][:], ALU.mult).then_inc(xw_ready, 1)
                dve.wait_ge(mixed, EX)
                for kind in range(3):
                    nc.vector.tensor_copy(qkv_t[:, kind, cols(1)], bank[2 * kind + 1][:]).then_inc(kept_dve, 1)
                for half in range(HALVES):
                    dve.wait_ge(s_made, half + 1)
                    nc.vector.tensor_tensor(rows(masked, half), bank[half][:].rearrange("p (b k) -> p b k", b=PER_BANK),
                                            core.causal[:].unsqueeze(1).broadcast_to([128, PER_BANK, S]),
                                            ALU.min).then_inc(mask_done, 1)
                    dve.wait_ge(mask_done, half + 1)
                    nc.vector.tensor_reduce(rows(top, half), rows(masked, half), AX.X, ALU.max).then_inc(top_ready, 1)
                    dve.wait_ge(top_ready, half + 1)
                    nc.vector.tensor_scalar(rows(neg_top, half), rows(top, half), -SCALE, None,
                                            ALU.mult).then_inc(neg_ready, 1)
                for half in range(HALVES):
                    dve.wait_ge(exp_done, half + 1)
                    nc.vector.reciprocal(rows(inv, half), rows(total, half)).then_inc(inv_ready, 1)
                    dve.wait_ge(inv_ready, half + 1)
                    nc.vector.tensor_tensor(rows(probs, half), rows(probs, half),
                                            rows(inv, half).unsqueeze(2).broadcast_to([128, PER_BANK, S]),
                                            ALU.mult).then_inc(p_ready, 1)
                for half in range(HALVES):
                    dve.wait_ge(z_made, half + 1)
                    nc.vector.tensor_copy(ao_t[:, cols(half)], bank[6 + half][:]).then_inc(z_kept, 1)
                dve.wait_ge(z_kept, 2)
                with dve.Fori(0, EX // 2) as i:
                    for p in range(2):
                        e = 2 * i + p
                        dve.wait_ge(mix2_in[p], loads(e, p))
                        nc.vector.tensor_tensor(aw[p][:], ao_t[:], aw[p][:], ALU.mult).then_inc(aw_ready, 1)
                dve.wait_ge(added, EX)
                for i, a in enumerate(acc):
                    nc.vector.tensor_tensor(core.y[:, 2 * i:2 * i + 2, :], core.x[:, 2 * i:2 * i + 2, :],
                                            a[:].rearrange("p (b c) -> p b c", b=2), ALU.add).then_inc(closed, 1)


def causal_heads(core, w_qkvo):
    nc = core.nc
    HEADS, E = 16, 128
    SCALE = float(E) ** -0.5
    xt, ident, bank = core.xt, core.ident, core.bank
    acc = bank[0:4]
    with ExitStack() as ctx:
        def sb(name, shape, dt=F32):
            return core.sb(ctx, "d_" + name, shape, dt)

        def sem(name):
            return core.sem(ctx, "d_" + name)

        w_slot = [sb(f"w_qkv{p}", [128, 3, CT, E]) for p in range(2)]
        wo_slot = [sb(f"w_o{p}", [128, C]) for p in range(2)]
        q_t, k_t = sb("q_t", [128, N]), sb("k_t", [128, N])
        v = sb("v", [128, B, E])
        masked = sb("masked", [128, B, S])
        probs = sb("probs", [128, B, S])
        probs_t = sb("probs_t", [128, B, S])
        z_t = sb("z_t", [128, N])
        top, neg_top, total, inv = (sb(n, [128, B]) for n in ("top", "neg_top", "total", "inv"))

        w_in = [sem(f"w_in{p}") for p in range(2)]
        wo_in = [sem(f"wo_in{p}") for p in range(2)]
        q_made, k_made, v_made, s_made, t_made, z_made = (
            sem(n) for n in ("q_made", "k_made", "v_made", "s_made", "t_made", "z_made"))
        q_kept, k_kept, v_kept, exp_done = (sem(n) for n in ("q_kept", "k_kept", "v_kept", "exp_done"))
        mask_done, top_ready, neg_ready, inv_ready, p_ready, z_kept = (
            sem(n) for n in ("mask_done", "top_ready", "neg_ready", "inv_ready", "p_ready", "z_kept"))
        t_kept = [sem(f"t_kept{half}") for half in range(HALVES)]
        head_out = sem("head_out")
        closed = sem("closed")

        def at(h, half):
            return 2 * h + (half + 1)

        def loads(h, p):
            return 8 * (h - p) + 16

        def cols(half):
            return slice(half * BANK, (half + 1) * BANK)

        def batches(half):
            return range(half * PER_BANK, (half + 1) * PER_BANK)

        def heads_of(eng, step):
            with eng.Fori(0, HEADS // 2 - 1) as i:
                step(2 * i, 0, True)
                step(2 * i + 1, 1, True)
            step(HEADS - 2, 0, True)
            step(HEADS - 1, 1, False)

        with nc.Block() as block:

            @block.sync
            def _(sp):
                def load_w(h, p):
                    sp.dma_start(w_slot[p][:], w_qkvo[bass.ds(h, 1), :, 0:3 * C]
                                 .rearrange("o p (k t e) -> (o p) k t e", k=3, t=CT)).then_inc(w_in[p], 16)

                def load_wo(h, p):
                    sp.dma_start(wo_slot[p][:], w_qkvo[bass.ds(h, 1), :, 3 * C:4 * C]
                                 .rearrange("o p c -> (o p) c")).then_inc(wo_in[p], 16)

                for h in range(2):
                    load_w(h, h)
                    load_wo(h, h)
                with sp.Fori(0, HEADS // 2 - 1) as i:
                    for p in range(2):
                        h = 2 * i + p
                        sp.wait_ge(v_made, at(h, 1))
                        load_w(h + 2, p)
                        sp.wait_ge(head_out, h + 1)
                        load_wo(h + 2, p)

            @block.tensor
            def _(pe):
                def project(dst, slot, kind, half):
                    for ct in range(CT):
                        mm = nc.tensor.matmul(dst, w_slot[slot][:, kind, ct, :], xt[:, ct, cols(half)],
                                              start=(ct == 0), stop=(ct == CT - 1))
                    return mm

                def values(dst, slot, half):
                    for k, b in enumerate(batches(half)):
                        for ct in range(CT):
                            mm = nc.tensor.matmul(dst[:, k * E:(k + 1) * E], xt[:, ct, b * S:(b + 1) * S],
                                                  w_slot[slot][:, 2, ct, :], start=(ct == 0), stop=(ct == CT - 1))
                    return mm

                for a in acc:
                    nc.tensor.matmul(a[:], core.zero_bf[:, 0:128], core.zero_bf[:], start=True, stop=True,
                                     skip_group_check=True)
                pe.wait_ge(w_in[0], 16)
                project(bank[6][:], 0, 0, 0).then_inc(q_made, 1)
                project(bank[7][:], 0, 0, 1).then_inc(q_made, 1)
                project(bank[4][:], 0, 1, 0).then_inc(k_made, 1)
                project(bank[5][:], 0, 1, 1).then_inc(k_made, 1)
                pe.wait_ge(q_kept, 2)
                values(bank[6], 0, 0).then_inc(v_made, 1)
                values(bank[7], 0, 1).then_inc(v_made, 1)

                def step(h, p, more):
                    nxt = 1 - p
                    pe.wait_ge(k_kept, at(h, 1))
                    for half, dst in ((0, bank[4]), (1, bank[5])):
                        for k, b in enumerate(batches(half)):
                            mm = nc.tensor.matmul(dst[:, k * S:(k + 1) * S], q_t[:, b * S:(b + 1) * S],
                                                  k_t[:, b * S:(b + 1) * S], start=True, stop=True)
                        mm.then_inc(s_made, 1)
                    if more:
                        pe.wait_ge(w_in[nxt], loads(h + 1, nxt))
                        pe.wait_ge(v_kept, at(h, 0))
                        project(bank[6][:], nxt, 0, 0).then_inc(q_made, 1)
                        pe.wait_ge(v_kept, at(h, 1))
                        project(bank[7][:], nxt, 0, 1).then_inc(q_made, 1)
                        pe.wait_ge(mask_done, at(h, 0))
                        project(bank[4][:], nxt, 1, 0).then_inc(k_made, 1)
                    for half, dst in ((0, bank[5]), (1, bank[6])):
                        pe.wait_ge(p_ready, at(h, half))
                        if half == 0:
                            pe.wait_ge(mask_done, at(h, 1))
                        elif more:
                            pe.wait_ge(q_kept, at(h + 1, 0))
                        else:
                            pe.wait_ge(v_kept, at(h, 0))
                        for k, b in enumerate(batches(half)):
                            mm = nc.tensor.transpose(dst[:, k * S:(k + 1) * S], probs[:, b, :], ident[:])
                        mm.then_inc(t_made, 1)
                    if more:
                        pe.wait_ge(q_kept, at(h + 1, 1))
                        project(bank[7][:], nxt, 1, 1).then_inc(k_made, 1)
                        pe.wait_ge(k_kept, at(h + 1, 0))
                    pe.wait_ge(v_kept, at(h, 1))
                    for half, dst in ((0, bank[4]), (1, bank[5])):
                        pe.wait_ge(t_kept[half], h + 1)
                        for k, b in enumerate(batches(half)):
                            mm = nc.tensor.matmul(dst[:, k * S:(k + 1) * S], v[:, b, :], probs_t[:, b, :],
                                                  start=True, stop=True)
                        mm.then_inc(z_made, 1)
                    if more:
                        pe.wait_ge(t_kept[1], h + 1)
                        values(bank[6], nxt, 0).then_inc(v_made, 1)
                        pe.wait_ge(k_kept, at(h + 1, 1))
                        values(bank[7], nxt, 1).then_inc(v_made, 1)
                    pe.wait_ge(wo_in[p], loads(h, p))
                    for half in range(HALVES):
                        pe.wait_ge(z_kept, at(h, half))
                        for b in batches(half):
                            mm = nc.tensor.matmul(acc[b // 2][:, (b % 2) * C:(b % 2 + 1) * C],
                                                  z_t[:, b * S:(b + 1) * S], wo_slot[p][:],
                                                  start=False, stop=True, skip_group_check=True)
                    mm.then_inc(head_out, 1)

                heads_of(pe, step)

            @block.scalar
            def _(act):
                def keep(dst, src, made, kept, value):
                    act.wait_ge(made, value)
                    nc.scalar.copy(dst, src).then_inc(kept, 1)

                def keep_v(half, h):
                    keep(v[:, half * PER_BANK:(half + 1) * PER_BANK, :].rearrange("p b e -> p (b e)"),
                         bank[6 + half][:], v_made, v_kept, at(h, half))

                keep(q_t[:, cols(0)], bank[6][:], q_made, q_kept, 1)
                keep(q_t[:, cols(1)], bank[7][:], q_made, q_kept, 2)
                keep(k_t[:, cols(0)], bank[4][:], k_made, k_kept, 1)
                keep(k_t[:, cols(1)], bank[5][:], k_made, k_kept, 2)
                keep_v(0, 0)
                keep_v(1, 0)

                def exps(half, h):
                    act.wait_ge(neg_ready, at(h, half))
                    for b in batches(half):
                        ex = nc.scalar.activation(probs[:, b, :], masked[:, b, :], ACT.Exp, bias=neg_top[:, b:b + 1],
                                                  scale=SCALE, accum_out=total[:, b:b + 1])
                    ex.then_inc(exp_done, 1)

                def step(h, p, more):
                    exps(0, h)
                    if more:
                        keep(q_t[:, cols(0)], bank[6][:], q_made, q_kept, at(h + 1, 0))
                    exps(1, h)
                    if more:
                        keep(q_t[:, cols(1)], bank[7][:], q_made, q_kept, at(h + 1, 1))
                        keep(k_t[:, cols(0)], bank[4][:], k_made, k_kept, at(h + 1, 0))
                    act.wait_ge(t_made, at(h, 1))
                    nc.scalar.copy(probs_t[:, PER_BANK:, :].rearrange("p b e -> p (b e)"), bank[6][:]).then_inc(t_kept[1], 1)
                    if more:
                        keep(k_t[:, cols(1)], bank[7][:], k_made, k_kept, at(h + 1, 1))
                        keep_v(0, h + 1)
                        keep_v(1, h + 1)

                heads_of(act, step)

            @block.vector
            def _(dve):
                def rows(t, half):
                    return t[:, half * PER_BANK:(half + 1) * PER_BANK]

                def step(h, p, more):
                    for half in range(HALVES):
                        dve.wait_ge(s_made, at(h, half))
                        nc.vector.tensor_tensor(rows(masked, half), bank[4 + half][:].rearrange("p (b k) -> p b k", b=PER_BANK),
                                                core.causal[:].unsqueeze(1).broadcast_to([128, PER_BANK, S]),
                                                ALU.min).then_inc(mask_done, 1)
                        dve.wait_ge(mask_done, at(h, half))
                        nc.vector.tensor_reduce(rows(top, half), rows(masked, half), AX.X, ALU.max).then_inc(top_ready, 1)
                        dve.wait_ge(top_ready, at(h, half))
                        nc.vector.tensor_scalar(rows(neg_top, half), rows(top, half), -SCALE, None,
                                                ALU.mult).then_inc(neg_ready, 1)
                    for half in range(HALVES):
                        dve.wait_ge(exp_done, at(h, half))
                        nc.vector.reciprocal(rows(inv, half), rows(total, half)).then_inc(inv_ready, 1)
                        dve.wait_ge(inv_ready, at(h, half))
                        nc.vector.tensor_tensor(rows(probs, half), rows(probs, half),
                                                rows(inv, half).unsqueeze(2).broadcast_to([128, PER_BANK, S]),
                                                ALU.mult).then_inc(p_ready, 1)
                    dve.wait_ge(t_made, at(h, 0))
                    nc.vector.tensor_copy(rows(probs_t, 0).rearrange("p b e -> p (b e)"), bank[5][:]).then_inc(t_kept[0], 1)
                    for half in range(HALVES):
                        dve.wait_ge(z_made, at(h, half))
                        nc.vector.tensor_copy(z_t[:, cols(half)], bank[4 + half][:]).then_inc(z_kept, 1)

                heads_of(dve, step)
                dve.wait_ge(head_out, HEADS)
                for i, a in enumerate(acc):
                    nc.vector.tensor_tensor(core.y[:, 2 * i:2 * i + 2, :], core.x[:, 2 * i:2 * i + 2, :],
                                            a[:].rearrange("p (b c) -> p b c", b=2), ALU.add).then_inc(closed, 1)


def quantized_cross_attention(core, ctx_t_dram, wq_dram, bq_dram, wkv_dram, bkv_dram, wp_dram, bp_dram):
    nc = core.nc
    HEADS, D = 16, 16
    PARTS = 3
    HW = 64
    PAIRS = HEADS // 2
    LN255 = 5.541263545158426
    SCALE = 0.25
    UNITS = 2 * B
    psum, bank, xt, ident = core.psum, core.bank, core.xt, core.ident
    with ExitStack() as ctx:
        def sb(name, shape, dt=F32):
            return core.sb(ctx, "e_" + name, shape, dt)

        def sem(name):
            return core.sem(ctx, "e_" + name)

        ctx_t = sb("ctx_t", [128, CT, N])
        wq, wkv, wp = sb("wq", [128, CT, C]), sb("wkv", [128, CT, 2 * C]), sb("wp", [128, CT, C])
        bq, bkv, bp = sb("bq", [128, C]), sb("bkv", [128, 2 * C]), sb("bp", [128, C])
        q, k, v = (sb(n, [128, B, C]) for n in ("q", "k", "v"))
        work = sb("work", [128, B, C])
        q_int = sb("q_int", [128, B, HEADS, HW], BF16)
        k_part = sb("k_part", [128, B, HEADS, HW], BF16)
        v_int = sb("v_int", [128, B, C], BF16)
        q_top, q_scale, q_inv = (sb(n, [128, B * HEADS]) for n in ("q_top", "q_scale", "q_inv"))
        q_neg = sb("q_neg", [128, B * HEADS])
        k_top, k_scale, k_inv = (sb(n, [128, B * HEADS]) for n in ("k_top", "k_scale", "k_inv"))
        v_top, v_all, v_scale, v_inv = (sb(n, [128, C]) for n in ("v_top", "v_all", "v_scale", "v_inv"))
        q_t, k_t = sb("q_t", [128, N], BF16), sb("k_t", [128, N], BF16)
        e = [sb(f"e{i}", [128, N]) for i in range(2)]
        e_big = [sb(f"e_big{i}", [128, N], BF16) for i in range(2)]
        e_t = [sb(f"e_t{i}", [128, B, 128], BF16) for i in range(2)]
        top, bias = ([sb(f"{n}{i}", [128, 1]) for i in range(2)] for n in ("top", "bias"))
        total, inv = sb("total", [128, B * HEADS]), sb("inv", [128, B * HEADS])
        att = sb("att", [128, B, C])
        att_t = sb("att_t", [128, CT, N])

        w_in, pads_ready, step, q_made, k_made, kv_read, v_top_ready, v_all_ready = (
            sem(n) for n in ("w_in", "pads_ready", "step", "q_made", "kv_made", "kv_read", "v_top_ready", "v_all_ready"))
        added = sem("added")
        qt_made, kt_made, qt_kept, kt_kept = (sem(n) for n in ("qt_made", "kt_made", "qt_kept", "kt_kept"))
        s_made, top_ready, bias_ready, exp_done, round_ready, t_made, t_kept, inv_ready, pv_made, pv_kept = (
            sem(n) for n in ("s_made", "top_ready", "bias_ready", "exp_done", "round_ready", "t_made", "t_kept",
                             "inv_ready", "pv_made", "pv_kept"))
        att_ready, att_turned, att_kept_a, att_kept_d, out_made, y_part, closed = (
            sem(n) for n in ("att_ready", "att_turned", "att_kept_a", "att_kept_d", "out_made", "y_part", "closed"))

        def groups(t):
            return t[:].rearrange("p b (h d) -> p (b h) d", d=D)

        def over_d(t):
            return t[:].unsqueeze(2).broadcast_to([128, B * HEADS, D])

        def part(t, j):
            return t[:].rearrange("p b h w -> p (b h) w")[:, :, j * D:(j + 1) * D]

        with nc.Block() as block:

            @block.sync
            def _(sp):
                for dst, src in ((ctx_t, ctx_t_dram), (wq, wq_dram), (wkv, wkv_dram), (wp, wp_dram)):
                    sp.dma_start(dst[:], src.rearrange("(t p) n -> p t n", p=128)).then_inc(w_in, 16)
                for dst, src, n in ((bq, bq_dram, C), (bkv, bkv_dram, 2 * C), (bp, bp_dram, C)):
                    sp.dma_start(dst[:], src.unsqueeze(0).broadcast_to([128, n])).then_inc(w_in, 16)

            @block.gpsimd
            def _(pool):
                nc.gpsimd.memset(q_int[:], 0.0)
                nc.gpsimd.memset(k_part[:], 0.0).then_inc(pads_ready, 1)
                pool.wait_ge(v_top_ready, 1)
                nc.gpsimd.partition_all_reduce(v_all[:], v_top[:], 128,
                                               bass.bass_isa.ReduceOp.max).then_inc(v_all_ready, 1)

            @block.tensor
            def _(pe):
                pe.wait_ge(w_in, 16 * 7)
                for i in range(4):
                    for j in range(2):
                        b = 2 * i + j
                        for ct in range(CT):
                            mm = nc.tensor.matmul(bank[i][:, j * C:(j + 1) * C], xt[:, ct, b * S:(b + 1) * S],
                                                  wq[:, ct, :], start=(ct == 0), stop=(ct == CT - 1))
                    mm.then_inc(q_made, 1)
                for b in range(B):
                    if b >= 4:
                        pe.wait_ge(kv_read, b - 3)
                    for ct in range(CT):
                        mm = nc.tensor.matmul(bank[4 + b % 4], ctx_t[:, ct, b * S:(b + 1) * S], wkv[:, ct, :],
                                              start=(ct == 0), stop=(ct == CT - 1))
                    mm.then_inc(k_made, 1)

                def turn(src, dst, hp, made):
                    for b in range(B):
                        mm = nc.tensor.transpose(dst[:, b * S:(b + 1) * S],
                                                 src[:, b].rearrange("p h w -> p (h w)")[:, bass.ds(hp * 2 * HW, 2 * HW)],
                                                 core.ident_bf[:])
                    mm.then_inc(made, 1)

                def turn_pair(hp):
                    turn(q_int, core.bank_bf(7), hp, qt_made)
                    pe.wait_ge(qt_kept, hp + 1)
                    turn(k_part, core.bank_bf(7), hp, kt_made)

                def scores(hp, u, first=False):
                    p, j = u // B, u % B
                    if u == 0:
                        pe.wait_ge(kt_kept, hp + 1)
                    if not first:
                        pe.wait_ge(exp_done, UNITS * hp + u - 1)
                    for half in range(HALVES):
                        mm = nc.tensor.matmul(bank[2 * (u % 2) + half], q_t[HW * p:HW * p + PARTS * D, j * S:(j + 1) * S],
                                              k_t[HW * p:HW * p + PARTS * D, half * BANK:(half + 1) * BANK],
                                              start=True, stop=True)
                    mm.then_inc(s_made, 1)

                def turn_probs(hp, u, first=False):
                    pe.wait_ge(round_ready, UNITS * hp + (u + 1))
                    if not first:
                        pe.wait_ge(t_kept, UNITS * hp + u - 1)
                    for m in range(B):
                        mm = nc.tensor.transpose(core.bank_bf(4 + u % 2)[:, m * 128:(m + 1) * 128],
                                                 e_big[u % 2][:, m * 128:(m + 1) * 128], core.ident_bf[:])
                    mm.then_inc(t_made, 1)

                def mix(hp, u, first=False):
                    p, j = u // B, u % B
                    pe.wait_ge(t_kept, UNITS * hp + (u + 1))
                    if j == 0 and not (first and p == 0):
                        pe.wait_ge(pv_kept, 2 * hp + p)
                    for m in range(B):
                        mm = nc.tensor.matmul(bank[6][:, j * D:(j + 1) * D], e_t[u % 2][:, m, :],
                                              v_int[:, m, bass.ds(hp * 2 * D + p * D, D)], start=(m == 0), stop=(m == B - 1))
                    if j == B - 1:
                        mm.then_inc(pv_made, 1)

                def pair(hp, first, more):
                    for u in range(UNITS):
                        if u + 2 < UNITS:
                            scores(hp, u + 2)
                        elif more:
                            if u + 2 == UNITS:
                                turn_pair(hp + 1)
                            scores(hp + 1, u + 2 - UNITS)
                        turn_probs(hp, u, first and u < 2)
                        if u > 0:
                            mix(hp, u - 1, first)
                        elif not first:
                            mix(hp - 1, UNITS - 1)

                pe.wait_ge(step, PREP)
                turn_pair(0)
                scores(0, 0, True)
                scores(0, 1, True)
                pair(0, True, True)
                with pe.Fori(1, PAIRS - 1) as hp:
                    pair(hp, False, True)
                pair(PAIRS - 1, False, False)
                mix(PAIRS - 1, UNITS - 1)

                for half in range(HALVES):
                    pe.wait_ge(att_ready, 2)
                    for ct in range(CT):
                        for i in range(PER_BANK):
                            b = half * PER_BANK + i
                            mm = nc.tensor.transpose(bank[CT * half + ct][:, i * S:(i + 1) * S],
                                                     att[:, b, ct * 128:(ct + 1) * 128], ident[:])
                    mm.then_inc(att_turned, 1)
                pe.wait_ge(att_kept_a, HALVES)
                pe.wait_ge(att_kept_d, HALVES)
                for i in range(4):
                    for j in range(2):
                        b = 2 * i + j
                        for ct in range(CT):
                            mm = nc.tensor.matmul(bank[4 + i][:, j * C:(j + 1) * C], att_t[:, ct, b * S:(b + 1) * S],
                                                  wp[:, ct, :], start=(ct == 0), stop=(ct == CT - 1))
                    mm.then_inc(out_made, 1)

            @block.scalar
            def _(act):
                def keep_pair(hp):
                    act.wait_ge(qt_made, hp + 1)
                    nc.scalar.copy(q_t[:], core.bank_bf(7)).then_inc(qt_kept, 1)
                    act.wait_ge(kt_made, hp + 1)
                    nc.scalar.copy(k_t[:], core.bank_bf(7)).then_inc(kt_kept, 1)

                def exps(hp, u):
                    p, j = u // B, u % B
                    act.wait_ge(bias_ready, UNITS * hp + (u + 1))
                    act.wait_ge(w_in, 16)
                    nc.scalar.activation(e[u % 2][:], psum[:, 2 * (u % 2) * BANK:(2 * (u % 2) + 2) * BANK], ACT.Exp,
                                         bias=bias[u % 2][:],
                                         scale=q_scale[:, bass.ds(hp * 2 + (p + j * HEADS), 1)],
                                         accum_out=total[:, bass.ds(hp * 2 + (p + j * HEADS), 1)]).then_inc(exp_done, 1)

                def keep_probs(hp, u):
                    act.wait_ge(t_made, UNITS * hp + (u + 1))
                    nc.scalar.copy(e_t[u % 2][:].rearrange("p m n -> p (m n)"), core.bank_bf(4 + u % 2)).then_inc(t_kept, 1)

                def pair(hp, more):
                    for u in range(UNITS):
                        if u + 1 < UNITS:
                            exps(hp, u + 1)
                        elif more:
                            exps(hp + 1, 0)
                        if u == UNITS - 2 and more:
                            keep_pair(hp + 1)
                        keep_probs(hp, u)

                keep_pair(0)
                exps(0, 0)
                with act.Fori(0, PAIRS - 1) as hp:
                    pair(hp, True)
                pair(PAIRS - 1, False)
                for half in range(HALVES):
                    act.wait_ge(att_turned, half + 1)
                    nc.scalar.copy(att_t[:, 0, half * BANK:(half + 1) * BANK], bank[CT * half]).then_inc(att_kept_a, 1)

            @block.vector
            def _(dve):
                vec = nc.vector
                n = [0]

                def done(ins):
                    ins.then_inc(step, 1)
                    n[0] += 1
                    dve.wait_ge(step, n[0])

                dve.wait_ge(w_in, 16 * 7)
                dve.wait_ge(pads_ready, 1)
                for i in range(4):
                    dve.wait_ge(q_made, i + 1)
                    ins = vec.tensor_tensor(q[:, 2 * i:2 * i + 2, :], bank[i].rearrange("p (j c) -> p j c", j=2),
                                            bq[:].unsqueeze(1).broadcast_to([128, 2, C]), ALU.add)
                done(ins)
                for b in range(B):
                    dve.wait_ge(k_made, b + 1)
                    vec.tensor_tensor(k[:, b, :], bank[4 + b % 4][:, 0:C], bkv[:, 0:C], ALU.add)
                    ins = vec.tensor_tensor(v[:, b, :], bank[4 + b % 4][:, C:2 * C], bkv[:, C:2 * C],
                                            ALU.add)
                    ins.then_inc(kv_read, 1)
                dve.wait_ge(kv_read, B)
                vec.tensor_reduce(v_top[:], v[:].rearrange("p b c -> p c b"), AX.X, ALU.max,
                                  apply_absolute_value=True).then_inc(v_top_ready, 1)

                def scales(top_, scale, inverse, factor):
                    done(vec.tensor_scalar(scale[:], top_[:], factor / 127.0, 1e-8, ALU.mult, ALU.max))
                    done(vec.reciprocal(inverse[:], scale[:]))
                    if factor != 1.0:
                        done(vec.tensor_scalar(inverse[:], inverse[:], factor, None, ALU.mult))

                done(vec.tensor_reduce(q_top[:], groups(q), AX.X, ALU.max, apply_absolute_value=True))
                scales(q_top, q_scale, q_inv, SCALE)
                done(vec.tensor_scalar(q_neg[:], q_scale[:], -1.0, None, ALU.mult))
                done(vec.tensor_tensor(groups(work), groups(q), over_d(q_inv), ALU.mult))
                done(vec.tensor_scalar(work[:], work[:], ROUND, -ROUND, ALU.add, ALU.add))
                done(vec.tensor_scalar(work[:], work[:], 127.0, -127.0, ALU.min, ALU.max))
                for j in range(PARTS):
                    ins = vec.tensor_copy(part(q_int, j), groups(work))
                done(ins)
                done(vec.tensor_reduce(k_top[:], groups(k), AX.X, ALU.max, apply_absolute_value=True))
                scales(k_top, k_scale, k_inv, 1.0)
                done(vec.tensor_tensor(groups(work), groups(k), over_d(k_inv), ALU.mult))
                done(vec.tensor_scalar(work[:], work[:], ROUND, -ROUND, ALU.add, ALU.add))
                done(vec.tensor_scalar(work[:], work[:], 127.0, -127.0, ALU.min, ALU.max))
                done(vec.tensor_tensor(groups(work), groups(work), over_d(k_scale), ALU.mult))
                for j in range(PARTS):
                    done(vec.tensor_copy(part(k_part, j), groups(work)))
                    if j < PARTS - 1:
                        done(vec.tensor_tensor(groups(work), groups(work), part(k_part, j), ALU.subtract))
                dve.wait_ge(v_all_ready, 1)
                scales(v_all, v_scale, v_inv, 1.0)
                done(vec.tensor_tensor(work[:], v[:], v_inv[:].unsqueeze(1).broadcast_to([128, B, C]), ALU.mult))
                done(vec.tensor_scalar(work[:], work[:], ROUND, -ROUND, ALU.add, ALU.add))
                done(vec.tensor_scalar(v_int[:], work[:], 127.0, -127.0, ALU.min, ALU.max))
                assert n[0] == PREP, n[0]

                def maxima(hp, u):
                    p, j = u // B, u % B
                    dve.wait_ge(s_made, UNITS * hp + (u + 1))
                    vec.tensor_reduce(top[u % 2][:], psum[:, 2 * (u % 2) * BANK:(2 * (u % 2) + 2) * BANK], AX.X,
                                      ALU.max).then_inc(top_ready, 1)
                    dve.wait_ge(top_ready, UNITS * hp + (u + 1))
                    vec.tensor_scalar(bias[u % 2][:], top[u % 2][:], q_neg[:, bass.ds(hp * 2 + (p + j * HEADS), 1)],
                                      LN255, ALU.mult, ALU.add).then_inc(bias_ready, 1)

                def rounds(hp, u):
                    dve.wait_ge(exp_done, UNITS * hp + (u + 1))
                    vec.tensor_scalar(e_big[u % 2][:], e[u % 2][:], ROUND, -ROUND, ALU.add, ALU.add).then_inc(round_ready, 1)

                def keep_mix(hp, p):
                    dve.wait_ge(pv_made, 2 * hp + (p + 1))
                    vec.tensor_copy(att[:, :, bass.ds(hp * 2 * D + p * D, D)],
                                    bank[6][:, 0:B * D].rearrange("p (j d) -> p j d", j=B)).then_inc(pv_kept, 1)

                def pair(hp, first, more):
                    for u in range(UNITS):
                        rounds(hp, u)
                        if u + 2 < UNITS:
                            maxima(hp, u + 2)
                        elif more:
                            maxima(hp + 1, u + 2 - UNITS)
                        if u == B + 1:
                            keep_mix(hp, 0)
                        if u == 1 and not first:
                            keep_mix(hp - 1, 1)

                maxima(0, 0)
                maxima(0, 1)
                pair(0, True, True)
                with dve.Fori(1, PAIRS - 1) as hp:
                    pair(hp, False, True)
                pair(PAIRS - 1, False, False)
                keep_mix(PAIRS - 1, 1)
                vec.reciprocal(inv[:], total[:]).then_inc(inv_ready, 1)
                dve.wait_ge(inv_ready, 1)
                dve.wait_ge(pv_kept, 2 * PAIRS)
                vec.tensor_tensor(groups(att), groups(att), over_d(inv), ALU.mult).then_inc(att_ready, 1)
                dve.wait_ge(att_ready, 1)
                vec.tensor_tensor(att[:], att[:], v_scale[:].unsqueeze(1).broadcast_to([128, B, C]),
                                  ALU.mult).then_inc(att_ready, 1)
                for half in range(HALVES):
                    dve.wait_ge(att_turned, half + 1)
                    vec.tensor_copy(att_t[:, 1, half * BANK:(half + 1) * BANK], bank[CT * half + 1]).then_inc(att_kept_d, 1)
                vec.tensor_tensor(work[:], core.x[:], bp[:].unsqueeze(1).broadcast_to([128, B, C]), ALU.add).then_inc(y_part, 1)
                dve.wait_ge(y_part, 1)
                for i in range(4):
                    dve.wait_ge(out_made, i + 1)
                    vec.tensor_tensor(core.y[:, 2 * i:2 * i + 2, :], work[:, 2 * i:2 * i + 2, :],
                                      bank[4 + i].rearrange("p (j c) -> p j c", j=2), ALU.add).then_inc(closed, 1)


PREP = 27


def ternary_ffn(core, w_gate_up, w_down, norm_weight):
    nc = core.nc
    F, FP = 704, 88
    FT = F // FP
    psum, bank = core.psum, core.bank
    with ExitStack() as ctx:
        def sb(name, shape, dt=F32):
            return core.sb(ctx, "f_" + name, shape, dt)

        def sem(name):
            return core.sem(ctx, "f_" + name)

        wgu, wgu_q = sb("wgu", [128, CT * 2 * F]), sb("wgu_q", [128, CT * 2 * F], BF16)
        wd, wd_q = sb("wd", [FP, FT * C]), sb("wd_q", [FP, FT * C], BF16)
        wgu_qv = wgu_q[:].rearrange("p (t f) -> p t f", t=CT)
        wd_qv = wd_q[:].rearrange("p (t c) -> p t c", t=FT)
        nw = sb("nw", [128, C])
        w_sum, w_mean, w_scale = sb("w_sum", [128, 2]), sb("w_mean", [128, 2]), sb("w_scale", [128, 2])
        sq, var, rs, t0 = (sb(n, [128, B]) for n in ("sq", "var", "rs", "t0"))
        amax, a_scale, alpha, alpha3 = (sb(n, [128, B]) for n in ("amax", "a_scale", "alpha", "alpha3"))
        xn, xr, xq = sb("xn", [128, B, C]), sb("xr", [128, B, C]), sb("xq", [128, B, C], BF16)
        xq_t = sb("xq_t", [128, CT, N], BF16)
        g1, g2, h, hr = (sb(n, [128, F]) for n in ("g1", "g2", "h", "hr"))
        hq = sb("hq", [128, F], BF16)
        hq_t = sb("hq_t", [FP, FT, 128], BF16)
        hm, hc, hi, hs = (sb(n, [128, 1]) for n in ("hm", "hc", "hi", "hs"))
        mean2 = sb("mean2", [128, 1])
        w_in, wd_in, nw_in, sums_ready, sums_made, x_sq_done, x_sd_done = (
            sem(n) for n in ("w_in", "wd_in", "nw_in", "sums_ready", "sums_made", "x_sq_done", "x_sd_done"))
        step, xn_ready, xr_ready, xq_ready, xq_turned, xq_kept, wq_step = (
            sem(n) for n in ("step", "xn_ready", "xr_ready", "xq_ready", "xq_turned", "xq_kept", "wq_step"))
        gu_made, g1_done, g2_done, h_step, hq_ready, hq_turned, hq_kept, down_made, y_ready = (
            sem(n) for n in ("gu_made", "g1_done", "g2_done", "h_step", "hq_ready", "hq_turned", "hq_kept",
                             "down_made", "y_ready"))
        dq_ready, wq_ready = sem("dq_ready"), sem("wq_ready")
        H_STEPS = 6

        with nc.Block() as block:

            @block.sync
            def _(sp):
                sp.dma_start(wgu[:], w_gate_up).then_inc(w_in, 16)
                sp.dma_start(wd[:], w_down).then_inc(wd_in, 16)
                sp.dma_start(nw[:], norm_weight.unsqueeze(0).broadcast_to([128, C])).then_inc(nw_in, 16)

            @block.tensor
            def _(pe):
                pe.wait_ge(sums_ready, 2)
                nc.tensor.matmul(bank[7][:, 0:1], core.ones[:], w_sum[:, 0:1], start=True, stop=True)
                nc.tensor.matmul(bank[7][:, 1:2], core.ones[0:FP, :], w_sum[0:FP, 1:2], start=True,
                                 stop=True).then_inc(sums_made, 1)
                pe.wait_ge(xq_ready, 1)
                for ct in range(CT):
                    for b in range(B):
                        mm = nc.tensor.transpose(core.bank_bf(5 + ct)[:, b * S:(b + 1) * S],
                                                 xq[:, b, ct * 128:(ct + 1) * 128], core.ident_bf[:])
                    mm.then_inc(xq_turned, 1)
                pe.wait_ge(xq_kept, CT)
                pe.wait_ge(wq_ready, 2)
                with pe.Fori(0, B) as b:
                    for part in range(2):
                        for lo, hi_ in ((0, BANK), (BANK, F)):
                            for ct in range(CT):
                                mm = nc.tensor.matmul(psum[:, part * 2 * BANK + lo:part * 2 * BANK + hi_],
                                                      xq_t[:, ct, bass.ds(b * S, S)],
                                                      wgu_qv[:, ct, part * F + lo:part * F + hi_],
                                                      start=(ct == 0), stop=(ct == CT - 1))
                    mm.then_inc(gu_made, 1)
                    pe.wait_ge(hq_ready, b + 1)
                    for t in range(FT):
                        mm = nc.tensor.transpose(core.bank_bf(4)[0:FP, t * 128:(t + 1) * 128],
                                                 hq[:, t * FP:(t + 1) * FP], core.ident_bf[:])
                    mm.then_inc(hq_turned, 1)
                    pe.wait_ge(hq_kept, b + 1)
                    for t in range(FT):
                        mm = nc.tensor.matmul(bank[5][:, 0:C], hq_t[:, t, :], wd_qv[:, t, :],
                                              start=(t == 0), stop=(t == FT - 1))
                    mm.then_inc(down_made, 1)
                    pe.wait_ge(y_ready, b + 1)

            @block.scalar
            def _(act):
                for b in range(B):
                    ins = nc.scalar.activation(core.y[:, b, :], core.x[:, b, :], ACT.Square, accum_out=sq[:, b:b + 1])
                ins.then_inc(x_sq_done, 1)
                act.wait_ge(step, 1)
                nc.scalar.activation(rs[:], var[:], ACT.Sqrt).then_inc(x_sd_done, 1)
                for ct in range(CT):
                    act.wait_ge(xq_turned, ct + 1)
                    nc.scalar.copy(xq_t[:, ct, :], core.bank_bf(5 + ct)).then_inc(xq_kept, 1)
                with act.Fori(0, B) as b:
                    act.wait_ge(gu_made, b + 1)
                    nc.scalar.activation(g1[:], psum[:, 0:F], ACT.Relu).then_inc(g1_done, 1)
                    act.wait_ge(g1_done, b + 1)
                    nc.scalar.activation(g2[:], g1[:], ACT.Square).then_inc(g2_done, 1)
                    act.wait_ge(hq_turned, b + 1)
                    nc.scalar.copy(hq_t[:].rearrange("p t n -> p (t n)"), core.bank_bf(4)[0:FP, :]).then_inc(hq_kept, 1)

            @block.vector
            def _(dve):
                v = nc.vector
                dve.wait_ge(x_sq_done, 1)
                v.tensor_scalar(var[:], sq[:], 1.0 / C, 1e-5, ALU.mult, ALU.add).then_inc(step, 1)
                dve.wait_ge(w_in, 16)
                v.tensor_reduce(w_sum[:, 0:1], wgu[:], AX.X, ALU.add, apply_absolute_value=True).then_inc(sums_ready, 1)
                dve.wait_ge(wd_in, 16)
                v.tensor_reduce(w_sum[0:FP, 1:2], wd[:], AX.X, ALU.add, apply_absolute_value=True).then_inc(sums_ready, 1)
                dve.wait_ge(x_sd_done, 1)
                v.reciprocal(rs[:], rs[:]).then_inc(step, 1)
                dve.wait_ge(step, 2)
                v.tensor_tensor(t0[:], rs[:], rs[:], ALU.mult).then_inc(step, 1)
                dve.wait_ge(step, 3)
                v.tensor_tensor(t0[:], t0[:], var[:], ALU.mult).then_inc(step, 1)
                dve.wait_ge(step, 4)
                v.tensor_scalar(t0[:], t0[:], -0.5, 1.5, ALU.mult, ALU.add).then_inc(step, 1)
                dve.wait_ge(step, 5)
                v.tensor_tensor(rs[:], rs[:], t0[:], ALU.mult).then_inc(step, 1)
                dve.wait_ge(step, 6)
                dve.wait_ge(nw_in, 16)
                for b in range(B):
                    v.scalar_tensor_tensor(out=xn[:, b, :], in0=core.x[:, b, :], scalar=rs[:, b:b + 1], in1=nw[:],
                                           op0=ALU.mult, op1=ALU.mult).then_inc(xn_ready, 1)
                dve.wait_ge(xn_ready, B)
                v.tensor_reduce(amax[:], xn[:], AX.X, ALU.max, apply_absolute_value=True).then_inc(step, 1)
                dve.wait_ge(sums_made, 1)
                v.tensor_scalar(w_mean[:, 0:1], bank[7][:, 0:1], 1.0 / (2 * F * C), 1e-5, ALU.mult,
                                ALU.max).then_inc(wq_step, 1)
                v.tensor_scalar(w_mean[:, 1:2], bank[7][:, 1:2], 1.0 / (F * C), 1e-5, ALU.mult,
                                ALU.max).then_inc(wq_step, 1)
                dve.wait_ge(step, 7)
                v.tensor_scalar(amax[:], amax[:], 1e-5, None, ALU.max).then_inc(step, 1)
                dve.wait_ge(step, 8)
                v.reciprocal(a_scale[:], amax[:]).then_inc(step, 1)
                dve.wait_ge(step, 9)
                v.tensor_scalar(a_scale[:], a_scale[:], 127.0, None, ALU.mult).then_inc(step, 1)
                dve.wait_ge(step, 10)
                for b in range(B):
                    v.tensor_scalar(xr[:, b, :], xn[:, b, :], a_scale[:, b:b + 1], ROUND, ALU.mult,
                                    ALU.add).then_inc(xr_ready, 1)
                dve.wait_ge(xr_ready, B)
                v.tensor_scalar(xq[:], xr[:], -ROUND, None, ALU.add).then_inc(xq_ready, 1)
                dve.wait_ge(wq_step, 2)
                v.reciprocal(w_scale[:], w_mean[:]).then_inc(step, 1)
                v.tensor_scalar(mean2[:], w_mean[:, 1:2], 1.0 / 127.0, None, ALU.mult).then_inc(step, 1)
                v.tensor_scalar(alpha[:], amax[:], w_mean[:, 0:1], 1.0 / 127.0, ALU.mult, ALU.mult).then_inc(step, 1)
                dve.wait_ge(step, 13)
                v.tensor_tensor(alpha3[:], alpha[:], alpha[:], ALU.mult).then_inc(step, 1)
                for k, (w, q, s) in enumerate(((wgu[:], wgu_q[:], w_scale[:, 0:1]), (wd[:], wd_q[:], w_scale[0:FP, 1:2]))):
                    v.tensor_scalar(w, w, s, 1.0, ALU.mult, ALU.min).then_inc(wq_step, 1)
                    dve.wait_ge(wq_step, 2 * k + 3)
                    v.tensor_scalar(w, w, -1.0, ROUND, ALU.max, ALU.add).then_inc(wq_step, 1)
                    dve.wait_ge(wq_step, 2 * k + 4)
                    v.tensor_scalar(q, w, -ROUND, None, ALU.add).then_inc(wq_ready, 1)
                dve.wait_ge(step, 14)
                v.tensor_tensor(alpha3[:], alpha3[:], alpha[:], ALU.mult).then_inc(step, 1)
                dve.wait_ge(step, 15)
                with dve.Fori(0, B) as b:
                    dve.wait_ge(g2_done, b + 1)
                    v.tensor_tensor(h[:], g2[:], psum[:, 2 * BANK:2 * BANK + F], ALU.mult).then_inc(h_step, 1)
                    dve.wait_ge(h_step, H_STEPS * b + 1)
                    v.tensor_reduce(hm[:], h[:], AX.X, ALU.max, apply_absolute_value=True).then_inc(h_step, 1)
                    dve.wait_ge(h_step, H_STEPS * b + 2)
                    v.tensor_scalar(hc[:], hm[:], alpha3[:, bass.ds(b, 1)], 1e-5, ALU.mult, ALU.max).then_inc(h_step, 1)
                    dve.wait_ge(h_step, H_STEPS * b + 3)
                    v.reciprocal(hi[:], hc[:]).then_inc(h_step, 1)
                    dve.wait_ge(h_step, H_STEPS * b + 4)
                    v.tensor_scalar(hs[:], hi[:], 127.0, alpha3[:, bass.ds(b, 1)], ALU.mult, ALU.mult).then_inc(h_step, 1)
                    dve.wait_ge(h_step, H_STEPS * b + 5)
                    v.tensor_scalar(hr[:], h[:], hs[:], ROUND, ALU.mult, ALU.add).then_inc(h_step, 1)
                    dve.wait_ge(h_step, H_STEPS * b + 6)
                    v.tensor_scalar(hq[:], hr[:], -ROUND, None, ALU.add).then_inc(hq_ready, 1)
                    dve.wait_ge(down_made, b + 1)
                    v.tensor_scalar(hi[:], hc[:], mean2[:], None, ALU.mult).then_inc(dq_ready, 1)
                    dve.wait_ge(dq_ready, b + 1)
                    v.scalar_tensor_tensor(out=core.y[:, bass.ds(b, 1), :].rearrange("p o c -> p (o c)"),
                                           in0=bank[5][:, 0:C], scalar=hi[:],
                                           in1=core.x[:, bass.ds(b, 1), :].rearrange("p o c -> p (o c)"),
                                           op0=ALU.mult, op1=ALU.add).then_inc(y_ready, 1)


def decoder(nc, d, out):
    expert_weights = nc.dram_tensor("expert_weights", [16, N], F32).ap()
    with ExitStack() as ctx:
        core = Core(nc, ctx)
        make_constants(core, d["x"])
        norm_and_turn(core, "n0", normalize=False)
        gated_delta(core, d["delta_heads"], d["delta_small"], d["delta_bias"], d["delta_rms"], d["delta_masks"])
        norm_and_turn(core, "n1", turn=False)
        core.end_stage()
        rotary_cross_attention(core, d["ctx"], d["rotary_w"], d["rotary_cols"], d["rotary_bv"], d["rotary_enc"], d["rotary_sign"])
        norm_and_turn(core, "n2")
        core.end_stage()
        route_tokens(core, d["sim"], d["gates"], expert_weights)
        expert_attention(core, d["expert_qkv"], d["expert_o"], expert_weights)
        norm_and_turn(core, "n3")
        core.end_stage()
        causal_heads(core, d["heads_qkvo"])
        norm_and_turn(core, "n4")
        core.end_stage()
        quantized_cross_attention(core, d["ctx_t"], d["xattn_wq"], d["xattn_bq"], d["xattn_wkv"], d["xattn_bkv"],
                                  d["xattn_wp"], d["xattn_bp"])
        norm_and_turn(core, "n5", turn=False)
        core.end_stage()
        ternary_ffn(core, d["ffn_gate_up"], d["ffn_down"], d["ffn_norm"])
        norm_and_turn(core, "n6", turn=False, out_dram=out)


def lay_out_delta(w_qkv, w_gate, w_beta, w_alpha, log_A, dt_bias, conv_w, rms_w, w_out):
    def by_head(w, n):
        return w.reshape(n, 128, 2, 128).transpose(0, 3, 2, 1)

    q, k = by_head(w_qkv[:1024], 8), by_head(w_qkv[1024:2048], 8)
    v = by_head(w_qkv[2048:], 16).reshape(8, 2, 128, 2, 128)
    qkv = np.stack([q, k, v[:, 0], v[:, 1]], axis=2).reshape(8, 128, 1024)
    cq, ck = conv_w[:1024, 0].reshape(8, 128, 4), conv_w[1024:2048, 0].reshape(8, 128, 4)
    cv = conv_w[2048:, 0].reshape(8, 2, 128, 4)
    taps = np.stack([cq, ck, cv[:, 0], cv[:, 1]], axis=2).reshape(8, 128, 16)
    gate = w_gate.reshape(8, 256, 2, 128).transpose(0, 3, 2, 1).reshape(8, 128, 512)
    out = w_out.T.reshape(8, 2, 128, 256).transpose(0, 2, 1, 3).reshape(8, 128, 512)
    small = np.concatenate([w_beta, w_alpha]).T.reshape(2, 128, 32).transpose(1, 0, 2).reshape(128, 64)
    return {"delta_heads": np.concatenate([qkv, taps, gate, out], axis=2), "delta_small": small,
            "delta_bias": np.stack([dt_bias, log_A]), "delta_rms": rms_w[:, None], "delta_masks": delta_masks()}


def lay_out_rotary(encoding, Wq, bq, Wk, bk, Wv, bv, Wm, bm):
    channel = np.arange(128)
    swap = ((channel // 16) ^ 1) * 16 + channel % 16
    by_head = (channel % 8) * 16 + channel // 8
    w = np.stack([Wq.T, Wq[swap].T, Wk.T, Wk[swap].T, Wv[by_head].T, Wm[:, by_head].T], axis=1).reshape(128, 768)
    sign = np.where((channel // 16) % 2 == 0, -1, 1).astype(np.float32)[:, None]
    return {"rotary_w": w, "rotary_cols": np.stack([bq, bq[swap], bk, bk[swap], bm], axis=1),
            "rotary_bv": bv[by_head], "rotary_enc": encoding[:, 0, 0].transpose(0, 2, 1), "rotary_sign": sign}


def lay_out_experts(sim_matrix, gates, q_proj, k_proj, v_proj, o_proj):
    def tiles(w):
        return w.reshape(16, 2, 128, 128).transpose(0, 2, 1, 3).reshape(16, 128, 256)

    return {"sim": sim_matrix, "gates": gates, "expert_o": o_proj,
            "expert_qkv": np.concatenate([tiles(q_proj), tiles(k_proj), tiles(v_proj)], axis=2)}


def lay_out_heads(W_Q, W_K, W_V, W_O):
    def tiles(w):
        return w.transpose(0, 2, 1).reshape(16, 2, 128, 128).transpose(0, 2, 1, 3).reshape(16, 128, 256)

    return {"heads_qkvo": np.concatenate([tiles(W_Q), tiles(W_K), tiles(W_V), W_O.transpose(0, 2, 1)], axis=2)}


def lay_out_ffn(w_gate_up, w_down, norm_weight):
    return {"ffn_gate_up": w_gate_up.T.reshape(2, 128, 1408).transpose(1, 0, 2).reshape(128, 2816),
            "ffn_down": w_down.T.reshape(8, 88, 256).transpose(1, 0, 2).reshape(88, 2048), "ffn_norm": norm_weight}


def lay_out(inputs):
    inputs = {name: np.asarray(a) for name, a in inputs.items()}

    def part(prefix):
        return {name[len(prefix):]: a for name, a in inputs.items() if name.startswith(prefix)}

    laid = {"x": inputs["x"], "ctx": inputs["ctx_2048"], "ctx_t": inputs["ctx_2048"].reshape(N, C).T}
    laid.update(lay_out_delta(**part("L0_attn_")))
    laid.update(lay_out_rotary(**part("L0_xattn_")))
    laid.update(lay_out_experts(**part("L0_ffn_")))
    laid.update(lay_out_heads(**part("L1_attn_")))
    laid.update({"xattn_" + name.lower(): a for name, a in part("L1_xattn_").items()})
    laid.update(lay_out_ffn(**part("L1_ffn_")))
    return {name: np.ascontiguousarray(a) for name, a in laid.items()}


def kernel(**inputs):
    import concourse.bacc as bacc
    from concourse.bass_utils import run_bass_kernel_spmd

    nc = bacc.Bacc("TRN2", target_bir_lowering=False, num_devices=1)
    arrays, d = {}, {}
    for name, a in lay_out(inputs).items():
        arrays[f"in_{name}"] = a
        d[name] = nc.dram_tensor(f"in_{name}", a.shape, mybir.dt.from_np(a.dtype), kind="ExternalInput").ap()
    out = nc.dram_tensor("out_y", (B, S, C), F32, kind="ExternalOutput").ap()
    decoder(nc, d, out)
    r = run_bass_kernel_spmd(nc, [arrays], core_ids=[0])
    return r.results[0]["out_y"]
```

```python
import numpy as np
from contextlib import ExitStack

import concourse.bass as bass
from concourse import mybir

F32 = mybir.dt.float32
BF16 = mybir.dt.bfloat16
ALU = mybir.AluOpType
ACT = mybir.ActivationFunctionType
AX = mybir.AxisListType

B, S, C = 8, 128, 256
N = B * S
CT = C // 128
BANK = 512
PER_BANK = BANK // 128
HALVES = N // BANK
LN_EPS = 1e-5
ROUND = 12582912.0
MASKED = -1e9
ALLOWED = 3e38


class Core:

    def __init__(self, nc, ctx):
        self.nc, self.ctx = nc, ctx
        self.stage_sems = []
        self.x = self.sb(ctx, "x_tok", [128, B, C])
        self.y = self.sb(ctx, "y_tok", [128, B, C])
        self.xt = self.sb(ctx, "x_chan", [128, CT, N])
        self.ident = self.sb(ctx, "ident", [128, 128])
        self.ident_bf = self.sb(ctx, "ident_bf", [128, 128], BF16)
        self.zero_bf = self.sb(ctx, "zero_bf", [128, BANK], BF16)
        self.ones = self.sb(ctx, "ones", [128, 128])
        self.causal = self.sb(ctx, "causal", [128, 128])
        self.stats = self.sb(ctx, "y_stats", [128, B, 6])
        self.psum = ctx.enter_context(nc.psum_tensor("psum", [128, 8 * BANK], F32))
        self.bank = [self.psum[:, i * BANK:(i + 1) * BANK] for i in range(8)]

    def sb(self, ctx, name, shape, dt=F32):
        return ctx.enter_context(self.nc.sbuf_tensor(name, shape, dt))

    def bank_bf(self, i):
        return self.bank[i].bitcast(BF16)

    def sem(self, ctx, name):
        handle = self.nc.alloc_semaphore(name)
        self.stage_sems.append(handle)
        return handle

    def batch_stats(self, b):
        return self.nc.vector.bn_stats(self.stats[:, b, :], self.y[:, b, :])

    def end_stage(self):
        self.nc.clear_and_free_semaphores(self.stage_sems)
        self.nc.all_engine_barrier()
        self.stage_sems = []


def make_constants(core, x_dram):
    nc = core.nc
    with ExitStack() as ctx:
        filled, shaped, x_in = (core.sem(ctx, n) for n in ("const_filled", "const_shaped", "x_in"))
        with nc.Block() as block:

            @block.sync
            def _(sp):
                sp.dma_start(core.x[:], x_dram.rearrange("b s c -> s b c")).then_inc(x_in, 16)
                sp.wait_ge(x_in, 16)

            @block.gpsimd
            def _(pool):
                nc.gpsimd.memset(core.ident[:], 0.0)
                nc.gpsimd.memset(core.ones[:], 1.0)
                nc.gpsimd.memset(core.zero_bf[:], 0.0)
                nc.gpsimd.memset(core.causal[:], ALLOWED).then_inc(filled, 1)
                pool.wait_ge(filled, 1)
                nc.gpsimd.affine_select(out=core.ident[:], in_=core.ident[:], compare_op=ALU.not_equal, fill=1.0,
                                        base=0, pattern=[[-1, 128]], channel_multiplier=1).then_inc(shaped, 1)
                nc.gpsimd.affine_select(out=core.causal[:], in_=core.causal[:], compare_op=ALU.is_ge, fill=MASKED,
                                        base=0, pattern=[[-1, 128]], channel_multiplier=1).then_inc(shaped, 1)
                pool.wait_ge(shaped, 1)
                nc.gpsimd.tensor_copy(core.ident_bf[:], core.ident[:]).then_inc(shaped, 1)


def norm_and_turn(core, tag, normalize=True, turn=True, out_dram=None, loads=None, sums=True):
    nc = core.nc
    with ExitStack() as ctx:
        stats = core.stats
        mv = core.sb(ctx, f"{tag}_mv", [128, B, 2])
        var = core.sb(ctx, f"{tag}_var", [128, B])
        sd = core.sb(ctx, f"{tag}_sd", [128, B])
        rstd = core.sb(ctx, f"{tag}_rstd", [128, B])
        t0 = core.sb(ctx, f"{tag}_t0", [128, B])
        shift = core.sb(ctx, f"{tag}_shift", [128, B])
        stats_ready, mv_ready, var_ready, sd_ready, rstd_steps, x_even, x_odd, turned, stored = (
            core.sem(ctx, f"{tag}_{n}") for n in
            ("stats_ready", "mv_ready", "var_ready", "sd_ready", "rstd_steps", "x_even", "x_odd", "turned", "stored"))
        with nc.Block() as block:

            @block.vector
            def _(dve):
                if normalize:
                    if sums:
                        for b in range(B):
                            core.batch_stats(b).then_inc(stats_ready, 1)
                    for b in range(B):
                        if sums:
                            dve.wait_ge(stats_ready, b + 1)
                        nc.vector.bn_aggr(mv[:, b, :], stats[:, b, :]).then_inc(mv_ready, 1)
                    dve.wait_ge(mv_ready, B)
                    nc.vector.tensor_scalar(var[:], mv[:, :, 1], LN_EPS, None, ALU.add).then_inc(var_ready, 1)
                    dve.wait_ge(sd_ready, 1)
                    nc.vector.reciprocal(rstd[:], sd[:]).then_inc(rstd_steps, 1)
                    dve.wait_ge(rstd_steps, 1)
                    nc.vector.tensor_tensor(t0[:], rstd[:], rstd[:], ALU.mult).then_inc(rstd_steps, 1)
                    dve.wait_ge(rstd_steps, 2)
                    nc.vector.tensor_tensor(t0[:], t0[:], var[:], ALU.mult).then_inc(rstd_steps, 1)
                    dve.wait_ge(rstd_steps, 3)
                    nc.vector.tensor_scalar(t0[:], t0[:], -0.5, 1.5, ALU.mult, ALU.add).then_inc(rstd_steps, 1)
                    dve.wait_ge(rstd_steps, 4)
                    nc.vector.tensor_tensor(rstd[:], rstd[:], t0[:], ALU.mult).then_inc(rstd_steps, 1)
                    dve.wait_ge(rstd_steps, 5)
                    nc.vector.scalar_tensor_tensor(out=shift[:], in0=mv[:, :, 0], scalar=-1.0, in1=rstd[:],
                                                   op0=ALU.mult, op1=ALU.mult).then_inc(rstd_steps, 1)
                    for b in range(0, B, 2):
                        nc.vector.tensor_scalar(core.x[:, b, :], core.y[:, b, :], mv[:, b, 0:1], rstd[:, b:b + 1],
                                                ALU.subtract, ALU.mult).then_inc(x_even, 1)
                if turn:
                    for half in range(HALVES):
                        dve.wait_ge(turned, half + 1)
                        nc.vector.tensor_copy(core.xt[:, 1, half * BANK:(half + 1) * BANK], core.bank[half * CT + 1][:])

            @block.scalar
            def _(act):
                if normalize:
                    act.wait_ge(var_ready, 1)
                    nc.scalar.activation(sd[:], var[:], ACT.Sqrt).then_inc(sd_ready, 1)
                    act.wait_ge(rstd_steps, 6)
                    for b in range(1, B, 2):
                        nc.scalar.activation(core.x[:, b, :], core.y[:, b, :], ACT.Identity, bias=shift[:, b:b + 1],
                                             scale=rstd[:, b:b + 1]).then_inc(x_odd, 1)
                if turn:
                    for half in range(HALVES):
                        act.wait_ge(turned, half + 1)
                        nc.scalar.copy(core.xt[:, 0, half * BANK:(half + 1) * BANK], core.bank[half * CT][:])

            if turn:
                @block.tensor
                def _(pe):
                    for half in range(HALVES):
                        for k in range(PER_BANK):
                            b = half * PER_BANK + k
                            if normalize:
                                pe.wait_ge(x_odd if b % 2 else x_even, b // 2 + 1)
                            for ct in range(CT):
                                mm = nc.tensor.transpose(core.bank[half * CT + ct][:, k * 128:(k + 1) * 128],
                                                         core.x[:, b, ct * 128:(ct + 1) * 128], core.ident[:])
                        mm.then_inc(turned, 1)

            if loads is not None:
                @block.sync
                def _(sp):
                    loads(sp)

            if out_dram is not None:
                @block.sync
                def _(sp):
                    sp.wait_ge(x_even, B // 2)
                    sp.wait_ge(x_odd, B // 2)
                    sp.dma_start(out_dram.rearrange("b s c -> s b c"), core.x[:]).then_inc(stored, 16)
                    sp.wait_ge(stored, 16)


GRAM_HEADS = 8
DELTA_LEVELS = 6


def delta_masks():
    i = np.arange(128)
    up_to = (i[:, None] <= i[None, :])
    after = (i[:, None] > i[None, :])
    first = -((i[None, :] == i[:, None] + 1) & (i[:, None] % 2 == 0)).astype(np.float32)
    parts = [up_to, after, first]
    for level in range(DELTA_LEVELS):
        m = 2 << level
        parts.append(i[:, None] // m == 2 * np.arange(64 // m)[None, :] + 1)
    for level in range(DELTA_LEVELS):
        m = 2 << level
        parts.append(-(i[:, None] // m % 2 == 0).astype(np.float32))
    return np.concatenate([p.astype(np.float32) for p in parts], axis=1)


def gated_delta(core, w_dram, w_small_dram, bias_dram, rms_dram, masks_dram, enter):
    nc = core.nc
    G, V, K, TAPS = GRAM_HEADS, 2, 4, 4
    EPS = 1e-6
    LV = DELTA_LEVELS
    PAD = TAPS - 1
    WQKV, WTAP, WGATE = K * CT * 128, K * TAPS, CT * V * 128
    xt, ident, bank, psum = core.xt, core.ident, core.bank, core.psum
    LOG_TERMS = (1 / 15, 1 / 13, 1 / 11, 1 / 9, 1 / 7, 1 / 5, 1 / 3)
    with ExitStack() as ctx:
        def sb(name, shape, dt=F32):
            return core.sb(ctx, "a_" + name, shape, dt)

        def sem(name):
            return core.sem(ctx, "a_" + name)

        masks = sb("masks", [128, masks_dram.shape[1]])
        up_to, after, first_pairs = (masks[:, i * 128:(i + 1) * 128] for i in range(3))
        odd_rows, even_rows, at_col = [], [], 3 * 128
        for level in range(LV):
            odd_rows.append(masks[:, at_col:at_col + (32 >> level)])
            at_col += 32 >> level
        for level in range(LV):
            even_rows.append(masks[:, at_col + level:at_col + level + 1])

        w_qkv, taps = sb("w_qkv", [128, K, CT, 128]), sb("taps", [128, K, TAPS])
        w_gate, w_out = sb("w_gate", [128, CT, V * 128]), sb("w_out", [128, V, C])
        w_small, bias, rms_col = sb("w_small", [128, CT, 32]), sb("bias", [128, 2, 16]), sb("rms_col", [128, 1])
        beta, la = sb("beta", [128, V * G, B]), sb("log_alpha", [128, V * G, B])
        s0, s1, s2, s3 = (sb(f"small{i}", [128, V * G, B]) for i in range(4))
        pads = [sb(f"pad{k}", [128, B, PAD + S]) for k in range(K)]
        act_t = [sb(f"act_t{k}", [128, B, S]) for k in range(K)]
        squares = sb("squares", [128, 2, B, S])
        ss, norm, rr, r0, nt = (sb(n, [128, 2, B]) for n in ("ss", "norm", "rr", "r0", "nt"))
        length = sb("length", [128, B])
        cs = sb("cs", [128, V, B])
        steps = [sb(f"steps{v}", [128, B, S]) for v in range(V)]
        decay = [sb(f"decay{v}", [128, B, S]) for v in range(V)]
        at = [sb(f"at{v}", [128, B, S]) for v in range(V)]
        lt = [sb(f"lt{v}", [128, B, S]) for v in range(V)]
        x_inv = [sb(f"x_inv{v}", [128, B, S]) for v in range(V)]
        xt_inv = [sb(f"xt_inv{v}", [128, B, S]) for v in range(V)]
        y_buf = [sb(f"y_buf{v}", [128, B, S]) for v in range(V)]
        rhs = [sb(f"rhs{v}", [128, B, S]) for v in range(V)]
        gate = sb("gate", [128, B, V, 128])
        sol = [sb(f"sol{v}", [128, B, 128]) for v in range(V)]
        out_ss, m2, n2, q2, t2 = (sb(n, [128, V, B]) for n in ("out_ss", "m2", "n2", "q2", "t2"))

        small_in, masks_in, wq_in, wg_in, wo_in = (sem(n) for n in ("small_in", "masks_in", "wq_in", "wg_in", "wo_in"))
        cleared, small_made, pre_a, pre_d = (sem(n) for n in ("cleared", "small_made", "pre_a", "pre_d"))
        masked = [sem(f"masked{v}") for v in range(V)]
        p_made, p_kept, tapped, silued = (sem(n) for n in ("p_made", "p_kept", "tapped", "silued"))
        sq_ready, ss_made, ss_ready, norm_ready, g_made, q_made, ss_out, out_norm, y_added = (
            sem(n) for n in ("sq_ready", "ss_made", "ss_ready", "norm_ready", "g_made", "q_made", "ss_out",
                             "out_norm", "y_added"))
        chain, out_chain, gate_made, gate_kept, out_made, scratch, horner = (
            sem(n) for n in ("chain", "out_chain", "gate_made", "gate_kept", "out_made", "scratch", "horner"))
        first_step = sem("first_step")
        steps_ready, d_made, decay_ready, l_ready, a_ready, vt_made, rhs_ready, xt_first, xi_made, x_first = (
            [sem(f"{n}{v}") for v in range(V)] for n in
            ("steps_ready", "d_made", "decay_ready", "l_ready", "a_ready", "vt_made", "rhs_ready", "xt_first",
             "xi_made", "x_first"))
        w_made, w_kept, o_made, o_kept, ct_made, ct_kept = (
            [sem(f"{n}{v}") for v in range(V)] for n in ("w_made", "w_kept", "o_made", "o_kept", "ct_made", "ct_kept"))
        y_made, y_kept, u_made, x_kept, ut_made, xt_kept = (
            [sem(f"{n}{v}") for v in range(V)] for n in ("y_made", "y_kept", "u_made", "x_kept", "ut_made", "xt_kept"))

        CHAIN, OUT_CHAIN = 8, 8
        TILED = 32
        POINTS = 2 * LV

        def pair(v):
            return psum[:, (4 + 2 * v) * BANK:(6 + 2 * v) * BANK].rearrange("p (b t) -> p b t", b=B)

        def low_pair(v):
            return psum[:, 2 * v * BANK:2 * (v + 1) * BANK].rearrange("p (b t) -> p b t", b=B)

        def flat(t):
            return t[:].rearrange("p b t -> p (b t)")

        def even(t3, m):
            return t3.rearrange("p b (j two m) -> p b j two m", two=2, m=m)[:, :, :, 0, :]

        def odd(t3, m):
            return t3.rearrange("p b (j two m) -> p b j two m", two=2, m=m)[:, :, :, 1, :]

        def split(bank_ap, m):
            return bank_ap.rearrange("p (b j m) -> p b j m", b=B, m=m)

        def blocks(m):
            return [(slice(i, i + m), slice(i + m, i + 2 * m)) for i in range(0, 128, 2 * m)]

        def tile(bank_ap, rows, e, b, m):
            return bank_ap[rows, b * 64 + e.start // 2:b * 64 + e.start // 2 + m]

        def tiles(bank_ap, rows, e, m):
            return bank_ap[rows].rearrange("p (b c) -> p b c", b=B)[:, :, e.start // 2:e.start // 2 + m]

        def heads_of(eng, step):
            step(0, True, True)
            with eng.Fori(1, G - 1) as g:
                step(g, False, True)
            step(G - 1, False, False)

        def row(g):
            return w_dram[bass.ds(g, 1)].rearrange("o p c -> (o p) c")

        def load_qkv(sp, g):
            sp.dma_start(w_qkv[:].rearrange("p k t e -> p (k t e)"), row(g)[:, 0:WQKV]).then_inc(wq_in, 16)
            sp.dma_start(taps[:].rearrange("p k j -> p (k j)"), row(g)[:, WQKV:WQKV + WTAP]).then_inc(wq_in, 16)

        def load_gate(sp, g):
            sp.dma_start(w_gate[:].rearrange("p t e -> p (t e)"),
                         row(g)[:, WQKV + WTAP:WQKV + WTAP + WGATE]).then_inc(wg_in, 16)

        def load_out(sp, g):
            sp.dma_start(w_out[:].rearrange("p v c -> p (v c)"), row(g)[:, WQKV + WTAP + WGATE:]).then_inc(wo_in, 16)

        def first_loads(sp):
            sp.dma_start(w_small[:].rearrange("p t e -> p (t e)"), w_small_dram).then_inc(small_in, 16)
            sp.dma_start(bias[:], bias_dram.unsqueeze(0).broadcast_to([128, 2, 16])).then_inc(small_in, 16)
            sp.dma_start(rms_col[:], rms_dram).then_inc(small_in, 16)
            load_qkv(sp, 0)
            sp.dma_start(masks[:], masks_dram).then_inc(masks_in, 16)
            load_gate(sp, 0)
            load_out(sp, 0)

        enter(first_loads)
        with nc.Block() as block:

            @block.sync
            def _(sp):
                sp.wait_ge(tapped, K * TAPS)
                load_qkv(sp, 1)

                def reload(g, more):
                    sp.wait_ge(gate_made, 4 * g + 4)
                    load_gate(sp, g + 1)
                    if more:
                        sp.wait_ge(tapped, K * TAPS * (g + 2))
                        load_qkv(sp, g + 2)
                    sp.wait_ge(out_made, 4 * g + 4)
                    load_out(sp, g + 1)

                with sp.Fori(0, G - 2) as g:
                    reload(g, True)
                reload(G - 2, False)

            @block.gpsimd
            def _(pool):
                for v in range(V):
                    nc.gpsimd.memset(y_buf[v][:], 0.0).then_inc(cleared, 1)
                for k in range(K):
                    nc.gpsimd.memset(pads[k][:], 0.0).then_inc(cleared, 1)
                pool.wait_ge(masks_in, 16)

                def square(g, kind):
                    pool.wait_ge(silued, K * g + kind + 1)
                    nc.gpsimd.tensor_tensor(squares[:, kind], act_t[kind][:], act_t[kind][:], ALU.mult).then_inc(sq_ready, 1)

                def make_steps(g, v):
                    nc.gpsimd.tensor_tensor(steps[v][:],
                                            la[:, bass.ds(V * g + v, 1), :].rearrange("p o b -> p (o b)").unsqueeze(2).broadcast_to([128, B, S]),
                                            up_to.unsqueeze(1).broadcast_to([128, B, S]), ALU.mult).then_inc(steps_ready[v], 1)

                def first_xt(h, first=False):
                    pool.wait_ge(l_ready[0], h + 1)
                    if not first:
                        pool.wait_ge(w_made[0], h)
                    nc.gpsimd.tensor_tensor(xt_inv[0][:], lt[0][:], first_pairs.unsqueeze(1).broadcast_to([128, B, S]),
                                            ALU.mult).then_inc(scratch, 1)
                    pool.wait_ge(scratch, h + 1)
                    nc.gpsimd.tensor_tensor(xt_inv[0][:], xt_inv[0][:], ident[:].unsqueeze(1).broadcast_to([128, B, S]),
                                            ALU.add).then_inc(xt_first[0], 1)

                def mask(h):
                    for v in range(V):
                        pool.wait_ge(a_ready[v], h + 1)
                        nc.gpsimd.tensor_tensor(at[v][:], at[v][:], up_to.unsqueeze(1).broadcast_to([128, B, S]),
                                                ALU.mult).then_inc(masked[v], 1)

                def step(g, first, more):
                    mask(g)
                    if more:
                        for v in range(V):
                            pool.wait_ge(d_made[v], g + 1)
                            make_steps(g + 1, v)
                        pool.wait_ge(ss_made, g + 1)
                        for kind in range(2):
                            square(g + 1, kind)
                        first_xt(g + 1)

                pool.wait_ge(pre_d, 17)
                for v in range(V):
                    make_steps(0, v)
                for kind in range(2):
                    square(0, kind)
                first_xt(0, True)
                heads_of(pool, step)

            @block.tensor
            def _(pe):
                def project(g, n):
                    kind, half = n // 2, n % 2
                    for ct in range(CT):
                        mm = nc.tensor.matmul(bank[n % 4], w_qkv[:, kind, ct, :], xt[:, ct, half * BANK:(half + 1) * BANK],
                                              start=(ct == 0), stop=(ct == CT - 1))
                    mm.then_inc(p_made, 1)

                def project_gate(j):
                    for k in range(2):
                        b = 2 * j + k
                        for ct in range(CT):
                            mm = nc.tensor.matmul(bank[j][:, k * V * 128:(k + 1) * V * 128], xt[:, ct, b * S:(b + 1) * S],
                                                  w_gate[:, ct, :], start=(ct == 0), stop=(ct == CT - 1))
                    mm.then_inc(gate_made, 1)

                def log_decays(h, v):
                    pe.wait_ge(steps_ready[v], h + 1)
                    for half in range(HALVES):
                        dst = bank[2 * v + half]
                        mm = nc.tensor.matmul(dst, after, steps[v][:, half * PER_BANK:(half + 1) * PER_BANK, :].rearrange("p b t -> p (b t)"),
                                         start=True, stop=True)
                    mm.then_inc(d_made[v], 1)

                def turn_values(h, v):
                    pe.wait_ge(silued, K * h + 3 + v)
                    for b in range(B):
                        mm = nc.tensor.transpose(low_pair(v)[:, b, :], act_t[2 + v][:, b, :], ident[:])
                    mm.then_inc(vt_made[v], 1)

                def grams(h, first=False):
                    pe.wait_ge(sq_ready, 2 * h + 2)
                    if first:
                        for v in range(V):
                            pe.wait_ge(decay_ready[v], 1)
                    else:
                        pe.wait_ge(gate_kept, 4 * h)
                    for kind in range(2):
                        for b in range(B):
                            mm = nc.tensor.matmul(bank[3][:, kind * B + b:kind * B + b + 1], squares[:, kind, b, :],
                                                  core.ones[:, 0:1], start=True, stop=True)
                    mm.then_inc(ss_made, 1)
                    pe.wait_ge(silued, K * h + 2)
                    for kind, made in ((1, g_made), (0, q_made)):
                        if kind == 0:
                            pe.wait_ge(ss_ready, h + 1)
                        for b in range(B):
                            o = (0 if kind == 1 else 2) * BANK + b * S
                            mm = nc.tensor.matmul(psum[:, o:o + S], act_t[1][:, b, :], act_t[kind][:, b, :],
                                                  start=True, stop=True)
                        mm.then_inc(made, 1)

                def first_x(h, v, first=False):
                    pe.wait_ge(xt_first[v], h + 1)
                    if not first:
                        pe.wait_ge(y_added, 4 * h - 2 + 2 * v)
                    for b in range(B):
                        mm = nc.tensor.transpose(pair(v)[:, b, :], xt_inv[v][:, b, :], ident[:])
                    mm.then_inc(xi_made[v], 1)

                def point(g, i, more):
                    if i < 2:
                        if i == 0:
                            for v in range(V):
                                pe.wait_ge(a_ready[v], g + 1)
                        turn_values(g, i)
                    elif more and i < 4:
                        pe.wait_ge(rhs_ready[i - 2], g + 1)
                        log_decays(g + 1, i - 2)
                    elif more:
                        n = i - 4
                        if n == 0:
                            pe.wait_ge(wq_in, 32 * (g + 2))
                        if n < 4:
                            pe.wait_ge(decay_ready[n // 2], g + 2)
                        else:
                            pe.wait_ge(p_kept, 8 * (g + 1) + n - 3)
                        project(g + 1, n)

                def gates(g, j, more):
                    if j == 0:
                        pe.wait_ge(wg_in, 16 * (g + 1))
                    if more:
                        pe.wait_ge(p_kept, 8 * (g + 1) + 5 + j)
                    else:
                        pe.wait_ge(rhs_ready[j // 2], g + 1)
                    project_gate(j)

                def open_tiles(m, dst):
                    if m >= TILED:
                        nc.tensor.matmul(dst[:, 0:64], core.zero_bf[:, 0:128], core.zero_bf[:, 0:64], start=True, stop=True)

                def step(g, first, more):
                    for level in range(LV):
                        m = 2 << level
                        for v in range(V):
                            if level == 0:
                                pe.wait_ge(x_first[v], g + 1)
                            else:
                                pe.wait_ge(x_kept[v], (LV - 1) * g + level)
                                pe.wait_ge(xt_kept[v], LV * g + level)
                            open_tiles(m, bank[4 + 2 * v])
                            for b in range(B):
                                if m >= TILED:
                                    for e, o in blocks(m):
                                        mm = nc.tensor.matmul(tile(bank[4 + 2 * v], o, e, b, m), lt[v][e, b, o],
                                                              x_inv[v][e, b, e], start=True, stop=True)
                                else:
                                    mm = nc.tensor.matmul(split(bank[4 + 2 * v], m)[:, b], lt[v][:, b, :],
                                                          even(x_inv[v][:], m)[:, b], start=True, stop=True)
                            mm.then_inc(y_made[v], 1)
                        point(g, 2 * level, more)
                        for v in range(V):
                            pe.wait_ge(y_kept[v], LV * g + level + 1)
                            open_tiles(m, bank[(5 if level < LV - 1 else 4) + 2 * v])
                            if level < LV - 1:
                                for b in range(B):
                                    if m >= TILED:
                                        e, o = blocks(m)[0]
                                        mm = nc.tensor.matmul(tile(bank[5 + 2 * v], o, e, b, m), xt_inv[v][o, b, o],
                                                              y_buf[v][o, b, e], start=True, stop=True)
                                    else:
                                        mm = nc.tensor.matmul(split(bank[5 + 2 * v], m)[:, b], xt_inv[v][:, b, :],
                                                              even(y_buf[v][:], m)[:, b], start=True, stop=True)
                                mm.then_inc(u_made[v], 1)
                            for b in range(B):
                                if m >= TILED:
                                    for e, o in blocks(m):
                                        mm = nc.tensor.matmul(tile(bank[4 + 2 * v], e, e, b, m), y_buf[v][o, b, e],
                                                              xt_inv[v][o, b, o], start=True, stop=True)
                                else:
                                    mm = nc.tensor.matmul(split(bank[4 + 2 * v], m)[:, b], y_buf[v][:, b, :],
                                                          odd(xt_inv[v][:], m)[:, b], start=True, stop=True)
                            mm.then_inc(ut_made[v], 1)
                        point(g, 2 * level + 1, more)
                    for v in range(V):
                        pe.wait_ge(xt_kept[v], LV * g + LV)
                        pe.wait_ge(rhs_ready[v], g + 1)
                        for b in range(B):
                            mm = nc.tensor.matmul(pair(v)[:, b, :], xt_inv[v][:, b, :], rhs[v][:, b, :], start=True, stop=True)
                        mm.then_inc(w_made[v], 1)
                    gates(g, 0, more)
                    gates(g, 1, more)
                    for v in range(V):
                        pe.wait_ge(w_kept[v], g + 1)
                        pe.wait_ge(masked[v], g + 1)
                        for b in range(B):
                            mm = nc.tensor.matmul(pair(v)[:, b, :], at[v][:, b, :], sol[v][:, b, :], start=True, stop=True)
                        mm.then_inc(o_made[v], 1)
                    gates(g, 2, more)
                    gates(g, 3, more)
                    if more:
                        grams(g + 1)
                    for v in range(V):
                        pe.wait_ge(o_kept[v], g + 1)
                        for b in range(B):
                            mm = nc.tensor.transpose(pair(v)[:, b, :], sol[v][:, b, :], ident[:])
                        mm.then_inc(ct_made[v], 1)
                    pe.wait_ge(wo_in, 16 * (g + 1))
                    for v in range(V):
                        pe.wait_ge(ct_kept[v], g + 1)
                    for j in range(4):
                        for k in range(2):
                            b = 2 * j + k
                            for v in range(V):
                                mm = nc.tensor.matmul(bank[4 + j][:, k * C:(k + 1) * C], rhs[v][:, b, :], w_out[:, v, :],
                                                      start=(v == 0), stop=(v == V - 1))
                        mm.then_inc(out_made, 1)
                    if more:
                        for v in range(V):
                            first_x(g + 1, v)

                pe.wait_ge(small_in, 48)
                for b in range(B):
                    for ct in range(CT):
                        mm = nc.tensor.matmul(bank[4][:, b * 32:(b + 1) * 32], xt[:, ct, b * S:(b + 1) * S], w_small[:, ct, :],
                                              start=(ct == 0), stop=(ct == CT - 1))
                mm.then_inc(small_made, 1)
                pe.wait_ge(wq_in, 32)
                for n in range(8):
                    if n >= 4:
                        pe.wait_ge(p_kept, n - 3)
                    project(0, n)
                pe.wait_ge(masks_in, 16)
                for v in range(V):
                    pe.wait_ge(p_kept, 6 + 2 * v)
                    log_decays(0, v)
                grams(0, True)
                for v in range(V):
                    first_x(0, v, True)
                heads_of(pe, step)

            @block.scalar
            def _(act):
                def keep_projection(g, n):
                    kind, half = n // 2, n % 2
                    act.wait_ge(p_made, 8 * g + n + 1)
                    nc.scalar.copy(pads[kind][:, half * PER_BANK:(half + 1) * PER_BANK, PAD:],
                                   bank[n % 4].rearrange("p (b t) -> p b t", b=PER_BANK)).then_inc(p_kept, 1)

                def silu(g, kind):
                    act.wait_ge(tapped, K * TAPS * g + TAPS * (kind + 1))
                    nc.scalar.activation(flat(act_t[kind]), flat(act_t[kind]), ACT.Silu).then_inc(silued, 1)

                def keep_gate(g, j):
                    act.wait_ge(gate_made, 4 * g + j + 1)
                    nc.scalar.activation(gate[:, 2 * j:2 * j + 2].rearrange("p b v e -> p (b v e)"), bank[j], ACT.Silu).then_inc(gate_kept, 1)

                def keep_values(g, v, first):
                    if v == 0:
                        act.wait_ge(chain, CHAIN * (g + 1))
                    act.wait_ge(vt_made[v], g + 1)
                    if not first:
                        act.wait_ge(out_made, 4 * g)
                    for b in range(B):
                        mm = nc.scalar.activation(rhs[v][:, b, :], low_pair(v)[:, b, :], ACT.Copy, scale=length[:, b:b + 1])
                    mm.then_inc(rhs_ready[v], 1)

                def decays(h, v, first=False):
                    act.wait_ge(d_made[v], h + 1)
                    if not first:
                        act.wait_ge(a_ready[v], h)
                    nc.scalar.activation(flat(decay[v]), low_pair(v).rearrange("p b t -> p (b t)"), ACT.Exp).then_inc(decay_ready[v], 1)

                def norms(h):
                    act.wait_ge(ss_ready, h + 1)
                    nc.scalar.activation(norm[:], ss[:], ACT.Sqrt).then_inc(norm_ready, 1)

                def keep_first_x(h, v):
                    act.wait_ge(xi_made[v], h + 1)
                    nc.scalar.copy(flat(x_inv[v]), pair(v).rearrange("p b t -> p (b t)")).then_inc(x_first[v], 1)

                def point(g, i, first, more):
                    if i < 2:
                        keep_values(g, i, first)
                    elif more and i < 4:
                        decays(g + 1, i - 2)
                    elif more:
                        keep_projection(g + 1, i - 4)
                    if more and i in (8, 10):
                        silu(g + 1, (i - 8) // 2)

                def step(g, first, more):
                    for i in range(POINTS):
                        point(g, i, first, more)
                    for v in range(V):
                        act.wait_ge(w_made[v], g + 1)
                        if not first:
                            act.wait_ge(ct_made[v], g)
                        nc.scalar.copy(flat(sol[v]), pair(v).rearrange("p b t -> p (b t)")).then_inc(w_kept[v], 1)
                    keep_gate(g, 0)
                    keep_gate(g, 1)
                    if more:
                        silu(g + 1, 2)
                    for v in range(V):
                        act.wait_ge(o_made[v], g + 1)
                        for b in range(B):
                            mm = nc.scalar.activation(x_inv[v][:, b, :], pair(v)[:, b, :], ACT.Square, accum_out=out_ss[:, v, b:b + 1])
                    mm.then_inc(ss_out, 1)
                    keep_gate(g, 2)
                    keep_gate(g, 3)
                    if more:
                        silu(g + 1, 3)
                    act.wait_ge(out_chain, OUT_CHAIN * g + 2)
                    nc.scalar.activation(n2[:], m2[:], ACT.Sqrt).then_inc(out_norm, 1)
                    if more:
                        norms(g + 1)
                    for v in range(V):
                        act.wait_ge(ct_made[v], g + 1)
                        nc.scalar.activation(flat(rhs[v]), pair(v).rearrange("p b t -> p (b t)"), ACT.Copy, scale=rms_col[:]).then_inc(ct_kept[v], 1)
                    if more:
                        for v in range(V):
                            keep_first_x(g + 1, v)

                act.wait_ge(pre_d, 2)
                nc.scalar.activation(s0[:], s0[:], ACT.Exp, scale=-1.0).then_inc(pre_a, 1)
                act.wait_ge(pre_d, 3)
                nc.scalar.activation(s2[:], s2[:], ACT.Exp).then_inc(pre_a, 1)
                nc.scalar.activation(bias[:, 1], bias[:, 1], ACT.Exp).then_inc(pre_a, 1)
                act.wait_ge(cleared, V + K)
                for n in range(8):
                    keep_projection(0, n)
                for v in range(V):
                    decays(0, v, True)
                for kind in range(K):
                    silu(0, kind)
                norms(0)
                for v in range(V):
                    keep_first_x(0, v)
                heads_of(act, step)

            @block.vector
            def _(dve):
                vec = nc.vector

                def tap(g, kind, j):
                    n = K * TAPS * g + TAPS * kind + j
                    src = pads[kind][:, :, j:j + S]
                    if j == 0:
                        dve.wait_ge(wq_in, 32 * (g + 1))
                        dve.wait_ge(p_kept, 8 * g + 2 * kind + 2)
                        vec.tensor_scalar(act_t[kind][:], src, taps[:, kind, 0:1], None, ALU.mult).then_inc(tapped, 1)
                    else:
                        dve.wait_ge(tapped, n)
                        vec.scalar_tensor_tensor(out=act_t[kind][:], in0=src, scalar=taps[:, kind, j:j + 1], in1=act_t[kind][:],
                                                 op0=ALU.mult, op1=ALU.add).then_inc(tapped, 1)

                def point(g, i, more):
                    if more and i >= 6:
                        n = 2 * (i - 6)
                        if i == 10:
                            dve.wait_ge(vt_made[0], g + 1)
                        for t in (n, n + 1):
                            tap(g + 1, t // TAPS, t % TAPS)

                def lengths(h, first=False):
                    def link(i):
                        dve.wait_ge(chain, CHAIN * h + i)

                    dve.wait_ge(ss_made, h + 1)
                    if not first:
                        dve.wait_ge(out_chain, OUT_CHAIN * h)
                    vec.tensor_scalar(ss[:].rearrange("p k b -> p (k b)"), bank[3][:, 0:2 * B], EPS, None, ALU.add).then_inc(ss_ready, 1)
                    dve.wait_ge(ss_ready, h + 1)
                    vec.reciprocal(rr[:], ss[:]).then_inc(chain, 1)
                    link(1)
                    if not first:
                        for v in range(V):
                            dve.wait_ge(a_ready[v], h)
                    vec.tensor_tensor(cs[:], beta[:, bass.ds(V * h, V), :], rr[:, 1:2].broadcast_to([128, V, B]), ALU.mult).then_inc(chain, 1)
                    dve.wait_ge(norm_ready, h + 1)
                    vec.reciprocal(r0[:], norm[:]).then_inc(chain, 1)
                    link(3)
                    vec.tensor_tensor(nt[:], r0[:], r0[:], ALU.mult).then_inc(chain, 1)
                    link(4)
                    vec.tensor_tensor(nt[:], nt[:], ss[:], ALU.mult).then_inc(chain, 1)
                    link(5)
                    vec.tensor_scalar(nt[:], nt[:], -0.5, 1.5, ALU.mult, ALU.add).then_inc(chain, 1)
                    link(6)
                    vec.tensor_tensor(r0[:], r0[:], nt[:], ALU.mult).then_inc(chain, 1)
                    link(7)
                    if not first:
                        dve.wait_ge(rhs_ready[V - 1], h)
                    vec.tensor_tensor(length[:], r0[:, 1], ss[:, 1], ALU.mult).then_inc(chain, 1)

                def weigh(h, v, out, base, made, ready):
                    dve.wait_ge(decay_ready[v], h + 1)
                    dve.wait_ge(chain, CHAIN * h + 2)
                    dve.wait_ge(made, h + 1)
                    for b in range(B):
                        o = base * BANK + b * S
                        mm = vec.scalar_tensor_tensor(out=out[v][:, b, :], in0=decay[v][:, b, :], scalar=cs[:, v, b:b + 1],
                                                      in1=psum[:, o:o + S], op0=ALU.mult, op1=ALU.mult)
                    mm.then_inc(ready[v], 1)

                def first_xt(h, first=False):
                    dve.wait_ge(l_ready[1], h + 1)
                    if not first:
                        dve.wait_ge(w_made[1], h)
                    vec.tensor_tensor(xt_inv[1][:], lt[1][:], first_pairs.unsqueeze(1).broadcast_to([128, B, S]),
                                      ALU.mult).then_inc(first_step, 1)
                    dve.wait_ge(first_step, h + 1)
                    vec.tensor_tensor(xt_inv[1][:], xt_inv[1][:], ident[:].unsqueeze(1).broadcast_to([128, B, S]),
                                      ALU.add).then_inc(xt_first[1], 1)

                def step(g, first, more):
                    def link(i):
                        dve.wait_ge(out_chain, OUT_CHAIN * g + i)

                    for level in range(LV):
                        m = 2 << level
                        for v in range(V):
                            dve.wait_ge(y_made[v], LV * g + level + 1)
                            if m >= TILED:
                                for e, o in blocks(m):
                                    ins = vec.tensor_copy(y_buf[v][o, :, e], tiles(bank[4 + 2 * v], o, e, m))
                                ins.then_inc(y_kept[v], 1)
                                continue
                            vec.tensor_tensor(even(y_buf[v][:], m), split(bank[4 + 2 * v], m),
                                              odd_rows[level].unsqueeze(1).unsqueeze(3).broadcast_to([128, B, 64 // m, m]),
                                              ALU.mult).then_inc(y_kept[v], 1)
                        point(g, 2 * level, more)
                        for v in range(V):
                            if level < LV - 1:
                                dve.wait_ge(u_made[v], (LV - 1) * g + level + 1)
                                if m >= TILED:
                                    e, o = blocks(m)[0]
                                    vec.tensor_tensor(x_inv[v][o, :, e], x_inv[v][o, :, e], tiles(bank[5 + 2 * v], o, e, m),
                                                      ALU.subtract).then_inc(x_kept[v], 1)
                                else:
                                    vec.tensor_tensor(even(x_inv[v][:], m), even(x_inv[v][:], m), split(bank[5 + 2 * v], m),
                                                      ALU.subtract).then_inc(x_kept[v], 1)
                            dve.wait_ge(ut_made[v], LV * g + level + 1)
                            if m >= TILED:
                                for e, o in blocks(m):
                                    ins = vec.tensor_tensor(xt_inv[v][e, :, o], xt_inv[v][e, :, o], tiles(bank[4 + 2 * v], e, e, m),
                                                            ALU.subtract)
                                ins.then_inc(xt_kept[v], 1)
                                continue
                            vec.scalar_tensor_tensor(out=odd(xt_inv[v][:], m), in0=split(bank[4 + 2 * v], m),
                                                     scalar=even_rows[level], in1=odd(xt_inv[v][:], m),
                                                     op0=ALU.mult, op1=ALU.add).then_inc(xt_kept[v], 1)
                        point(g, 2 * level + 1, more)
                    if more:
                        dve.wait_ge(vt_made[1], g + 1)
                        for j in range(TAPS):
                            tap(g + 1, 3, j)
                    dve.wait_ge(ss_out, g + 1)
                    vec.tensor_tensor(m2[:], out_ss[:], rr[:, 0:1].broadcast_to([128, V, B]), ALU.mult).then_inc(out_chain, 1)
                    link(1)
                    vec.tensor_scalar(m2[:], m2[:], 1.0 / (128 * 128), EPS, ALU.mult, ALU.add).then_inc(out_chain, 1)
                    dve.wait_ge(out_norm, g + 1)
                    vec.reciprocal(q2[:], n2[:]).then_inc(out_chain, 1)
                    link(3)
                    vec.tensor_tensor(t2[:], q2[:], q2[:], ALU.mult).then_inc(out_chain, 1)
                    link(4)
                    vec.tensor_tensor(t2[:], t2[:], m2[:], ALU.mult).then_inc(out_chain, 1)
                    link(5)
                    vec.tensor_scalar(t2[:], t2[:], -0.5 * 128 ** -0.5, 1.5 * 128 ** -0.5, ALU.mult, ALU.add).then_inc(out_chain, 1)
                    link(6)
                    vec.tensor_tensor(q2[:], q2[:], t2[:], ALU.mult).then_inc(out_chain, 1)
                    link(7)
                    vec.tensor_tensor(q2[:], q2[:], r0[:, 0:1].broadcast_to([128, V, B]), ALU.mult).then_inc(out_chain, 1)
                    link(8)
                    dve.wait_ge(gate_kept, 4 * g + 4)
                    for v in range(V):
                        dve.wait_ge(o_made[v], g + 1)
                        for b in range(B):
                            mm = vec.scalar_tensor_tensor(out=sol[v][:, b, :], in0=pair(v)[:, b, :], scalar=q2[:, v, b:b + 1],
                                                          in1=gate[:, b, v, :], op0=ALU.mult, op1=ALU.mult)
                        mm.then_inc(o_kept[v], 1)
                    if more:
                        lengths(g + 1)
                        for v in range(V):
                            weigh(g + 1, v, lt, 0, g_made, l_ready)
                        first_xt(g + 1)
                    for j in range(4):
                        dve.wait_ge(out_made, 4 * g + j + 1)
                        if not first:
                            dve.wait_ge(y_added, 4 * (g - 1) + j + 1)
                        res = core.x if first else core.y
                        vec.tensor_tensor(core.y[:, 2 * j:2 * j + 2, :], res[:, 2 * j:2 * j + 2, :],
                                          bank[4 + j].rearrange("p (b c) -> p b c", b=2), ALU.add).then_inc(y_added, 1)
                        if not more:
                            dve.wait_ge(y_added, 4 * g + j + 1)
                            core.batch_stats(2 * j)
                            core.batch_stats(2 * j + 1)
                    if more:
                        for v in range(V):
                            weigh(g + 1, v, at, 2, q_made, a_ready)

                dve.wait_ge(small_made, 1)
                dve.wait_ge(small_in, 48)

                def pre(i):
                    dve.wait_ge(pre_d, i)

                proj = bank[4][:, 0:B * 32].rearrange("p (b h) -> p h b", b=B)
                vec.tensor_tensor(s1[:], proj[:, 16:32, :], bias[:, 0, :].unsqueeze(2).broadcast_to([128, 16, B]), ALU.add).then_inc(pre_d, 1)
                vec.tensor_copy(s0[:], proj[:, 0:16, :]).then_inc(pre_d, 1)
                pre(1)
                vec.scalar_tensor_tensor(out=s2[:], in0=s1[:], scalar=-1.0, in1=s1[:], op0=ALU.mult, op1=ALU.min).then_inc(pre_d, 1)
                dve.wait_ge(pre_a, 1)
                vec.tensor_scalar(s0[:], s0[:], 1.0, None, ALU.add).then_inc(pre_d, 1)
                pre(4)
                vec.reciprocal(beta[:], s0[:]).then_inc(pre_d, 1)
                dve.wait_ge(pre_a, 2)
                pre(5)
                vec.tensor_scalar(s0[:], s2[:], 2.0, None, ALU.add).then_inc(pre_d, 1)
                pre(6)
                vec.reciprocal(s0[:], s0[:]).then_inc(pre_d, 1)
                pre(7)
                vec.tensor_tensor(s2[:], s2[:], s0[:], ALU.mult).then_inc(pre_d, 1)
                pre(8)
                vec.tensor_tensor(s3[:], s2[:], s2[:], ALU.mult).then_inc(pre_d, 1)
                pre(9)
                vec.tensor_scalar(s0[:], s3[:], LOG_TERMS[0], LOG_TERMS[1], ALU.mult, ALU.add).then_inc(pre_d, 1)
                pre(10)
                for i, c in enumerate(LOG_TERMS[2:] + (1.0,)):
                    vec.tensor_tensor(s0[:], s0[:], s3[:], ALU.mult).then_inc(horner, 1)
                    dve.wait_ge(horner, 2 * i + 1)
                    vec.tensor_scalar(s0[:], s0[:], c, None, ALU.add).then_inc(horner, 1)
                    dve.wait_ge(horner, 2 * i + 2)
                vec.tensor_tensor(s0[:], s0[:], s2[:], ALU.mult).then_inc(pre_d, 1)
                vec.tensor_scalar(s1[:], s1[:], 0.0, None, ALU.max).then_inc(pre_d, 1)
                pre(12)
                vec.tensor_scalar(s0[:], s0[:], 2.0, None, ALU.mult).then_inc(pre_d, 1)
                pre(13)
                vec.tensor_tensor(s1[:], s0[:], s1[:], ALU.add).then_inc(pre_d, 1)
                dve.wait_ge(pre_a, 3)
                pre(14)
                vec.tensor_tensor(s1[:], s1[:], bias[:, 1, :].unsqueeze(2).broadcast_to([128, 16, B]), ALU.mult).then_inc(pre_d, 1)
                pre(15)
                vec.tensor_scalar(la[:], s1[:], -1.0, None, ALU.mult).then_inc(pre_d, 2)
                pre(17)
                dve.wait_ge(cleared, V + K)
                dve.wait_ge(masks_in, 16)
                for kind in range(K):
                    for j in range(TAPS):
                        tap(0, kind, j)
                lengths(0, True)
                for v in range(V):
                    weigh(0, v, lt, 0, g_made, l_ready)
                first_xt(0, True)
                for v in range(V):
                    weigh(0, v, at, 2, q_made, a_ready)
                heads_of(dve, step)


def rotary_cross_attention(core, ctx_dram, w_dram, cols_dram, bv_dram, enc_dram, sign_dram, enter):
    nc = core.nc
    HEADS, D, P = 16, 8, C
    SCALE = float(D) ** -0.5
    PT = P // 128
    G = 4
    UNITS = (HEADS // G) * PT
    Q_PARTS, K_PARTS = (0, 0, 0, 1, 1, 2), (0, 1, 2, 0, 1, 0)
    ROWS = len(Q_PARTS) * D
    ALL_ROWS = ROWS + 2
    DIAG = 128 + D
    AHEAD = 3
    HG = HEADS // 2
    psum, bank = core.psum, core.bank
    with ExitStack() as ctx:
        def sb(name, shape, dt=F32):
            return core.sb(ctx, "b_" + name, shape, dt)

        def sem(name):
            return core.sem(ctx, "b_" + name)

        w = sb("w", [128, 6, 128])
        cols, bv, sign = sb("cols", [128, 5]), sb("bv", [128, 128]), sb("sign", [128, 1])
        enc = sb("enc", [128, 2, P])
        src = sb("src", [128, P])
        t1, t2 = sb("t1", [128, P]), sb("t2", [128, P])
        rot = [sb(f"rot{j}", [128, P]) for j in range(2)]
        rest = [sb(f"rest{j}", [128, P]) for j in range(2)]
        parts = [sb(f"parts{j}", [128, 3, P], BF16) for j in range(2)]
        ones_bf = sb("ones_bf", [2 * HEADS, P], BF16)
        stack = [sb(f"stack{j}", [ALL_ROWS, B, HEADS, P], BF16) for j in range(2)]
        v = sb("v", [128, B, PT, HEADS, D])
        v_wide = sb("v_wide", [128, PT * 2, HG * DIAG])
        top = sb("top", [128, PT, HEADS])
        top_bf = sb("top_bf", [128, PT, 4, HEADS], BF16)
        neg_top = sb("neg_top", [128, 128], BF16)
        probs = [sb(f"probs{i}", [128, 2, PT, P]) for i in range(2)]
        mixes = core.xt[:, 0, 0:2 * P].rearrange("p (g q) -> p g q", g=2)
        inv = sb("inv", [128, P])
        att_t = sb("att_t", [128, P])

        w_in, sign_done, filled, src_in, stack_in, rows_in = (
            sem(n) for n in ("w_in", "sign_done", "filled", "src_in", "stack_in", "rows_in"))
        made, read, rotated, high_done, rest_done, mid_done, low_done = (
            [sem(f"{n}{j}") for j in range(2)] for n in ("made", "read", "rotated", "high_done", "rest_done", "mid_done", "low_done"))
        v_made, v_kept, top_high, top_low, top_turned, neg_kept, out_made, y_done = (
            sem(n) for n in ("v_made", "v_kept", "top_high", "top_low", "top_turned", "neg_kept", "out_made", "y_done"))
        mix_kept, inv_ready, att_ready = sem("mix_kept"), sem("inv_ready"), sem("att_ready")
        wide_ready = sem("wide_ready")
        s_made, top_ready, st_made, exp_done, mixed = (
            sem(n) for n in ("s_made", "top_ready", "st_made", "exp_done", "mixed"))
        STACK_LOADS = 16 * (len(Q_PARTS) + len(K_PARTS) + 1)
        LAST = B - 1

        def ahead(b, u):
            return (b + 1, u + AHEAD) if u + AHEAD < UNITS else (b + 2, u + AHEAD - UNITS)

        def periods(eng, period, prologue):
            prologue()
            period(0, True)
            with eng.Fori(1, B - AHEAD) as b:
                period(b, False)
            for b in range(B - AHEAD, B):
                period(b, False)

        def wide(g, side):
            tiles = v_wide[:].rearrange("p (t g) (h c) -> p t g h c", g=2, c=DIAG)
            return tiles[:, :, g, :, side * HG * D:side * HG * D + D]

        def has(b, distance):
            return not isinstance(b, int) or b + distance < B

        def load_context(sp, b):
            sp.dma_start(src[:], ctx_dram[bass.ds(b, 1)].rearrange("o s p -> (o s) p")).then_inc(src_in, 16)

        def first_loads(sp):
            sp.dma_start(w[:].rearrange("p k o -> p (k o)"), w_dram).then_inc(w_in, 16)
            sp.dma_start(cols[:], cols_dram).then_inc(w_in, 16)
            sp.dma_start(sign[:], sign_dram).then_inc(w_in, 16)
            sp.dma_start(bv[:], bv_dram.unsqueeze(0).broadcast_to([128, 128])).then_inc(w_in, 16)
            for d in range(D):
                sp.dma_start(enc[d * HEADS:(d + 1) * HEADS, :, :],
                             enc_dram[:, d, :].unsqueeze(0).broadcast_to([HEADS, 2, P])).then_inc(w_in, 16)

            load_context(sp, 0)

        enter(first_loads)
        with nc.Block() as block:

            @block.sync
            def _(sp):
                def spread(b):
                    for j in range(2):
                        sp.wait_ge(low_done[j], b + 1)
                    for j, which in ((0, Q_PARTS), (1, K_PARTS)):
                        for r, part in enumerate(which):
                            sp.dma_start(stack[j][r * D:(r + 1) * D, bass.ds(b, 1)].rearrange("d o h p -> d (o h) p"),
                                         parts[j][:, part, :]).then_inc(stack_in, 16)
                    sp.dma_start(stack[1][ROWS:ALL_ROWS, bass.ds(b, 1)].rearrange("d o h p -> d (o h) p"),
                                 ones_bf[:]).then_inc(stack_in, 16)

                def prologue():
                    sp.wait_ge(filled, 1)
                    for b in range(AHEAD):
                        spread(b)
                        sp.wait_ge(v_made, b + 1)
                        load_context(sp, b + 1)

                def period(b, first):
                    if has(b, AHEAD):
                        spread(b + AHEAD)
                    if has(b, AHEAD + 1):
                        sp.wait_ge(v_made, b + AHEAD + 1)
                        load_context(sp, b + AHEAD + 1)

                prologue()
                period(0, True)
                with sp.Fori(1, B - AHEAD - 1) as b:
                    period(b, False)
                for b in range(B - AHEAD - 1, B):
                    period(b, False)

            @block.gpsimd
            def _(pool):
                nc.gpsimd.memset(ones_bf[:], 1.0).then_inc(filled, 1)
                nc.gpsimd.memset(top_bf[:], 0.0).then_inc(filled, 1)
                nc.gpsimd.memset(v_wide[:], 0.0).then_inc(filled, 1)
                pool.wait_ge(filled, 3)
                for g in range(2):
                    nc.gpsimd.memset(wide(g, 1 - g), 1.0).then_inc(filled, 1)

                def widen(b, g):
                    nc.gpsimd.tensor_copy(wide(g, g), v[:, bass.ds(b, 1), :, g * HG:(g + 1) * HG, :].rearrange("p o t h d -> p (o t) h d")
                                          ).then_inc(wide_ready, 1)

                def split(b):
                    for j in range(2):
                        pool.wait_ge(high_done[j], b + 1)
                        nc.gpsimd.tensor_tensor(rest[j][:], rot[j][:], parts[j][:, 0, :], ALU.subtract).then_inc(rest_done[j], 1)
                        pool.wait_ge(mid_done[j], b + 1)
                        nc.gpsimd.tensor_tensor(parts[j][:, 2, :], rest[j][:], parts[j][:, 1, :], ALU.subtract).then_inc(low_done[j], 1)

                def period(b, more):
                    if more:
                        split(b + AHEAD)
                    pool.wait_ge(mixed, UNITS * b + UNITS // 2)
                    widen(b + 1, 0)
                    pool.wait_ge(mixed, UNITS * (b + 1))
                    widen(b + 1, 1)

                for b in range(AHEAD):
                    split(b)
                pool.wait_ge(v_kept, 1)
                for g in range(2):
                    widen(0, g)
                with pool.Fori(0, B - AHEAD) as b:
                    period(b, True)
                for b in range(B - AHEAD, LAST):
                    period(b, False)

            @block.tensor
            def _(pe):
                def project(b, j):
                    rhs = core.x[:, bass.ds(b, 1), :].rearrange("p o c -> p (o c)") if j == 0 else src[:]
                    for i in range(2):
                        mm = nc.tensor.matmul(bank[7][:, i * P:(i + 1) * P], w[:, 2 * j + i, :], rhs, start=True, stop=True)
                    mm.then_inc(made[j], 1)

                def prepare_k(b):
                    pe.wait_ge(src_in, 16 * b + 16)
                    pe.wait_ge(read[0], b + 1)
                    project(b, 1)

                def prepare_v(b):
                    pe.wait_ge(read[1], b + 1)
                    for t in range(PT):
                        mm = nc.tensor.matmul(bank[7][:, t * 128:(t + 1) * 128], src[:, t * 128:(t + 1) * 128],
                                              w[:, 4, :], start=True, stop=True)
                    mm.then_inc(v_made, 1)

                def scores(b, u, first=False):
                    g, t = u // PT, u % PT
                    if u == 0:
                        pe.wait_ge(stack_in, STACK_LOADS * (b + 1))
                    if not first:
                        pe.wait_ge(top_ready, UNITS * b + u)
                    for i in range(G):
                        h = g * G + i
                        mm = nc.tensor.matmul(psum[:, i * P:(i + 1) * P],
                                              stack[0][0:ROWS, bass.ds(b, 1), h, t * 128:(t + 1) * 128].rearrange("k o q -> k (o q)"),
                                              stack[1][0:ROWS, bass.ds(b, 1), h, :].rearrange("k o q -> k (o q)"), start=True, stop=True)
                    mm.then_inc(s_made, 1)

                def turn_top(b):
                    pe.wait_ge(top_low, b + 1)
                    pe.wait_ge(w_in, 16)
                    nc.tensor.transpose(core.bank_bf(7)[:, 0:128], top_bf[:].rearrange("p t k h -> p (t k h)"),
                                        core.ident_bf[:]).then_inc(top_turned, 1)

                def scores_t(b, u, first):
                    if u == 0:
                        pe.wait_ge(rows_in, 32 * b + 32)
                    if not (first and u < 2):
                        pe.wait_ge(exp_done, UNITS * b + u - 1)
                    for i in range(2):
                        for m in range(PT):
                            o = (2 + 2 * (u % 2)) * BANK + (i * PT + m) * P
                            mm = nc.tensor.matmul(psum[:, o:o + P],
                                                  stack[1][:, bass.ds(b, 1), 2 * u + i, m * 128:(m + 1) * 128].rearrange("k o q -> k (o q)"),
                                                  stack[0][:, bass.ds(b, 1), 2 * u + i, :].rearrange("k o q -> k (o q)"), start=True, stop=True)
                    mm.then_inc(st_made, 1)

                def mix(b, u):
                    g = u // (UNITS // 2)
                    pe.wait_ge(exp_done, UNITS * b + u + 1)
                    if u % (UNITS // 2) == 0:
                        pe.wait_ge(wide_ready, 2 * b + g + 1)
                        if g == 0 and not (isinstance(b, int) and b == 0):
                            pe.wait_ge(mix_kept, b)
                    for i in range(2):
                        h = (2 * u + i) % HG
                        for m in range(PT):
                            mm = nc.tensor.matmul(bank[6][:, g * P:(g + 1) * P], v_wide[:, 2 * m + g, h * 128:(h + 1) * 128],
                                                  probs[u % 2][:, i, m, :], start=(h == 0 and m == 0),
                                                  stop=(h == HG - 1 and m == PT - 1))
                    mm.then_inc(mixed, 1)

                def output(b):
                    pe.wait_ge(att_ready, b + 1)
                    nc.tensor.matmul(bank[7][:, 0:P], w[:, 5, :], att_t[:], start=True, stop=True).then_inc(out_made, 1)

                def prologue():
                    pe.wait_ge(w_in, 16 * (4 + D))
                    for b in range(AHEAD):
                        if b > 0:
                            pe.wait_ge(v_kept, b)
                        project(b, 0)
                        prepare_k(b)
                        prepare_v(b)
                    for u in range(UNITS):
                        scores(0, u, u == 0)
                    pe.wait_ge(v_kept, AHEAD)
                    turn_top(0)
                    for u in range(AHEAD):
                        scores(1, u)

                def period(b, first):
                    for u in range(UNITS):
                        scores_t(b, u, first)
                        nb, nu = ahead(b, u)
                        if has(b, 1 if u + AHEAD < UNITS else 2):
                            scores(nb, nu)
                        if u > 0:
                            mix(b, u - 1)
                        elif not first:
                            mix(b - 1, UNITS - 1)
                        if has(b, AHEAD):
                            if u == 0:
                                pe.wait_ge(neg_kept, b + 1)
                                project(b + AHEAD, 0)
                            elif u == 1:
                                prepare_k(b + AHEAD)
                            elif u == 2:
                                prepare_v(b + AHEAD)
                        if u == 3 and not first:
                            if has(b, AHEAD):
                                pe.wait_ge(v_kept, b + AHEAD + 1)
                            else:
                                pe.wait_ge(neg_kept, b + 1)
                            output(b - 1)
                        if u == 5 and has(b, 1):
                            if first:
                                pe.wait_ge(v_kept, AHEAD + 1)
                            else:
                                pe.wait_ge(y_done, b)
                            turn_top(b + 1)

                periods(pe, period, prologue)
                mix(LAST, UNITS - 1)
                pe.wait_ge(y_done, LAST)
                output(LAST)

            @block.scalar
            def _(act):
                def split(b, j, again=True):
                    act.wait_ge(rotated[j], b + 1)
                    if again:
                        act.wait_ge(stack_in, STACK_LOADS * b)
                    nc.scalar.copy(parts[j][:, 0, :], rot[j][:]).then_inc(high_done[j], 1)
                    act.wait_ge(rest_done[j], b + 1)
                    nc.scalar.copy(parts[j][:, 1, :], rest[j][:]).then_inc(mid_done[j], 1)

                def keep_neg(b, again=True):
                    act.wait_ge(top_turned, b + 1)
                    if again:
                        act.wait_ge(rows_in, 32 * b)
                    nc.scalar.activation(neg_top[:], core.bank_bf(7)[:, 0:128], ACT.Copy,
                                         scale=-1.0).then_inc(neg_kept, 1)
                    act.wait_ge(neg_kept, b + 1)
                    for t in range(PT):
                        act.dma_start(stack[0][ROWS:ALL_ROWS, bass.ds(b, 1), :, t * 128:(t + 1) * 128].rearrange("d o h p -> d (o h) p"),
                                      neg_top[t * 4 * HEADS:(t * 4 + 2) * HEADS, :]).then_inc(rows_in, 16)

                def exps(b, u, first):
                    act.wait_ge(st_made, UNITS * b + u + 1)
                    if not (first and u < 2):
                        act.wait_ge(mixed, UNITS * b + u - 1)
                    o = (2 + 2 * (u % 2)) * BANK
                    nc.scalar.activation(probs[u % 2][:].rearrange("p i m q -> p (i m q)"), psum[:, o:o + 2 * BANK],
                                         ACT.Exp, scale=SCALE).then_inc(exp_done, 1)

                def keep_mix(b):
                    act.wait_ge(mixed, UNITS * (b + 1))
                    if not (isinstance(b, int) and b == 0):
                        act.wait_ge(att_ready, b)
                    side = [slice(g * HG * D, (g + 1) * HG * D) for g in range(2)]
                    for g in range(2):
                        nc.scalar.copy(mixes[side[g], 0, :], bank[6][side[g], g * P:(g + 1) * P])
                        ins = nc.scalar.copy(mixes[side[g], 1, :], bank[6][side[1 - g], g * P:(g + 1) * P])
                    ins.then_inc(mix_kept, 1)

                def prologue():
                    for b in range(AHEAD):
                        split(b, 0, b > 0)
                        split(b, 1, b > 0)
                    keep_neg(0, False)

                def period(b, first):
                    for u in range(UNITS):
                        if u == 1 and not first:
                            keep_mix(b - 1)
                        exps(b, u, first)
                        if has(b, AHEAD) and 1 <= u <= 2:
                            split(b + AHEAD, u - 1)
                        if u == 5 and has(b, 1):
                            keep_neg(b + 1)

                periods(act, period, prologue)
                keep_mix(LAST)

            @block.vector
            def _(dve):
                vec = nc.vector

                def rotate(b, j, again=True):
                    dve.wait_ge(made[j], b + 1)
                    if j == 1:
                        dve.wait_ge(rotated[0], b + 1)
                    elif again:
                        dve.wait_ge(rotated[1], b)
                    vec.scalar_tensor_tensor(out=t1[:], in0=bank[7][:, 0:P], scalar=cols[:, 2 * j:2 * j + 1],
                                             in1=enc[:, 0, :], op0=ALU.add, op1=ALU.mult)
                    vec.scalar_tensor_tensor(out=t2[:], in0=bank[7][:, P:2 * P], scalar=cols[:, 2 * j + 1:2 * j + 2],
                                             in1=enc[:, 1, :], op0=ALU.add, op1=ALU.mult).then_inc(read[j], 1)
                    dve.wait_ge(read[j], b + 1)
                    if again:
                        dve.wait_ge(rest_done[j], b)
                    vec.tensor_tensor(rot[j][:], t1[:], t2[:], ALU.add).then_inc(rotated[j], 1)

                def keep_v(b):
                    dve.wait_ge(v_made, b + 1)
                    vec.tensor_tensor(v[:, bass.ds(b, 1), :, :, 0:D].rearrange("p o t h d -> p (o t) h d"),
                                      bank[7][:, 0:P].rearrange("p (t h d) -> p t h d", t=PT, d=D),
                                      bv[:].rearrange("p (h d) -> p h d", d=D).unsqueeze(1).broadcast_to([128, PT, HEADS, D]),
                                      ALU.add).then_inc(v_kept, 1)

                def maxima(b, u):
                    g, t = u // PT, u % PT
                    dve.wait_ge(s_made, UNITS * b + u + 1)
                    if u == 0 and not (isinstance(b, int) and b == 0):
                        dve.wait_ge(top_low, b)
                    vec.tensor_reduce(top[:, t, g * G:(g + 1) * G], psum[:, 0:G * P].rearrange("p (i m) -> p i m", i=G), AX.X,
                                      ALU.max).then_inc(top_ready, 1)
                    if u == UNITS - 1:
                        dve.wait_ge(top_ready, UNITS * (b + 1))
                        if not (isinstance(b, int) and b == 0):
                            dve.wait_ge(top_turned, b)
                        vec.tensor_copy(top_bf[:, :, 0, :], top[:]).then_inc(top_high, 1)
                        dve.wait_ge(top_high, b + 1)
                        vec.tensor_tensor(top_bf[:, :, 1, :], top[:], top_bf[:, :, 0, :], ALU.subtract).then_inc(top_low, 1)

                def normalize(b):
                    dve.wait_ge(mix_kept, b + 1)
                    if not (isinstance(b, int) and b == 0):
                        dve.wait_ge(att_ready, b)
                        dve.wait_ge(out_made, b)
                    vec.reciprocal(inv[:], mixes[:, 1, :]).then_inc(inv_ready, 1)
                    dve.wait_ge(inv_ready, b + 1)
                    vec.tensor_tensor(att_t[:], mixes[:, 0, :], inv[:], ALU.mult).then_inc(att_ready, 1)

                def finish(b):
                    dve.wait_ge(out_made, b + 1)
                    vec.scalar_tensor_tensor(out=core.y[:, bass.ds(b, 1), :].rearrange("p o c -> p (o c)"),
                                             in0=bank[7][:, 0:P], scalar=cols[:, 4:5],
                                             in1=core.x[:, bass.ds(b, 1), :].rearrange("p o c -> p (o c)"),
                                             op0=ALU.add, op1=ALU.add).then_inc(y_done, 1)

                def prologue():
                    dve.wait_ge(w_in, 16 * (4 + D))
                    vec.tensor_scalar(enc[:, 1, :], enc[:, 1, :], sign[:], None, ALU.mult).then_inc(sign_done, 1)
                    dve.wait_ge(sign_done, 1)
                    for b in range(AHEAD):
                        rotate(b, 0, b > 0)
                        rotate(b, 1, b > 0)
                        keep_v(b)
                    dve.wait_ge(filled, 2)
                    for u in range(UNITS):
                        maxima(0, u)
                    for u in range(AHEAD):
                        maxima(1, u)

                def period(b, first):
                    for u in range(UNITS):
                        nb, nu = ahead(b, u)
                        if has(b, 1 if u + AHEAD < UNITS else 2):
                            maxima(nb, nu)
                        if u == 2 and not first:
                            normalize(b - 1)
                        if has(b, AHEAD):
                            if u < 2:
                                rotate(b + AHEAD, u)
                            elif u == 2:
                                keep_v(b + AHEAD)
                        if u == 4 and not first:
                            finish(b - 1)
                        if isinstance(b, int) and b == LAST and u < LAST:
                            dve.wait_ge(y_done, u + 1)
                            core.batch_stats(u)

                periods(dve, period, prologue)
                normalize(LAST)
                finish(LAST)
                dve.wait_ge(y_done, B)
                core.batch_stats(LAST)


def route_tokens(core, sim_dram, gates_dram, weights_dram, enter):
    nc = core.nc
    EX = 16
    FIRST = 64.0
    with ExitStack() as ctx:
        def sb(name, shape, dt=F32):
            return core.sb(ctx, "r_" + name, shape, dt)

        def sem(name):
            return core.sem(ctx, "r_" + name)

        sim, sim_sq = sb("sim", [128, CT, EX]), sb("sim_sq", [128, CT, EX])
        gates, number = sb("gates", [128, EX]), sb("number", [128, EX])
        sim_len, x_len = sb("sim_len", [128, EX]), sb("x_len", [128, B])
        x_sq = sb("x_sq", [128, B])
        logits, e_all, is_on, key, pick1, pick2, low = (
            sb(n, [128, B, EX]) for n in ("logits", "e_all", "is_on", "key", "pick1", "pick2", "low"))
        top, top2, first, idle, total = (sb(n, [128, B]) for n in ("top", "top2", "first", "idle", "total"))
        w_t = sb("w_t", [EX, N])
        inputs_in, number_ready, sim_sq_ready, sim_sums, logits_made, w_turned = (
            sem(n) for n in ("inputs_in", "number_ready", "sim_sq_ready", "sim_sums", "logits_made", "w_turned"))
        act_step, step, w_kept, stored = (sem(n) for n in ("act_step", "step", "w_kept", "stored"))
        sums, raw = core.bank[7][:, 0:EX], core.bank[6][:, 0:B * EX].rearrange("p (b e) -> p b e", b=B)

        def over_e(t):
            return t[:].unsqueeze(2).broadcast_to([128, B, EX])

        def over_b(t):
            return t[:].unsqueeze(1).broadcast_to([128, B, EX])

        def first_loads(sp):
            sp.dma_start(sim[:], sim_dram.rearrange("(t p) e -> p t e", p=128)).then_inc(inputs_in, 16)
            sp.dma_start(gates[:], gates_dram.unsqueeze(0).broadcast_to([128, EX])).then_inc(inputs_in, 16)

        enter(first_loads)
        with nc.Block() as block:

            @block.sync
            def _(sp):
                sp.wait_ge(w_kept, 2)
                sp.dma_start(weights_dram, w_t[:]).then_inc(stored, 16)
                sp.wait_ge(stored, 16)

            @block.gpsimd
            def _(pool):
                nc.gpsimd.iota(number[:], [[1, EX]], base=0, channel_multiplier=0,
                               allow_small_or_imprecise_dtypes=True).then_inc(number_ready, 1)

            @block.tensor
            def _(pe):
                pe.wait_ge(sim_sq_ready, 1)
                for ct in range(CT):
                    mm = nc.tensor.matmul(sums, core.ones[:], sim_sq[:, ct, :], start=(ct == 0), stop=(ct == CT - 1))
                mm.then_inc(sim_sums, 1)
                pe.wait_ge(step, 3)
                for b in range(B):
                    for ct in range(CT):
                        mm = nc.tensor.matmul(raw[:, b, :], core.xt[:, ct, b * S:(b + 1) * S], sim[:, ct, :],
                                              start=(ct == 0), stop=(ct == CT - 1))
                mm.then_inc(logits_made, 1)
                pe.wait_ge(step, LAST)
                for b in range(B):
                    mm = nc.tensor.transpose(core.bank[4 + b // PER_BANK][0:EX, (b % PER_BANK) * S:(b % PER_BANK + 1) * S],
                                             e_all[:, b, :], core.ident[:])
                mm.then_inc(w_turned, 1)

            @block.scalar
            def _(act):
                for b in range(B):
                    sq = nc.scalar.activation(core.y[:, b, :], core.x[:, b, :], ACT.Square, accum_out=x_sq[:, b:b + 1])
                sq.then_inc(act_step, 1)
                act.wait_ge(act_step, 1)
                nc.scalar.activation(x_len[:], x_sq[:], ACT.Sqrt).then_inc(act_step, 1)
                act.wait_ge(sim_sums, 1)
                nc.scalar.activation(sim_len[:], sums, ACT.Sqrt).then_inc(act_step, 1)
                act.wait_ge(inputs_in, 32)
                nc.scalar.activation(gates[:], gates[:], ACT.Exp, scale=-1.0).then_inc(act_step, 1)
                act.wait_ge(step, SHIFTED)
                nc.scalar.activation(e_all[:], e_all[:], ACT.Exp).then_inc(act_step, 1)
                act.wait_ge(w_turned, 1)
                for half in range(HALVES):
                    nc.scalar.copy(w_t[:, half * BANK:(half + 1) * BANK],
                                   core.bank[4 + half][0:EX, :]).then_inc(w_kept, 1)

            @block.vector
            def _(dve):
                v = nc.vector
                dve.wait_ge(inputs_in, 32)
                v.tensor_tensor(sim_sq[:], sim[:], sim[:], ALU.mult).then_inc(sim_sq_ready, 1)
                dve.wait_ge(act_step, 3)
                v.tensor_scalar(sim_len[:], sim_len[:], 1e-12, None, ALU.max).then_inc(step, 1)
                dve.wait_ge(step, 1)
                v.reciprocal(sim_len[:], sim_len[:]).then_inc(step, 1)
                dve.wait_ge(step, 2)
                v.tensor_tensor(sim[:], sim[:], sim_len[:].unsqueeze(1).broadcast_to([128, CT, EX]),
                                ALU.mult).then_inc(step, 1)
                v.tensor_scalar(x_len[:], x_len[:], 1e-12, None, ALU.max).then_inc(step, 1)
                dve.wait_ge(step, 4)
                v.reciprocal(x_len[:], x_len[:]).then_inc(step, 1)
                dve.wait_ge(act_step, 4)
                v.tensor_scalar(gates[:], gates[:], 1.0, None, ALU.add).then_inc(step, 1)
                dve.wait_ge(step, 6)
                v.reciprocal(gates[:], gates[:]).then_inc(step, 1)
                dve.wait_ge(logits_made, 1)
                dve.wait_ge(step, 7)
                v.tensor_tensor(logits[:], raw, over_e(x_len), ALU.mult).then_inc(step, 1)
                dve.wait_ge(step, 8)
                v.tensor_tensor(logits[:], logits[:], over_b(gates), ALU.subtract).then_inc(step, 1)
                dve.wait_ge(step, 9)
                v.tensor_reduce(top[:], logits[:], AX.X, ALU.max).then_inc(step, 1)
                dve.wait_ge(step, 10)
                v.tensor_tensor(e_all[:], logits[:], over_e(top), ALU.subtract).then_inc(step, 1)
                v.tensor_scalar(is_on[:], logits[:], 0.0, None, ALU.is_gt).then_inc(step, 1)
                v.tensor_scalar(idle[:], top[:], 0.0, None, ALU.is_le).then_inc(step, 1)
                dve.wait_ge(number_ready, 1)
                v.tensor_tensor(pick1[:], logits[:], over_e(top), ALU.is_equal).then_inc(step, 1)
                dve.wait_ge(step, 14)
                v.scalar_tensor_tensor(out=key[:], in0=pick1[:], scalar=-FIRST, in1=over_b(number),
                                       op0=ALU.mult, op1=ALU.add).then_inc(step, 1)
                dve.wait_ge(step, 15)
                v.tensor_reduce(first[:], key[:], AX.X, ALU.min).then_inc(step, 1)
                dve.wait_ge(step, 16)
                v.tensor_tensor(pick1[:], key[:], over_e(first), ALU.is_equal).then_inc(step, 1)
                dve.wait_ge(step, 17)
                v.scalar_tensor_tensor(out=low[:], in0=pick1[:], scalar=-1e30, in1=logits[:],
                                       op0=ALU.mult, op1=ALU.add).then_inc(step, 1)
                dve.wait_ge(step, 18)
                v.tensor_reduce(top2[:], low[:], AX.X, ALU.max).then_inc(step, 1)
                dve.wait_ge(step, 19)
                v.tensor_tensor(pick2[:], low[:], over_e(top2), ALU.is_equal).then_inc(step, 1)
                dve.wait_ge(step, 20)
                v.scalar_tensor_tensor(out=key[:], in0=pick2[:], scalar=-FIRST, in1=over_b(number),
                                       op0=ALU.mult, op1=ALU.add).then_inc(step, 1)
                dve.wait_ge(step, 21)
                v.tensor_reduce(first[:], key[:], AX.X, ALU.min).then_inc(step, 1)
                dve.wait_ge(step, 22)
                v.tensor_tensor(pick2[:], key[:], over_e(first), ALU.is_equal).then_inc(step, 1)
                dve.wait_ge(step, 23)
                v.tensor_tensor(pick1[:], pick1[:], pick2[:], ALU.add).then_inc(step, 1)
                dve.wait_ge(step, 24)
                v.tensor_tensor(pick1[:], pick1[:], over_e(idle), ALU.mult).then_inc(step, 1)
                dve.wait_ge(act_step, 5)
                v.tensor_tensor(e_all[:], e_all[:], is_on[:], ALU.mult).then_inc(step, 1)
                dve.wait_ge(step, 26)
                v.tensor_tensor(e_all[:], e_all[:], pick1[:], ALU.add).then_inc(step, 1)
                dve.wait_ge(step, 27)
                v.tensor_reduce(total[:], e_all[:], AX.X, ALU.add).then_inc(step, 1)
                dve.wait_ge(step, 28)
                v.reciprocal(total[:], total[:]).then_inc(step, 1)
                dve.wait_ge(step, 29)
                v.tensor_tensor(e_all[:], e_all[:], over_e(total), ALU.mult).then_inc(step, 1)


SHIFTED, LAST = 11, 30


def expert_attention(core, w_qkv, w_o, weights_dram):
    nc = core.nc
    EX, H = 16, 128
    SCALE = float(H) ** -0.5
    xt, ident, bank = core.xt, core.ident, core.bank
    acc = bank[0:4]
    with ExitStack() as ctx:
        def sb(name, shape, dt=F32):
            return core.sb(ctx, "c_" + name, shape, dt)

        def sem(name):
            return core.sem(ctx, "c_" + name)

        w_slot = [sb(f"w_qkv{p}", [128, 3, CT, H]) for p in range(2)]
        wo_slot = [sb(f"w_o{p}", [128, C]) for p in range(2)]
        mix = [sb(f"mix{p}", [128, N]) for p in range(2)]
        xw = [sb(f"xw{p}", [128, CT, N]) for p in range(2)]
        aw = [sb(f"aw{p}", [128, N]) for p in range(2)]
        qkv_t = sb("qkv_t", [128, 3, N])
        v = sb("v", [128, B, H])
        masked, probs, probs_t = (sb(n, [128, B, S]) for n in ("masked", "probs", "probs_t"))
        ao_t = sb("ao_t", [128, N])
        top, neg_top, total, inv = (sb(n, [128, B]) for n in ("top", "neg_top", "total", "inv"))
        w_in, mix_in, wo_in, mix2_in = ([sem(f"{n}{p}") for p in range(2)] for n in ("w_in", "mix_in", "wo_in", "mix2_in"))
        xw_ready, mixed, aw_ready, added, closed = (sem(n) for n in ("xw_ready", "mixed", "aw_ready", "added", "closed"))
        kept_act, kept_dve, v_turned, v_kept, s_made, t_made, z_made = (
            sem(n) for n in ("kept_act", "kept_dve", "v_turned", "v_kept", "s_made", "t_made", "z_made"))
        mask_done, top_ready, neg_ready, exp_done, inv_ready, p_ready, z_kept = (
            sem(n) for n in ("mask_done", "top_ready", "neg_ready", "exp_done", "inv_ready", "p_ready", "z_kept"))
        t_kept = sem("t_kept")

        def loads(e, p):
            return 8 * (e - p) + 16

        def cols(half):
            return slice(half * BANK, (half + 1) * BANK)

        def rows(t, half):
            return t[:, half * PER_BANK:(half + 1) * PER_BANK]

        def flat(t, half):
            return rows(t, half).rearrange("p b e -> p (b e)")

        with nc.Block() as block:

            @block.sync
            def _(sp):
                def row(e):
                    return weights_dram[bass.ds(e, 1), :].broadcast_to([128, N])

                def load(e, p):
                    sp.dma_start(mix[p][:], row(e)).then_inc(mix_in[p], 16)
                    sp.dma_start(w_slot[p][:], w_qkv[bass.ds(e, 1)].rearrange("o p (k t e) -> (o p) k t e", k=3, t=CT)
                                 ).then_inc(w_in[p], 16)

                def load_out(e, p):
                    sp.dma_start(aw[p][:], row(e)).then_inc(mix2_in[p], 16)
                    sp.dma_start(wo_slot[p][:], w_o[bass.ds(e, 1)].rearrange("o p c -> (o p) c")).then_inc(wo_in[p], 16)

                for e in range(2):
                    load(e, e)
                with sp.Fori(0, EX // 2 - 1) as i:
                    for p in range(2):
                        sp.wait_ge(mixed, 2 * i + p + 1)
                        load(2 * i + p + 2, p)
                for e in range(2):
                    load_out(e, e)
                with sp.Fori(0, EX // 2 - 1) as i:
                    for p in range(2):
                        sp.wait_ge(added, 2 * i + p + 1)
                        load_out(2 * i + p + 2, p)

            @block.tensor
            def _(pe):
                def clear(banks):
                    for a in banks:
                        nc.tensor.matmul(a[:], core.zero_bf[:, 0:128], core.zero_bf[:], start=True, stop=True,
                                         skip_group_check=True)

                clear(bank[0:6])
                with pe.Fori(0, EX // 2) as i:
                    for p in range(2):
                        e = 2 * i + p
                        pe.wait_ge(w_in[p], loads(e, p))
                        for ct in range(CT):
                            pe.wait_ge(xw_ready, 2 * e + (ct + 1))
                            for kind in range(3):
                                for half in range(HALVES):
                                    mm = nc.tensor.matmul(bank[2 * kind + half][:], w_slot[p][:, kind, ct, :],
                                                          xw[p][:, ct, cols(half)], start=False, stop=True,
                                                          skip_group_check=True)
                        mm.then_inc(mixed, 1)
                pe.wait_ge(kept_act, 3)
                pe.wait_ge(kept_dve, 3)
                for half in range(HALVES):
                    for k in range(PER_BANK):
                        b = half * PER_BANK + k
                        mm = nc.tensor.matmul(bank[half][:, k * S:(k + 1) * S], qkv_t[:, 0, b * S:(b + 1) * S],
                                              qkv_t[:, 1, b * S:(b + 1) * S], start=True, stop=True)
                    mm.then_inc(s_made, 1)
                for half in range(HALVES):
                    for k in range(PER_BANK):
                        b = half * PER_BANK + k
                        mm = nc.tensor.transpose(bank[2 + half][:, k * S:(k + 1) * S], qkv_t[:, 2, b * S:(b + 1) * S],
                                                 ident[:])
                    mm.then_inc(v_turned, 1)
                for half in range(HALVES):
                    pe.wait_ge(p_ready, half + 1)
                    for k in range(PER_BANK):
                        mm = nc.tensor.transpose(bank[4 + half][:, k * S:(k + 1) * S], probs[:, half * PER_BANK + k, :],
                                                 ident[:])
                    mm.then_inc(t_made, 1)
                pe.wait_ge(v_kept, 2)
                for half in range(HALVES):
                    pe.wait_ge(t_kept, half + 1)
                    for k in range(PER_BANK):
                        b = half * PER_BANK + k
                        mm = nc.tensor.matmul(bank[6 + half][:, k * S:(k + 1) * S], v[:, b, :], probs_t[:, b, :],
                                              start=True, stop=True)
                    mm.then_inc(z_made, 1)
                pe.wait_ge(mask_done, 2)
                clear(acc)
                with pe.Fori(0, EX // 2) as i:
                    for p in range(2):
                        e = 2 * i + p
                        pe.wait_ge(wo_in[p], loads(e, p))
                        pe.wait_ge(aw_ready, e + 1)
                        for b in range(B):
                            mm = nc.tensor.matmul(acc[b // 2][:, (b % 2) * C:(b % 2 + 1) * C],
                                                  aw[p][:, b * S:(b + 1) * S], wo_slot[p][:],
                                                  start=False, stop=True, skip_group_check=True)
                        mm.then_inc(added, 1)

            @block.scalar
            def _(act):
                act.wait_ge(mixed, EX)
                for kind in range(3):
                    nc.scalar.copy(qkv_t[:, kind, cols(0)], bank[2 * kind][:]).then_inc(kept_act, 1)
                for half in range(HALVES):
                    act.wait_ge(v_turned, half + 1)
                    nc.scalar.copy(flat(v, half), bank[2 + half][:]).then_inc(v_kept, 1)
                for half in range(HALVES):
                    act.wait_ge(neg_ready, half + 1)
                    for b in range(half * PER_BANK, (half + 1) * PER_BANK):
                        ex = nc.scalar.activation(probs[:, b, :], masked[:, b, :], ACT.Exp, bias=neg_top[:, b:b + 1],
                                                  scale=SCALE, accum_out=total[:, b:b + 1])
                    ex.then_inc(exp_done, 1)
                for half in range(HALVES):
                    act.wait_ge(t_made, half + 1)
                    nc.scalar.copy(flat(probs_t, half), bank[4 + half][:]).then_inc(t_kept, 1)

            @block.vector
            def _(dve):
                with dve.Fori(0, EX // 2) as i:
                    for p in range(2):
                        e = 2 * i + p
                        dve.wait_ge(mix_in[p], loads(e, p))
                        for ct in range(CT):
                            nc.vector.tensor_tensor(xw[p][:, ct, :], xt[:, ct, :], mix[p][:], ALU.mult).then_inc(xw_ready, 1)
                dve.wait_ge(mixed, EX)
                for kind in range(3):
                    nc.vector.tensor_copy(qkv_t[:, kind, cols(1)], bank[2 * kind + 1][:]).then_inc(kept_dve, 1)
                for half in range(HALVES):
                    dve.wait_ge(s_made, half + 1)
                    nc.vector.tensor_tensor(rows(masked, half), bank[half][:].rearrange("p (b k) -> p b k", b=PER_BANK),
                                            core.causal[:].unsqueeze(1).broadcast_to([128, PER_BANK, S]),
                                            ALU.min).then_inc(mask_done, 1)
                    dve.wait_ge(mask_done, half + 1)
                    nc.vector.tensor_reduce(rows(top, half), rows(masked, half), AX.X, ALU.max).then_inc(top_ready, 1)
                    dve.wait_ge(top_ready, half + 1)
                    nc.vector.tensor_scalar(rows(neg_top, half), rows(top, half), -SCALE, None,
                                            ALU.mult).then_inc(neg_ready, 1)
                for half in range(HALVES):
                    dve.wait_ge(exp_done, half + 1)
                    nc.vector.reciprocal(rows(inv, half), rows(total, half)).then_inc(inv_ready, 1)
                    dve.wait_ge(inv_ready, half + 1)
                    nc.vector.tensor_tensor(rows(probs, half), rows(probs, half),
                                            rows(inv, half).unsqueeze(2).broadcast_to([128, PER_BANK, S]),
                                            ALU.mult).then_inc(p_ready, 1)
                for half in range(HALVES):
                    dve.wait_ge(z_made, half + 1)
                    nc.vector.tensor_copy(ao_t[:, cols(half)], bank[6 + half][:]).then_inc(z_kept, 1)
                dve.wait_ge(z_kept, 2)
                with dve.Fori(0, EX // 2) as i:
                    for p in range(2):
                        e = 2 * i + p
                        dve.wait_ge(mix2_in[p], loads(e, p))
                        nc.vector.tensor_tensor(aw[p][:], ao_t[:], aw[p][:], ALU.mult).then_inc(aw_ready, 1)
                dve.wait_ge(added, EX)
                for i, a in enumerate(acc):
                    nc.vector.tensor_tensor(core.y[:, 2 * i:2 * i + 2, :], core.x[:, 2 * i:2 * i + 2, :],
                                            a[:].rearrange("p (b c) -> p b c", b=2), ALU.add).then_inc(closed, 1)


def causal_heads(core, w_qkvo, enter):
    nc = core.nc
    HEADS, E = 16, 128
    SCALE = float(E) ** -0.5
    xt, ident, bank = core.xt, core.ident, core.bank
    acc = bank[0:4]
    with ExitStack() as ctx:
        def sb(name, shape, dt=F32):
            return core.sb(ctx, "d_" + name, shape, dt)

        def sem(name):
            return core.sem(ctx, "d_" + name)

        w_slot = [sb(f"w_qkv{p}", [128, 3, CT, E]) for p in range(2)]
        wo_slot = [sb(f"w_o{p}", [128, C]) for p in range(2)]
        q_t, k_t = sb("q_t", [128, N]), sb("k_t", [128, N])
        v = sb("v", [128, B, E])
        masked = sb("masked", [128, B, S])
        probs = sb("probs", [128, B, S])
        probs_t = sb("probs_t", [128, B, S])
        z_t = sb("z_t", [128, N])
        top, neg_top, total, inv = (sb(n, [128, B]) for n in ("top", "neg_top", "total", "inv"))

        w_in = [sem(f"w_in{p}") for p in range(2)]
        wo_in = [sem(f"wo_in{p}") for p in range(2)]
        q_made, k_made, v_made, s_made, t_made, z_made = (
            sem(n) for n in ("q_made", "k_made", "v_made", "s_made", "t_made", "z_made"))
        q_kept, k_kept, v_kept, exp_done = (sem(n) for n in ("q_kept", "k_kept", "v_kept", "exp_done"))
        mask_done, top_ready, neg_ready, inv_ready, p_ready, z_kept = (
            sem(n) for n in ("mask_done", "top_ready", "neg_ready", "inv_ready", "p_ready", "z_kept"))
        t_kept = [sem(f"t_kept{half}") for half in range(HALVES)]
        head_out = sem("head_out")
        closed = sem("closed")

        def at(h, half):
            return 2 * h + (half + 1)

        def loads(h, p):
            return 8 * (h - p) + 16

        def cols(half):
            return slice(half * BANK, (half + 1) * BANK)

        def batches(half):
            return range(half * PER_BANK, (half + 1) * PER_BANK)

        def heads_of(eng, step):
            with eng.Fori(0, HEADS // 2 - 1) as i:
                step(2 * i, 0, True)
                step(2 * i + 1, 1, True)
            step(HEADS - 2, 0, True)
            step(HEADS - 1, 1, False)

        def load_w(sp, h, p):
            sp.dma_start(w_slot[p][:], w_qkvo[bass.ds(h, 1), :, 0:3 * C]
                         .rearrange("o p (k t e) -> (o p) k t e", k=3, t=CT)).then_inc(w_in[p], 16)

        def load_wo(sp, h, p):
            sp.dma_start(wo_slot[p][:], w_qkvo[bass.ds(h, 1), :, 3 * C:4 * C]
                         .rearrange("o p c -> (o p) c")).then_inc(wo_in[p], 16)

        def first_loads(sp):
            for h in range(2):
                load_w(sp, h, h)
                load_wo(sp, h, h)

        enter(first_loads)
        with nc.Block() as block:

            @block.sync
            def _(sp):
                with sp.Fori(0, HEADS // 2 - 1) as i:
                    for p in range(2):
                        h = 2 * i + p
                        sp.wait_ge(v_made, at(h, 1))
                        load_w(sp, h + 2, p)
                        sp.wait_ge(head_out, h + 1)
                        load_wo(sp, h + 2, p)

            @block.tensor
            def _(pe):
                def project(dst, slot, kind, half):
                    for ct in range(CT):
                        mm = nc.tensor.matmul(dst, w_slot[slot][:, kind, ct, :], xt[:, ct, cols(half)],
                                              start=(ct == 0), stop=(ct == CT - 1))
                    return mm

                def values(dst, slot, half):
                    for k, b in enumerate(batches(half)):
                        for ct in range(CT):
                            mm = nc.tensor.matmul(dst[:, k * E:(k + 1) * E], xt[:, ct, b * S:(b + 1) * S],
                                                  w_slot[slot][:, 2, ct, :], start=(ct == 0), stop=(ct == CT - 1))
                    return mm

                for a in acc:
                    nc.tensor.matmul(a[:], core.zero_bf[:, 0:128], core.zero_bf[:], start=True, stop=True,
                                     skip_group_check=True)
                pe.wait_ge(w_in[0], 16)
                project(bank[6][:], 0, 0, 0).then_inc(q_made, 1)
                project(bank[7][:], 0, 0, 1).then_inc(q_made, 1)
                project(bank[4][:], 0, 1, 0).then_inc(k_made, 1)
                project(bank[5][:], 0, 1, 1).then_inc(k_made, 1)
                pe.wait_ge(q_kept, 2)
                values(bank[6], 0, 0).then_inc(v_made, 1)
                values(bank[7], 0, 1).then_inc(v_made, 1)

                def step(h, p, more):
                    nxt = 1 - p
                    pe.wait_ge(k_kept, at(h, 1))
                    for half, dst in ((0, bank[4]), (1, bank[5])):
                        for k, b in enumerate(batches(half)):
                            mm = nc.tensor.matmul(dst[:, k * S:(k + 1) * S], q_t[:, b * S:(b + 1) * S],
                                                  k_t[:, b * S:(b + 1) * S], start=True, stop=True)
                        mm.then_inc(s_made, 1)
                    if more:
                        pe.wait_ge(w_in[nxt], loads(h + 1, nxt))
                        pe.wait_ge(v_kept, at(h, 0))
                        project(bank[6][:], nxt, 0, 0).then_inc(q_made, 1)
                        pe.wait_ge(v_kept, at(h, 1))
                        project(bank[7][:], nxt, 0, 1).then_inc(q_made, 1)
                        pe.wait_ge(mask_done, at(h, 0))
                        project(bank[4][:], nxt, 1, 0).then_inc(k_made, 1)
                    for half, dst in ((0, bank[5]), (1, bank[6])):
                        pe.wait_ge(p_ready, at(h, half))
                        if half == 0:
                            pe.wait_ge(mask_done, at(h, 1))
                        elif more:
                            pe.wait_ge(q_kept, at(h + 1, 0))
                        else:
                            pe.wait_ge(v_kept, at(h, 0))
                        for k, b in enumerate(batches(half)):
                            mm = nc.tensor.transpose(dst[:, k * S:(k + 1) * S], probs[:, b, :], ident[:])
                        mm.then_inc(t_made, 1)
                    if more:
                        pe.wait_ge(q_kept, at(h + 1, 1))
                        project(bank[7][:], nxt, 1, 1).then_inc(k_made, 1)
                        pe.wait_ge(k_kept, at(h + 1, 0))
                    pe.wait_ge(v_kept, at(h, 1))
                    for half, dst in ((0, bank[4]), (1, bank[5])):
                        pe.wait_ge(t_kept[half], h + 1)
                        for k, b in enumerate(batches(half)):
                            mm = nc.tensor.matmul(dst[:, k * S:(k + 1) * S], v[:, b, :], probs_t[:, b, :],
                                                  start=True, stop=True)
                        mm.then_inc(z_made, 1)
                    if more:
                        pe.wait_ge(t_kept[1], h + 1)
                        values(bank[6], nxt, 0).then_inc(v_made, 1)
                        pe.wait_ge(k_kept, at(h + 1, 1))
                        values(bank[7], nxt, 1).then_inc(v_made, 1)
                    pe.wait_ge(wo_in[p], loads(h, p))
                    for half in range(HALVES):
                        pe.wait_ge(z_kept, at(h, half))
                        for b in batches(half):
                            mm = nc.tensor.matmul(acc[b // 2][:, (b % 2) * C:(b % 2 + 1) * C],
                                                  z_t[:, b * S:(b + 1) * S], wo_slot[p][:],
                                                  start=False, stop=True, skip_group_check=True)
                    mm.then_inc(head_out, 1)

                heads_of(pe, step)

            @block.scalar
            def _(act):
                def keep(dst, src, made, kept, value):
                    act.wait_ge(made, value)
                    nc.scalar.copy(dst, src).then_inc(kept, 1)

                def keep_v(half, h):
                    keep(v[:, half * PER_BANK:(half + 1) * PER_BANK, :].rearrange("p b e -> p (b e)"),
                         bank[6 + half][:], v_made, v_kept, at(h, half))

                keep(q_t[:, cols(0)], bank[6][:], q_made, q_kept, 1)
                keep(q_t[:, cols(1)], bank[7][:], q_made, q_kept, 2)
                keep(k_t[:, cols(0)], bank[4][:], k_made, k_kept, 1)
                keep(k_t[:, cols(1)], bank[5][:], k_made, k_kept, 2)
                keep_v(0, 0)
                keep_v(1, 0)

                def exps(half, h):
                    act.wait_ge(neg_ready, at(h, half))
                    for b in batches(half):
                        ex = nc.scalar.activation(probs[:, b, :], masked[:, b, :], ACT.Exp, bias=neg_top[:, b:b + 1],
                                                  scale=SCALE, accum_out=total[:, b:b + 1])
                    ex.then_inc(exp_done, 1)

                def step(h, p, more):
                    exps(0, h)
                    if more:
                        keep(q_t[:, cols(0)], bank[6][:], q_made, q_kept, at(h + 1, 0))
                    exps(1, h)
                    if more:
                        keep(q_t[:, cols(1)], bank[7][:], q_made, q_kept, at(h + 1, 1))
                        keep(k_t[:, cols(0)], bank[4][:], k_made, k_kept, at(h + 1, 0))
                    act.wait_ge(t_made, at(h, 1))
                    nc.scalar.copy(probs_t[:, PER_BANK:, :].rearrange("p b e -> p (b e)"), bank[6][:]).then_inc(t_kept[1], 1)
                    if more:
                        keep(k_t[:, cols(1)], bank[7][:], k_made, k_kept, at(h + 1, 1))
                        keep_v(0, h + 1)
                        keep_v(1, h + 1)

                heads_of(act, step)

            @block.vector
            def _(dve):
                def rows(t, half):
                    return t[:, half * PER_BANK:(half + 1) * PER_BANK]

                def step(h, p, more):
                    for half in range(HALVES):
                        dve.wait_ge(s_made, at(h, half))
                        nc.vector.tensor_tensor(rows(masked, half), bank[4 + half][:].rearrange("p (b k) -> p b k", b=PER_BANK),
                                                core.causal[:].unsqueeze(1).broadcast_to([128, PER_BANK, S]),
                                                ALU.min).then_inc(mask_done, 1)
                        dve.wait_ge(mask_done, at(h, half))
                        nc.vector.tensor_reduce(rows(top, half), rows(masked, half), AX.X, ALU.max).then_inc(top_ready, 1)
                        dve.wait_ge(top_ready, at(h, half))
                        nc.vector.tensor_scalar(rows(neg_top, half), rows(top, half), -SCALE, None,
                                                ALU.mult).then_inc(neg_ready, 1)
                    for half in range(HALVES):
                        dve.wait_ge(exp_done, at(h, half))
                        nc.vector.reciprocal(rows(inv, half), rows(total, half)).then_inc(inv_ready, 1)
                        dve.wait_ge(inv_ready, at(h, half))
                        nc.vector.tensor_tensor(rows(probs, half), rows(probs, half),
                                                rows(inv, half).unsqueeze(2).broadcast_to([128, PER_BANK, S]),
                                                ALU.mult).then_inc(p_ready, 1)
                    dve.wait_ge(t_made, at(h, 0))
                    nc.vector.tensor_copy(rows(probs_t, 0).rearrange("p b e -> p (b e)"), bank[5][:]).then_inc(t_kept[0], 1)
                    for half in range(HALVES):
                        dve.wait_ge(z_made, at(h, half))
                        nc.vector.tensor_copy(z_t[:, cols(half)], bank[4 + half][:]).then_inc(z_kept, 1)

                heads_of(dve, step)
                dve.wait_ge(head_out, HEADS)
                for i, a in enumerate(acc):
                    nc.vector.tensor_tensor(core.y[:, 2 * i:2 * i + 2, :], core.x[:, 2 * i:2 * i + 2, :],
                                            a[:].rearrange("p (b c) -> p b c", b=2), ALU.add).then_inc(closed, 1)


def quantized_cross_attention(core, ctx_t_dram, wq_dram, bq_dram, wkv_dram, bkv_dram, wp_dram, bp_dram, enter):
    nc = core.nc
    HEADS, D = 16, 16
    PARTS = 3
    HW = 64
    PAIRS = HEADS // 2
    LN255 = 5.541263545158426
    SCALE = 0.25
    UNITS = 2 * B
    psum, bank, xt, ident = core.psum, core.bank, core.xt, core.ident
    with ExitStack() as ctx:
        def sb(name, shape, dt=F32):
            return core.sb(ctx, "e_" + name, shape, dt)

        def sem(name):
            return core.sem(ctx, "e_" + name)

        ctx_t = sb("ctx_t", [128, CT, N])
        wq, wkv, wp = sb("wq", [128, CT, C]), sb("wkv", [128, CT, 2 * C]), sb("wp", [128, CT, C])
        bq, bkv, bp = sb("bq", [128, C]), sb("bkv", [128, 2 * C]), sb("bp", [128, C])
        q, k, v = (sb(n, [128, B, C]) for n in ("q", "k", "v"))
        work = sb("work", [128, B, C])
        q_int = sb("q_int", [128, B, HEADS, HW], BF16)
        k_part = sb("k_part", [128, B, HEADS, HW], BF16)
        v_int = sb("v_int", [128, B, C], BF16)
        q_top, q_scale, q_inv = (sb(n, [128, B * HEADS]) for n in ("q_top", "q_scale", "q_inv"))
        q_neg = sb("q_neg", [128, B * HEADS])
        k_top, k_scale, k_inv = (sb(n, [128, B * HEADS]) for n in ("k_top", "k_scale", "k_inv"))
        v_top, v_all, v_scale, v_inv = (sb(n, [128, C]) for n in ("v_top", "v_all", "v_scale", "v_inv"))
        q_t, k_t = ([sb(f"{n}_t{s}", [128, N], BF16) for s in range(2)] for n in "qk")
        e = [sb(f"e{i}", [128, N]) for i in range(2)]
        e_big = [sb(f"e_big{i}", [128, N], BF16) for i in range(2)]
        e_t = [sb(f"e_t{i}", [128, B, 128], BF16) for i in range(2)]
        top, bias = ([sb(f"{n}{i}", [128, 1]) for i in range(2)] for n in ("top", "bias"))
        total, inv = sb("total", [128, B * HEADS]), sb("inv", [128, B * HEADS])
        att = sb("att", [128, B, C])
        att_t = sb("att_t", [128, CT, N])

        w_in, pads_ready, step, q_made, k_made, kv_read, v_top_ready, v_all_ready = (
            sem(n) for n in ("w_in", "pads_ready", "step", "q_made", "kv_made", "kv_read", "v_top_ready", "v_all_ready"))
        v_inv_ready, v_step, q_first, q_copied, k_first, k_copied = (
            sem(n) for n in ("v_inv_ready", "v_step", "q_first", "q_copied", "k_first", "k_copied"))
        qt_made, kt_made, qt_kept, kt_kept = (sem(n) for n in ("qt_made", "kt_made", "qt_kept", "kt_kept"))
        s_made, top_ready, bias_ready, exp_done, round_ready, t_made, t_kept, inv_ready, pv_made, pv_kept = (
            sem(n) for n in ("s_made", "top_ready", "bias_ready", "exp_done", "round_ready", "t_made", "t_kept",
                             "inv_ready", "pv_made", "pv_kept"))
        att_ready, att_turned, att_kept_a, att_kept_d, out_made, y_part, closed = (
            sem(n) for n in ("att_ready", "att_turned", "att_kept_a", "att_kept_d", "out_made", "y_part", "closed"))

        TURN_Q, TURN_K = 4, 6

        def pairs_of(eng, pair):
            pair(0, 0, True, True)
            with eng.Fori(0, PAIRS // 2 - 1) as i:
                pair(2 * i + 1, 1, False, True)
                pair(2 * i + 2, 0, False, True)
            pair(PAIRS - 1, 1, False, False)

        def groups(t):
            return t[:].rearrange("p b (h d) -> p (b h) d", d=D)

        def over_d(t):
            return t[:].unsqueeze(2).broadcast_to([128, B * HEADS, D])

        def part(t, j):
            return t[:].rearrange("p b h w -> p (b h) w")[:, :, j * D:(j + 1) * D]

        def first_loads(sp):
            for dst, src in ((ctx_t, ctx_t_dram), (wq, wq_dram), (wkv, wkv_dram), (wp, wp_dram)):
                sp.dma_start(dst[:], src.rearrange("(t p) n -> p t n", p=128)).then_inc(w_in, 16)
            for dst, src, n in ((bq, bq_dram, C), (bkv, bkv_dram, 2 * C), (bp, bp_dram, C)):
                sp.dma_start(dst[:], src.unsqueeze(0).broadcast_to([128, n])).then_inc(w_in, 16)

        enter(first_loads)
        with nc.Block() as block:

            @block.gpsimd
            def _(pool):
                nc.gpsimd.memset(q_int[:, :, :, PARTS * D:], 0.0)
                nc.gpsimd.memset(k_part[:, :, :, PARTS * D:], 0.0).then_inc(pads_ready, 1)
                pool.wait_ge(v_top_ready, 1)
                nc.gpsimd.partition_all_reduce(v_all[:], v_top[:], 128,
                                               bass.bass_isa.ReduceOp.max).then_inc(v_all_ready, 1)
                pool.wait_ge(v_inv_ready, 1)
                nc.gpsimd.tensor_tensor(v[:], v[:], v_inv[:].unsqueeze(1).broadcast_to([128, B, C]), ALU.mult).then_inc(v_step, 1)
                pool.wait_ge(v_step, 1)
                nc.gpsimd.tensor_scalar(v[:], v[:], ROUND, -ROUND, ALU.add, ALU.add).then_inc(v_step, 1)
                pool.wait_ge(v_step, 2)
                nc.gpsimd.tensor_scalar(v_int[:], v[:], 127.0, -127.0, ALU.min, ALU.max).then_inc(v_step, 1)

            @block.tensor
            def _(pe):
                pe.wait_ge(w_in, 16 * 7)
                for b in range(B):
                    if b >= 4:
                        pe.wait_ge(kv_read, b - 3)
                    for ct in range(CT):
                        mm = nc.tensor.matmul(bank[4 + b % 4], ctx_t[:, ct, b * S:(b + 1) * S], wkv[:, ct, :],
                                              start=(ct == 0), stop=(ct == CT - 1))
                    mm.then_inc(k_made, 1)
                for i in range(4):
                    for j in range(2):
                        b = 2 * i + j
                        for ct in range(CT):
                            mm = nc.tensor.matmul(bank[i][:, j * C:(j + 1) * C], xt[:, ct, b * S:(b + 1) * S],
                                                  wq[:, ct, :], start=(ct == 0), stop=(ct == CT - 1))
                    mm.then_inc(q_made, 1)

                def turn(src, dst, hp, made):
                    for b in range(B):
                        mm = nc.tensor.transpose(dst[:, b * S:(b + 1) * S],
                                                 src[:, b].rearrange("p h w -> p (h w)")[:, bass.ds(hp * 2 * HW, 2 * HW)],
                                                 core.ident_bf[:])
                    mm.then_inc(made, 1)

                def turn_k(hp):
                    pe.wait_ge(qt_kept, hp + 1)
                    turn(k_part, core.bank_bf(7), hp, kt_made)

                def scores(hp, s, u, first=False):
                    p, j = u // B, u % B
                    if u == 0:
                        pe.wait_ge(kt_kept, hp + 1)
                    if not first:
                        pe.wait_ge(exp_done, UNITS * hp + u - 1)
                    for half in range(HALVES):
                        mm = nc.tensor.matmul(bank[2 * (u % 2) + half], q_t[s][HW * p:HW * p + PARTS * D, j * S:(j + 1) * S],
                                              k_t[s][HW * p:HW * p + PARTS * D, half * BANK:(half + 1) * BANK],
                                              start=True, stop=True)
                    mm.then_inc(s_made, 1)

                def turn_probs(hp, u, first=False):
                    pe.wait_ge(round_ready, UNITS * hp + (u + 1))
                    if not first:
                        pe.wait_ge(t_kept, UNITS * hp + u - 1)
                    for m in range(B):
                        mm = nc.tensor.transpose(core.bank_bf(4 + u % 2)[:, m * 128:(m + 1) * 128],
                                                 e_big[u % 2][:, m * 128:(m + 1) * 128], core.ident_bf[:])
                    mm.then_inc(t_made, 1)

                def mix(hp, u, first=False, more=True):
                    p, j = u // B, u % B
                    pe.wait_ge(t_kept, UNITS * hp + (u + 1))
                    if j == 0 and p == 0 and not first:
                        pe.wait_ge(pv_kept, 2 * hp - 1)
                    if j == 0 and p == 1:
                        pe.wait_ge(kt_kept, hp + 2 if more else hp + 1)
                        if not more:
                            pe.wait_ge(pv_kept, 2 * hp)
                    for m in range(B):
                        mm = nc.tensor.matmul(bank[6 + p][:, j * D:(j + 1) * D], e_t[u % 2][:, m, :],
                                              v_int[:, m, bass.ds(hp * 2 * D + p * D, D)], start=(m == 0), stop=(m == B - 1))
                    if j == B - 1:
                        mm.then_inc(pv_made, 1)

                def pair(hp, s, first, more):
                    for u in range(UNITS):
                        if more and u == TURN_Q:
                            pe.wait_ge(kt_kept, hp + 1)
                            if not first:
                                pe.wait_ge(pv_kept, 2 * hp)
                            turn(q_int, core.bank_bf(7), hp + 1, qt_made)
                        if more and u == TURN_K:
                            turn_k(hp + 1)
                        if u + 2 < UNITS:
                            scores(hp, s, u + 2)
                        elif more:
                            scores(hp + 1, 1 - s, u + 2 - UNITS)
                        turn_probs(hp, u, first and u < 2)
                        if u > 0:
                            mix(hp, u - 1, first, more)
                        elif not first:
                            mix(hp - 1, UNITS - 1)

                pe.wait_ge(step, PREP)
                pe.wait_ge(q_copied, PARTS - 1)
                turn(q_int, core.bank_bf(7), 0, qt_made)
                turn_k(0)
                scores(0, 0, 0, True)
                scores(0, 0, 1, True)
                pe.wait_ge(v_step, 3)
                pairs_of(pe, pair)
                mix(PAIRS - 1, UNITS - 1)

                for half in range(HALVES):
                    pe.wait_ge(att_ready, 2)
                    for ct in range(CT):
                        for i in range(PER_BANK):
                            b = half * PER_BANK + i
                            mm = nc.tensor.transpose(bank[CT * half + ct][:, i * S:(i + 1) * S],
                                                     att[:, b, ct * 128:(ct + 1) * 128], ident[:])
                    mm.then_inc(att_turned, 1)
                pe.wait_ge(att_kept_a, HALVES)
                pe.wait_ge(att_kept_d, HALVES)
                for i in range(4):
                    for j in range(2):
                        b = 2 * i + j
                        for ct in range(CT):
                            mm = nc.tensor.matmul(bank[4 + i][:, j * C:(j + 1) * C], att_t[:, ct, b * S:(b + 1) * S],
                                                  wp[:, ct, :], start=(ct == 0), stop=(ct == CT - 1))
                    mm.then_inc(out_made, 1)

            @block.scalar
            def _(act):
                def keep_q(hp, s):
                    act.wait_ge(qt_made, hp + 1)
                    nc.scalar.copy(q_t[s][:], core.bank_bf(7)).then_inc(qt_kept, 1)

                def keep_k(hp, s):
                    act.wait_ge(kt_made, hp + 1)
                    nc.scalar.copy(k_t[s][:], core.bank_bf(7)).then_inc(kt_kept, 1)

                def exps(hp, u):
                    p, j = u // B, u % B
                    act.wait_ge(bias_ready, UNITS * hp + (u + 1))
                    act.wait_ge(w_in, 16)
                    nc.scalar.activation(e[u % 2][:], psum[:, 2 * (u % 2) * BANK:(2 * (u % 2) + 2) * BANK], ACT.Exp,
                                         bias=bias[u % 2][:],
                                         scale=q_scale[:, bass.ds(hp * 2 + (p + j * HEADS), 1)],
                                         accum_out=total[:, bass.ds(hp * 2 + (p + j * HEADS), 1)]).then_inc(exp_done, 1)

                def keep_probs(hp, u):
                    act.wait_ge(t_made, UNITS * hp + (u + 1))
                    nc.scalar.copy(e_t[u % 2][:].rearrange("p m n -> p (m n)"), core.bank_bf(4 + u % 2)).then_inc(t_kept, 1)

                def pair(hp, s, first, more):
                    for u in range(UNITS):
                        if u + 1 < UNITS:
                            exps(hp, u + 1)
                        elif more:
                            exps(hp + 1, 0)
                        keep_probs(hp, u)
                        if more and u == TURN_Q:
                            keep_q(hp + 1, 1 - s)
                        if more and u == TURN_K:
                            keep_k(hp + 1, 1 - s)

                act.wait_ge(k_first, 1)
                nc.scalar.copy(part(k_part, 0), groups(k)).then_inc(k_copied, 1)
                act.wait_ge(k_first, 2)
                nc.scalar.copy(part(k_part, 1), groups(k)).then_inc(k_copied, 1)
                act.wait_ge(q_first, 1)
                for j in range(1, PARTS):
                    nc.scalar.copy(part(q_int, j), part(q_int, 0)).then_inc(q_copied, 1)
                keep_q(0, 0)
                keep_k(0, 0)
                exps(0, 0)
                pairs_of(act, pair)
                for half in range(HALVES):
                    act.wait_ge(att_turned, half + 1)
                    nc.scalar.copy(att_t[:, 0, half * BANK:(half + 1) * BANK], bank[CT * half]).then_inc(att_kept_a, 1)

            @block.vector
            def _(dve):
                vec = nc.vector
                n = [0]

                def done(ins):
                    ins.then_inc(step, 1)
                    n[0] += 1
                    dve.wait_ge(step, n[0])

                dve.wait_ge(w_in, 16 * 7)
                dve.wait_ge(pads_ready, 1)
                for b in range(B):
                    dve.wait_ge(k_made, b + 1)
                    vec.tensor_tensor(k[:, b, :], bank[4 + b % 4][:, 0:C], bkv[:, 0:C], ALU.add)
                    ins = vec.tensor_tensor(v[:, b, :], bank[4 + b % 4][:, C:2 * C], bkv[:, C:2 * C],
                                            ALU.add)
                    ins.then_inc(kv_read, 1)
                dve.wait_ge(kv_read, B)
                vec.tensor_reduce(v_top[:], v[:].rearrange("p b c -> p c b"), AX.X, ALU.max,
                                  apply_absolute_value=True).then_inc(v_top_ready, 1)
                done(vec.tensor_reduce(k_top[:], groups(k), AX.X, ALU.max, apply_absolute_value=True))
                for i in range(4):
                    dve.wait_ge(q_made, i + 1)
                    ins = vec.tensor_tensor(q[:, 2 * i:2 * i + 2, :], bank[i].rearrange("p (j c) -> p j c", j=2),
                                            bq[:].unsqueeze(1).broadcast_to([128, 2, C]), ALU.add)
                done(ins)

                def scales(top_, scale, inverse, factor):
                    done(vec.tensor_scalar(scale[:], top_[:], factor / 127.0, 1e-8, ALU.mult, ALU.max))
                    done(vec.reciprocal(inverse[:], scale[:]))
                    if factor != 1.0:
                        done(vec.tensor_scalar(inverse[:], inverse[:], factor, None, ALU.mult))

                done(vec.tensor_reduce(q_top[:], groups(q), AX.X, ALU.max, apply_absolute_value=True))
                scales(q_top, q_scale, q_inv, SCALE)
                done(vec.tensor_scalar(q_neg[:], q_scale[:], -1.0, None, ALU.mult))
                dve.wait_ge(v_all_ready, 1)
                done(vec.tensor_scalar(v_scale[:], v_all[:], 1.0 / 127.0, 1e-8, ALU.mult, ALU.max))
                vec.reciprocal(v_inv[:], v_scale[:]).then_inc(v_inv_ready, 1)
                scales(k_top, k_scale, k_inv, 1.0)
                done(vec.tensor_tensor(groups(k), groups(k), over_d(k_inv), ALU.mult))
                done(vec.tensor_scalar(k[:], k[:], ROUND, -ROUND, ALU.add, ALU.add))
                done(vec.tensor_scalar(k[:], k[:], 127.0, -127.0, ALU.min, ALU.max))
                vec.tensor_tensor(groups(k), groups(k), over_d(k_scale), ALU.mult).then_inc(k_first, 1)
                done(vec.tensor_tensor(groups(q), groups(q), over_d(q_inv), ALU.mult))
                dve.wait_ge(k_copied, 1)
                vec.tensor_tensor(groups(k), groups(k), part(k_part, 0), ALU.subtract).then_inc(k_first, 1)
                done(vec.tensor_scalar(q[:], q[:], ROUND, -ROUND, ALU.add, ALU.add))
                vec.tensor_scalar(part(q_int, 0), groups(q), 127.0, -127.0, ALU.min, ALU.max).then_inc(q_first, 1)
                dve.wait_ge(k_copied, 2)
                done(vec.tensor_tensor(part(k_part, 2), groups(k), part(k_part, 1), ALU.subtract))
                assert n[0] == PREP, n[0]

                def maxima(hp, u):
                    p, j = u // B, u % B
                    dve.wait_ge(s_made, UNITS * hp + (u + 1))
                    vec.tensor_reduce(top[u % 2][:], psum[:, 2 * (u % 2) * BANK:(2 * (u % 2) + 2) * BANK], AX.X,
                                      ALU.max).then_inc(top_ready, 1)
                    dve.wait_ge(top_ready, UNITS * hp + (u + 1))
                    vec.tensor_scalar(bias[u % 2][:], top[u % 2][:], q_neg[:, bass.ds(hp * 2 + (p + j * HEADS), 1)],
                                      LN255, ALU.mult, ALU.add).then_inc(bias_ready, 1)

                def rounds(hp, u):
                    dve.wait_ge(exp_done, UNITS * hp + (u + 1))
                    vec.tensor_scalar(e_big[u % 2][:], e[u % 2][:], ROUND, -ROUND, ALU.add, ALU.add).then_inc(round_ready, 1)

                def keep_mix(hp, p):
                    dve.wait_ge(pv_made, 2 * hp + (p + 1))
                    vec.tensor_copy(att[:, :, bass.ds(hp * 2 * D + p * D, D)],
                                    bank[6 + p][:, 0:B * D].rearrange("p (j d) -> p j d", j=B)).then_inc(pv_kept, 1)

                def pair(hp, s, first, more):
                    for u in range(UNITS):
                        rounds(hp, u)
                        if u + 2 < UNITS:
                            maxima(hp, u + 2)
                        elif more:
                            maxima(hp + 1, u + 2 - UNITS)
                        if u == B + 2:
                            keep_mix(hp, 0)
                        if u == 2 and not first:
                            keep_mix(hp - 1, 1)

                maxima(0, 0)
                maxima(0, 1)
                pairs_of(dve, pair)
                keep_mix(PAIRS - 1, 1)
                vec.reciprocal(inv[:], total[:]).then_inc(inv_ready, 1)
                dve.wait_ge(inv_ready, 1)
                dve.wait_ge(pv_kept, 2 * PAIRS)
                vec.tensor_tensor(groups(att), groups(att), over_d(inv), ALU.mult).then_inc(att_ready, 1)
                dve.wait_ge(att_ready, 1)
                vec.tensor_tensor(att[:], att[:], v_scale[:].unsqueeze(1).broadcast_to([128, B, C]),
                                  ALU.mult).then_inc(att_ready, 1)
                for half in range(HALVES):
                    dve.wait_ge(att_turned, half + 1)
                    vec.tensor_copy(att_t[:, 1, half * BANK:(half + 1) * BANK], bank[CT * half + 1]).then_inc(att_kept_d, 1)
                vec.tensor_tensor(work[:], core.x[:], bp[:].unsqueeze(1).broadcast_to([128, B, C]), ALU.add).then_inc(y_part, 1)
                dve.wait_ge(y_part, 1)
                for i in range(4):
                    dve.wait_ge(out_made, i + 1)
                    vec.tensor_tensor(core.y[:, 2 * i:2 * i + 2, :], work[:, 2 * i:2 * i + 2, :],
                                      bank[4 + i].rearrange("p (j c) -> p j c", j=2), ALU.add).then_inc(closed, 1)
                    dve.wait_ge(closed, i + 1)
                    core.batch_stats(2 * i)
                    core.batch_stats(2 * i + 1)


PREP = 16


def ternary_ffn(core, w_gate_up, w_down, norm_weight, enter):
    nc = core.nc
    F, FP = 704, 88
    FT = F // FP
    psum, bank = core.psum, core.bank
    with ExitStack() as ctx:
        def sb(name, shape, dt=F32):
            return core.sb(ctx, "f_" + name, shape, dt)

        def sem(name):
            return core.sem(ctx, "f_" + name)

        wgu, wgu_q = sb("wgu", [128, CT * 2 * F]), sb("wgu_q", [128, CT * 2 * F], BF16)
        wd, wd_q = sb("wd", [FP, FT * C]), sb("wd_q", [FP, FT * C], BF16)
        wgu_qv = wgu_q[:].rearrange("p (t f) -> p t f", t=CT)
        wd_qv = wd_q[:].rearrange("p (t c) -> p t c", t=FT)
        nw = sb("nw", [128, C])
        w_sum, w_mean, w_scale = sb("w_sum", [128, 2]), sb("w_mean", [128, 2]), sb("w_scale", [128, 2])
        sq, var, rs, t0 = (sb(n, [128, B]) for n in ("sq", "var", "rs", "t0"))
        amax, a_scale, alpha, alpha3 = (sb(n, [128, B]) for n in ("amax", "a_scale", "alpha", "alpha3"))
        xn, xr, xq = sb("xn", [128, B, C]), sb("xr", [128, B, C]), sb("xq", [128, B, C], BF16)
        xq_t = sb("xq_t", [128, CT, N], BF16)
        g1, g2, h, hr = ([sb(f"{n}{p}", [128, F]) for p in range(2)] for n in ("g1", "g2", "h", "hr"))
        hq = [sb(f"hq{p}", [128, F], BF16) for p in range(2)]
        hq_t = [sb(f"hq_t{p}", [FP, FT, 128], BF16) for p in range(2)]
        hm, hc, hi, hs, down_scale = ([sb(f"{n}{p}", [128, 1]) for p in range(2)] for n in ("hm", "hc", "hi", "hs", "down_scale"))
        mean2 = sb("mean2", [128, 1])
        w_in, wd_in, nw_in, sums_ready, sums_made, x_sq_done, x_sd_done = (
            sem(n) for n in ("w_in", "wd_in", "nw_in", "sums_ready", "sums_made", "x_sq_done", "x_sd_done"))
        step, xn_ready, xr_ready, xq_ready, xq_turned, xq_kept, wq_step = (
            sem(n) for n in ("step", "xn_ready", "xr_ready", "xq_ready", "xq_turned", "xq_kept", "wq_step"))
        gu_made, g1_done, g2_done, h_step, hq_ready, hq_turned, hq_kept, down_made, y_ready = (
            sem(n) for n in ("gu_made", "g1_done", "g2_done", "h_step", "hq_ready", "hq_turned", "hq_kept",
                             "down_made", "y_ready"))
        g_made, wq_ready = sem("g_made"), sem("wq_ready")
        UP = (2, 4)
        H_STEPS = 7

        def batches(eng, one):
            one(0, 0, True, False)
            one(1, 1, False, False)
            with eng.Fori(1, B // 2 - 1) as i:
                one(2 * i, 0, False, False)
                one(2 * i + 1, 1, False, False)
            one(B - 2, 0, False, False)
            one(B - 1, 1, False, True)

        def first_loads(sp):
            sp.dma_start(wgu[:], w_gate_up).then_inc(w_in, 16)
            sp.dma_start(wd[:], w_down).then_inc(wd_in, 16)
            sp.dma_start(nw[:], norm_weight.unsqueeze(0).broadcast_to([128, C])).then_inc(nw_in, 16)

        enter(first_loads)
        with nc.Block() as block:

            @block.tensor
            def _(pe):
                pe.wait_ge(sums_ready, 2)
                nc.tensor.matmul(bank[7][:, 0:1], core.ones[:], w_sum[:, 0:1], start=True, stop=True)
                nc.tensor.matmul(bank[7][:, 1:2], core.ones[0:FP, :], w_sum[0:FP, 1:2], start=True,
                                 stop=True).then_inc(sums_made, 1)
                pe.wait_ge(xq_ready, 1)
                for ct in range(CT):
                    for b in range(B):
                        mm = nc.tensor.transpose(core.bank_bf(5 + ct)[:, b * S:(b + 1) * S],
                                                 xq[:, b, ct * 128:(ct + 1) * 128], core.ident_bf[:])
                    mm.then_inc(xq_turned, 1)
                pe.wait_ge(xq_kept, CT)
                pe.wait_ge(wq_ready, 1)

                def gate_up(b, p, first=False):
                    for part, base in ((0, 0), (1, UP[p])):
                        if part == 0 and not first:
                            pe.wait_ge(g1_done, b)
                        if part == 1 and not (isinstance(b, int) and b < 2):
                            pe.wait_ge(h_step, H_STEPS * (b - 2) + 1)
                        for lo, hi_ in ((0, BANK), (BANK, F)):
                            for ct in range(CT):
                                mm = nc.tensor.matmul(psum[:, base * BANK + lo:base * BANK + hi_],
                                                      xq_t[:, ct, bass.ds(b * S, S)],
                                                      wgu_qv[:, ct, part * F + lo:part * F + hi_],
                                                      start=(ct == 0), stop=(ct == CT - 1))
                        mm.then_inc(g_made if part == 0 else gu_made, 1)

                def down(b, p, first, last):
                    pe.wait_ge(hq_ready, b + 1)
                    if not first:
                        pe.wait_ge(hq_kept, b)
                    for t in range(FT):
                        mm = nc.tensor.transpose(core.bank_bf(6)[0:FP, t * 128:(t + 1) * 128],
                                                 hq[p][:, t * FP:(t + 1) * FP], core.ident_bf[:])
                    mm.then_inc(hq_turned, 1)
                    pe.wait_ge(hq_kept, b + 1)
                    if not first:
                        pe.wait_ge(y_ready, b)
                    for t in range(FT):
                        mm = nc.tensor.matmul(bank[7][:, 0:C], hq_t[p][:, t, :], wd_qv[:, t, :],
                                              start=(t == 0), stop=(t == FT - 1))
                    mm.then_inc(down_made, 1)

                def one(b, p, first, last):
                    if not last:
                        gate_up(b + 1, 1 - p)
                    down(b, p, first, last)

                gate_up(0, 0, True)
                pe.wait_ge(wq_ready, 2)
                batches(pe, one)

            @block.scalar
            def _(act):
                for b in range(B):
                    ins = nc.scalar.activation(core.y[:, b, :], core.x[:, b, :], ACT.Square, accum_out=sq[:, b:b + 1])
                ins.then_inc(x_sq_done, 1)
                act.wait_ge(step, 1)
                nc.scalar.activation(rs[:], var[:], ACT.Sqrt).then_inc(x_sd_done, 1)
                act.wait_ge(w_in, 16)
                nc.scalar.activation(wgu_q[:], wgu[:], ACT.Abs, accum_out=w_sum[:, 0:1]).then_inc(sums_ready, 1)
                act.wait_ge(wd_in, 16)
                nc.scalar.activation(wd_q[:], wd[:], ACT.Abs, accum_out=w_sum[0:FP, 1:2]).then_inc(sums_ready, 1)
                for ct in range(CT):
                    act.wait_ge(xq_turned, ct + 1)
                    nc.scalar.copy(xq_t[:, ct, :], core.bank_bf(5 + ct)).then_inc(xq_kept, 1)

                def squares(b, p):
                    act.wait_ge(g_made, b + 1)
                    if not (isinstance(b, int) and b < 2):
                        act.wait_ge(h_step, H_STEPS * (b - 2) + 1)
                    nc.scalar.activation(g1[p][:], psum[:, 0:F], ACT.Relu).then_inc(g1_done, 1)
                    act.wait_ge(g1_done, b + 1)
                    nc.scalar.activation(g2[p][:], g1[p][:], ACT.Square).then_inc(g2_done, 1)

                def one(b, p, first, last):
                    if not last:
                        squares(b + 1, 1 - p)
                    act.wait_ge(hq_turned, b + 1)
                    if not (isinstance(b, int) and b < 2):
                        act.wait_ge(down_made, b - 1)
                    nc.scalar.copy(hq_t[p][:].rearrange("p t n -> p (t n)"), core.bank_bf(6)[0:FP, :]).then_inc(hq_kept, 1)

                act.wait_ge(wq_step, 4)
                nc.scalar.activation(wgu_q[:], wgu[:], ACT.Copy, bias=-ROUND).then_inc(wq_ready, 1)
                act.wait_ge(wq_step, 6)
                nc.scalar.activation(wd_q[:], wd[:], ACT.Copy, bias=-ROUND).then_inc(wq_ready, 1)
                squares(0, 0)
                batches(act, one)

            @block.vector
            def _(dve):
                v = nc.vector
                dve.wait_ge(x_sq_done, 1)
                v.tensor_scalar(var[:], sq[:], 1.0 / C, 1e-5, ALU.mult, ALU.add).then_inc(step, 1)
                dve.wait_ge(x_sd_done, 1)
                v.reciprocal(rs[:], rs[:]).then_inc(step, 1)
                dve.wait_ge(step, 2)
                v.tensor_tensor(t0[:], rs[:], rs[:], ALU.mult).then_inc(step, 1)
                dve.wait_ge(step, 3)
                v.tensor_tensor(t0[:], t0[:], var[:], ALU.mult).then_inc(step, 1)
                dve.wait_ge(step, 4)
                v.tensor_scalar(t0[:], t0[:], -0.5, 1.5, ALU.mult, ALU.add).then_inc(step, 1)
                dve.wait_ge(step, 5)
                v.tensor_tensor(rs[:], rs[:], t0[:], ALU.mult).then_inc(step, 1)
                dve.wait_ge(step, 6)
                dve.wait_ge(nw_in, 16)
                for b in range(B):
                    v.scalar_tensor_tensor(out=xn[:, b, :], in0=core.x[:, b, :], scalar=rs[:, b:b + 1], in1=nw[:],
                                           op0=ALU.mult, op1=ALU.mult).then_inc(xn_ready, 1)
                dve.wait_ge(xn_ready, B)
                v.tensor_reduce(amax[:], xn[:], AX.X, ALU.max, apply_absolute_value=True).then_inc(step, 1)
                dve.wait_ge(sums_made, 1)
                v.tensor_scalar(w_mean[:, 0:1], bank[7][:, 0:1], 1.0 / (2 * F * C), 1e-5, ALU.mult,
                                ALU.max).then_inc(wq_step, 1)
                v.tensor_scalar(w_mean[:, 1:2], bank[7][:, 1:2], 1.0 / (F * C), 1e-5, ALU.mult,
                                ALU.max).then_inc(wq_step, 1)
                dve.wait_ge(step, 7)
                v.tensor_scalar(amax[:], amax[:], 1e-5, None, ALU.max).then_inc(step, 1)
                dve.wait_ge(step, 8)
                v.reciprocal(a_scale[:], amax[:]).then_inc(step, 1)
                dve.wait_ge(step, 9)
                v.tensor_scalar(a_scale[:], a_scale[:], 127.0, None, ALU.mult).then_inc(step, 1)
                dve.wait_ge(step, 10)
                for b in range(B):
                    v.tensor_scalar(xr[:, b, :], xn[:, b, :], a_scale[:, b:b + 1], ROUND, ALU.mult,
                                    ALU.add).then_inc(xr_ready, 1)
                dve.wait_ge(xr_ready, B)
                v.tensor_scalar(xq[:], xr[:], -ROUND, None, ALU.add).then_inc(xq_ready, 1)
                dve.wait_ge(wq_step, 2)
                v.reciprocal(w_scale[:], w_mean[:]).then_inc(step, 1)
                dve.wait_ge(step, 11)
                v.tensor_scalar(mean2[:], w_mean[:, 1:2], 1.0 / 127.0, None, ALU.mult).then_inc(step, 1)
                v.tensor_scalar(alpha[:], amax[:], w_mean[:, 0:1], 1.0 / 127.0, ALU.mult, ALU.mult).then_inc(step, 1)
                dve.wait_ge(step, 13)
                v.tensor_tensor(alpha3[:], alpha[:], alpha[:], ALU.mult).then_inc(step, 1)
                v.tensor_scalar(wgu[:], wgu[:], w_scale[:, 0:1], 1.0, ALU.mult, ALU.min).then_inc(wq_step, 1)
                dve.wait_ge(wq_step, 3)
                v.tensor_scalar(wgu[:], wgu[:], -1.0, ROUND, ALU.max, ALU.add).then_inc(wq_step, 1)
                dve.wait_ge(wq_step, 4)
                v.tensor_scalar(wd[:], wd[:], w_scale[0:FP, 1:2], 1.0, ALU.mult, ALU.min).then_inc(wq_step, 1)
                dve.wait_ge(wq_step, 5)
                v.tensor_scalar(wd[:], wd[:], -1.0, ROUND, ALU.max, ALU.add).then_inc(wq_step, 1)
                dve.wait_ge(step, 14)
                v.tensor_tensor(alpha3[:], alpha3[:], alpha[:], ALU.mult).then_inc(step, 1)
                dve.wait_ge(step, 15)

                def hidden(b, p):
                    def link(i):
                        dve.wait_ge(h_step, H_STEPS * b + i)

                    dve.wait_ge(g2_done, b + 1)
                    dve.wait_ge(gu_made, b + 1)
                    v.tensor_tensor(h[p][:], g2[p][:], psum[:, UP[p] * BANK:UP[p] * BANK + F], ALU.mult).then_inc(h_step, 1)
                    link(1)
                    v.tensor_reduce(hm[p][:], h[p][:], AX.X, ALU.max, apply_absolute_value=True).then_inc(h_step, 1)
                    link(2)
                    if not (isinstance(b, int) and b < 2):
                        dve.wait_ge(y_ready, b - 1)
                    v.tensor_scalar(hc[p][:], hm[p][:], alpha3[:, bass.ds(b, 1)], 1e-5, ALU.mult, ALU.max).then_inc(h_step, 1)
                    link(3)
                    v.reciprocal(hi[p][:], hc[p][:]).then_inc(h_step, 1)
                    link(4)
                    v.tensor_scalar(hs[p][:], hi[p][:], 127.0, alpha3[:, bass.ds(b, 1)], ALU.mult, ALU.mult).then_inc(h_step, 1)
                    link(5)
                    v.tensor_scalar(hr[p][:], h[p][:], hs[p][:], ROUND, ALU.mult, ALU.add).then_inc(h_step, 1)
                    link(6)
                    if not (isinstance(b, int) and b < 2):
                        dve.wait_ge(hq_turned, b - 1)
                    v.tensor_scalar(hq[p][:], hr[p][:], -ROUND, None, ALU.add).then_inc(hq_ready, 1)
                    v.tensor_scalar(down_scale[p][:], hc[p][:], mean2[:], None, ALU.mult).then_inc(h_step, 1)

                def finish(b, p):
                    dve.wait_ge(down_made, b + 1)
                    dve.wait_ge(h_step, H_STEPS * (b + 1))
                    v.scalar_tensor_tensor(out=core.y[:, bass.ds(b, 1), :].rearrange("p o c -> p (o c)"),
                                           in0=bank[7][:, 0:C], scalar=down_scale[p][:],
                                           in1=core.x[:, bass.ds(b, 1), :].rearrange("p o c -> p (o c)"),
                                           op0=ALU.mult, op1=ALU.add).then_inc(y_ready, 1)

                def one(b, p, first, last):
                    if not last:
                        hidden(b + 1, 1 - p)
                    else:
                        dve.wait_ge(y_ready, b)
                        for done in range(b):
                            core.batch_stats(done)
                    finish(b, p)
                    if last:
                        dve.wait_ge(y_ready, b + 1)
                        core.batch_stats(b)

                hidden(0, 0)
                batches(dve, one)


def decoder(nc, d, out):
    expert_weights = nc.dram_tensor("expert_weights", [16, N], F32).ap()
    with ExitStack() as ctx:
        core = Core(nc, ctx)
        make_constants(core, d["x"])

        def entered_by(tag, **how):
            return lambda loads: norm_and_turn(core, tag, loads=loads, **how)

        gated_delta(core, d["delta_heads"], d["delta_small"], d["delta_bias"], d["delta_rms"], d["delta_masks"],
                    entered_by("n0", normalize=False))
        core.end_stage()
        rotary_cross_attention(core, d["ctx"], d["rotary_w"], d["rotary_cols"], d["rotary_bv"], d["rotary_enc"],
                               d["rotary_sign"], entered_by("n1", turn=False, sums=False))
        core.end_stage()
        route_tokens(core, d["sim"], d["gates"], expert_weights, entered_by("n2", sums=False))
        expert_attention(core, d["expert_qkv"], d["expert_o"], expert_weights)
        core.end_stage()
        causal_heads(core, d["heads_qkvo"], entered_by("n3"))
        core.end_stage()
        quantized_cross_attention(core, d["ctx_t"], d["xattn_wq"], d["xattn_bq"], d["xattn_wkv"], d["xattn_bkv"],
                                  d["xattn_wp"], d["xattn_bp"], entered_by("n4"))
        core.end_stage()
        ternary_ffn(core, d["ffn_gate_up"], d["ffn_down"], d["ffn_norm"], entered_by("n5", turn=False, sums=False))
        norm_and_turn(core, "n6", turn=False, out_dram=out, sums=False)


def lay_out_delta(w_qkv, w_gate, w_beta, w_alpha, log_A, dt_bias, conv_w, rms_w, w_out):
    def by_head(w, n):
        return w.reshape(n, 128, 2, 128).transpose(0, 3, 2, 1)

    q, k = by_head(w_qkv[:1024], 8), by_head(w_qkv[1024:2048], 8)
    v = by_head(w_qkv[2048:], 16).reshape(8, 2, 128, 2, 128)
    qkv = np.stack([q, k, v[:, 0], v[:, 1]], axis=2).reshape(8, 128, 1024)
    cq, ck = conv_w[:1024, 0].reshape(8, 128, 4), conv_w[1024:2048, 0].reshape(8, 128, 4)
    cv = conv_w[2048:, 0].reshape(8, 2, 128, 4)
    taps = np.stack([cq, ck, cv[:, 0], cv[:, 1]], axis=2).reshape(8, 128, 16)
    gate = w_gate.reshape(8, 256, 2, 128).transpose(0, 3, 2, 1).reshape(8, 128, 512)
    out = w_out.T.reshape(8, 2, 128, 256).transpose(0, 2, 1, 3).reshape(8, 128, 512)
    small = np.concatenate([w_beta, w_alpha]).T.reshape(2, 128, 32).transpose(1, 0, 2).reshape(128, 64)
    return {"delta_heads": np.concatenate([qkv, taps, gate, out], axis=2), "delta_small": small,
            "delta_bias": np.stack([dt_bias, log_A]), "delta_rms": rms_w[:, None], "delta_masks": delta_masks()}


def lay_out_rotary(encoding, Wq, bq, Wk, bk, Wv, bv, Wm, bm):
    channel = np.arange(128)
    swap = ((channel // 16) ^ 1) * 16 + channel % 16
    by_head = (channel % 8) * 16 + channel // 8
    w = np.stack([Wq.T, Wq[swap].T, Wk.T, Wk[swap].T, Wv[by_head].T, Wm[:, by_head].T], axis=1).reshape(128, 768)
    sign = np.where((channel // 16) % 2 == 0, -1, 1).astype(np.float32)[:, None]
    return {"rotary_w": w, "rotary_cols": np.stack([bq, bq[swap], bk, bk[swap], bm], axis=1),
            "rotary_bv": bv[by_head], "rotary_enc": encoding[:, 0, 0].transpose(0, 2, 1), "rotary_sign": sign}


def lay_out_experts(sim_matrix, gates, q_proj, k_proj, v_proj, o_proj):
    def tiles(w):
        return w.reshape(16, 2, 128, 128).transpose(0, 2, 1, 3).reshape(16, 128, 256)

    return {"sim": sim_matrix, "gates": gates, "expert_o": o_proj,
            "expert_qkv": np.concatenate([tiles(q_proj), tiles(k_proj), tiles(v_proj)], axis=2)}


def lay_out_heads(W_Q, W_K, W_V, W_O):
    def tiles(w):
        return w.transpose(0, 2, 1).reshape(16, 2, 128, 128).transpose(0, 2, 1, 3).reshape(16, 128, 256)

    return {"heads_qkvo": np.concatenate([tiles(W_Q), tiles(W_K), tiles(W_V), W_O.transpose(0, 2, 1)], axis=2)}


def lay_out_ffn(w_gate_up, w_down, norm_weight):
    return {"ffn_gate_up": w_gate_up.T.reshape(2, 128, 1408).transpose(1, 0, 2).reshape(128, 2816),
            "ffn_down": w_down.T.reshape(8, 88, 256).transpose(1, 0, 2).reshape(88, 2048), "ffn_norm": norm_weight}


def lay_out(inputs):
    inputs = {name: np.asarray(a) for name, a in inputs.items()}

    def part(prefix):
        return {name[len(prefix):]: a for name, a in inputs.items() if name.startswith(prefix)}

    laid = {"x": inputs["x"], "ctx": inputs["ctx_2048"], "ctx_t": inputs["ctx_2048"].reshape(N, C).T}
    laid.update(lay_out_delta(**part("L0_attn_")))
    laid.update(lay_out_rotary(**part("L0_xattn_")))
    laid.update(lay_out_experts(**part("L0_ffn_")))
    laid.update(lay_out_heads(**part("L1_attn_")))
    laid.update({"xattn_" + name.lower(): a for name, a in part("L1_xattn_").items()})
    laid.update(lay_out_ffn(**part("L1_ffn_")))
    return {name: np.ascontiguousarray(a) for name, a in laid.items()}


def kernel(**inputs):
    import concourse.bacc as bacc
    from concourse.bass_utils import run_bass_kernel_spmd

    nc = bacc.Bacc("TRN2", target_bir_lowering=False, num_devices=1)
    arrays, d = {}, {}
    for name, a in lay_out(inputs).items():
        arrays[f"in_{name}"] = a
        d[name] = nc.dram_tensor(f"in_{name}", a.shape, mybir.dt.from_np(a.dtype), kind="ExternalInput").ap()
    out = nc.dram_tensor("out_y", (B, S, C), F32, kind="ExternalOutput").ap()
    decoder(nc, d, out)
    r = run_bass_kernel_spmd(nc, [arrays], core_ids=[0])
    return r.results[0]["out_y"]
```
